# Optimizing a Trainium2 kernel written in Bass

```python
import numpy as np
import jax
import jax.numpy as jnp

def _softmax(x, axis=-1):
    return jax.nn.softmax(x, axis=axis)

def _gelu(x):
    return jax.nn.gelu(x, approximate=True)

def _silu(x):
    return jax.nn.silu(x)

def _sigmoid(x):
    return jax.nn.sigmoid(x)

def _layernorm(x, axis=-1, eps=1e-05):
    m = jnp.mean(x, axis=axis, keepdims=True)
    v = jnp.var(x, axis=axis, keepdims=True)
    return (x - m) / jnp.sqrt(v + eps)

def _scatter_add(tgt, idx, src, axis=0):
    return tgt.at[idx].add(src)

def _segment_sum(src, seg, n):
    return jax.ops.segment_sum(src, seg, n)
kernel_name = 'mk_conv_attn_hybrid_d2_conv_nchw512_r4_a742fb'

def setup_inputs(seed: int=0):
    np.random.seed(seed)
    _w = jnp.asarray

    def _rec_inputs():
        import jax
        import jax.numpy as jnp
        _gk = jax.random.key(seed)
        x = 7.22e-05 + 1 * jax.random.normal(jax.random.fold_in(_gk, 1), (4, 128, 16, 16), jnp.float32)
        return x
    x = _rec_inputs()

    def _L0_conv_setup():
        import jax, jax.numpy as jnp
        import numpy as np
        B, C, H, W = (4, 128, 16, 16)
        NH, DH, NP = (8, 16, 8)
        GROUPS = 8
        EPS = 1e-05

        def _linear_params(key, din, dout, scale=0.02):
            kw, kb = jax.random.split(key)
            return (jax.random.normal(kw, (din, dout), jnp.float32) * scale, jax.random.normal(kb, (dout,), jnp.float32) * scale)

        def _layernorm(x, g, b):
            mu = x.mean(-1, keepdims=True)
            var = x.var(-1, keepdims=True)
            return (x - mu) / jnp.sqrt(var + EPS) * g + b

        def _groupnorm(x, g, b):
            bsz, c, h, w = x.shape
            xg = x.reshape(bsz, GROUPS, c // GROUPS, h, w)
            mu = xg.mean((2, 3, 4), keepdims=True)
            var = xg.var((2, 3, 4), keepdims=True)
            xg = (xg - mu) / jnp.sqrt(var + EPS)
            return xg.reshape(bsz, c, h, w) * g[None, :, None, None] + b[None, :, None, None]

        def _bilinear(v, px, py, Hl, Wl):
            x0 = jnp.floor(px)
            y0 = jnp.floor(py)
            lx = px - x0
            ly = py - y0
            x0i = x0.astype(jnp.int32)
            y0i = y0.astype(jnp.int32)
            d = v.shape[-1]

            def corner(xi, yi, wgt):
                valid = (xi >= 0) & (xi < Wl) & (yi >= 0) & (yi < Hl)
                idx = jnp.clip(yi, 0, Hl - 1) * Wl + jnp.clip(xi, 0, Wl - 1)
                idx = jnp.broadcast_to(idx[..., None], idx.shape + (d,))
                g = jnp.take_along_axis(v, idx, axis=2)
                return g * (wgt * valid)[..., None]
            return corner(x0i, y0i, (1 - lx) * (1 - ly)) + corner(x0i + 1, y0i, lx * (1 - ly)) + corner(x0i, y0i + 1, (1 - lx) * ly) + corner(x0i + 1, y0i + 1, lx * ly)

        def _msda(query, value, soff_w, soff_b, attw_w, attw_b, Hl, Wl):
            bsz, L, _ = query.shape
            d = C // NH
            v = value.reshape(bsz, L, NH, d).transpose(0, 2, 1, 3)
            off = (query @ soff_w + soff_b).reshape(bsz, L, NH, 1, NP, 2)
            aw = jax.nn.softmax((query @ attw_w + attw_b).reshape(bsz, L, NH, NP), axis=-1)
            normalizer = jnp.array([Wl, Hl], jnp.float32)
            loc = 0.5 + off[:, :, :, 0] / normalizer
            grid = 2.0 * loc - 1.0
            px = ((grid[..., 0] + 1.0) * Wl - 1.0) * 0.5
            py = ((grid[..., 1] + 1.0) * Hl - 1.0) * 0.5
            px = px.transpose(0, 2, 1, 3).reshape(bsz, NH, L * NP)
            py = py.transpose(0, 2, 1, 3).reshape(bsz, NH, L * NP)
            sampled = _bilinear(v, px, py, Hl, Wl).reshape(bsz, NH, L, NP, d)
            awt = aw.transpose(0, 2, 1, 3)
            return jnp.einsum('bhqpd,bhqp->bqhd', sampled, awt).reshape(bsz, L, C)
        key = jax.random.key(seed)
        ks = jax.random.split(key, 12)
        x = jax.random.normal(ks[0], (B, C, H, W), jnp.float32)
        pin_w, pin_b = _linear_params(ks[1], C, C)
        vproj_w, vproj_b = _linear_params(ks[2], C, C)
        mvp_w, mvp_b = _linear_params(ks[3], C, C)
        soff_w, soff_b = _linear_params(ks[4], C, NH * NP * 2, scale=0.1)
        attw_w, attw_b = _linear_params(ks[5], C, NH * NP)
        mop_w, mop_b = _linear_params(ks[6], C, C)
        dout_w, dout_b = _linear_params(ks[7], C, C)
        geglu_w, geglu_b = _linear_params(ks[8], C, C * 8)
        dense_w, dense_b = _linear_params(ks[9], C * 4, C)
        pout_w, pout_b = _linear_params(ks[10], C, C)
        return dict(x=x, gn_g=jnp.ones((C,), jnp.float32), gn_b=jnp.zeros((C,), jnp.float32), pin_w=pin_w, pin_b=pin_b, ln1_g=jnp.ones((C,), jnp.float32), ln1_b=jnp.zeros((C,), jnp.float32), vproj_w=vproj_w, vproj_b=vproj_b, mvp_w=mvp_w, mvp_b=mvp_b, soff_w=soff_w, soff_b=soff_b, attw_w=attw_w, attw_b=attw_b, mop_w=mop_w, mop_b=mop_b, dout_w=dout_w, dout_b=dout_b, ln3_g=jnp.ones((C,), jnp.float32), ln3_b=jnp.zeros((C,), jnp.float32), geglu_w=geglu_w, geglu_b=geglu_b, dense_w=dense_w, dense_b=dense_b, pout_w=pout_w, pout_b=pout_b)
    _L0_conv_all = _L0_conv_setup()
    _L0_conv_in = {k: v for k, v in _L0_conv_all.items() if k in ('gn_g', 'gn_b', 'pin_w', 'pin_b', 'ln1_g', 'ln1_b', 'vproj_w', 'vproj_b', 'mvp_w', 'mvp_b', 'soff_w', 'soff_b', 'attw_w', 'attw_b', 'mop_w', 'mop_b', 'dout_w', 'dout_b', 'ln3_g', 'ln3_b', 'geglu_w', 'geglu_b', 'dense_w', 'dense_b', 'pout_w', 'pout_b')}
    del _L0_conv_all

    def _L1_attn_setup():
        import jax, jax.numpy as jnp
        import numpy as np
        DIM = 128
        HEADS = 8
        HEAD_DIM = DIM // HEADS
        B, N = (2, 16 * 14 * 14)
        SCALE = HEAD_DIM ** (-0.5)
        key = jax.random.key(seed)
        kx, kq, kk, kv, kp = jax.random.split(key, 5)
        s = DIM ** (-0.5)
        return {'x': jax.random.normal(kx, (B, N, DIM), dtype=jnp.float32), 'wq': jax.random.normal(kq, (DIM, DIM), dtype=jnp.float32) * s, 'wk': jax.random.normal(kk, (DIM, DIM), dtype=jnp.float32) * s, 'wv': jax.random.normal(kv, (DIM, DIM), dtype=jnp.float32) * s, 'wproj': jax.random.normal(kp, (DIM, DIM), dtype=jnp.float32) * s}
    _L1_attn_all = _L1_attn_setup()
    _L1_attn_in = {k: v for k, v in _L1_attn_all.items() if k in ('wq', 'wk', 'wv', 'wproj')}
    del _L1_attn_all

    def _L1_ffn_setup():
        import jax, jax.numpy as jnp
        import numpy as np
        TOP_K = 2
        key = jax.random.key(seed)
        k1, k2, k3, k4 = jax.random.split(key, 4)
        B, S, D, F, E = (4, 128, 128, 512, 16)
        hidden_states = jax.random.normal(k1, (B, S, D), dtype=jnp.float32)
        gate_weight = jax.random.normal(k2, (E, D), dtype=jnp.float32) * 0.02
        w1 = jax.random.normal(k3, (E, F, D), dtype=jnp.float32) * 0.02
        w2 = jax.random.normal(k4, (E, D, F), dtype=jnp.float32) * 0.02
        return {'hidden_states': hidden_states, 'gate_weight': gate_weight, 'w1': w1, 'w2': w2}
    _L1_ffn_all = _L1_ffn_setup()
    _L1_ffn_in = {k: v for k, v in _L1_ffn_all.items() if k in ('gate_weight', 'w1', 'w2')}
    del _L1_ffn_all
    return {'x': x, 'L0_conv_gn_g': _L0_conv_in['gn_g'], 'L0_conv_gn_b': _L0_conv_in['gn_b'], 'L0_conv_pin_w': _L0_conv_in['pin_w'], 'L0_conv_pin_b': _L0_conv_in['pin_b'], 'L0_conv_ln1_g': _L0_conv_in['ln1_g'], 'L0_conv_ln1_b': _L0_conv_in['ln1_b'], 'L0_conv_vproj_w': _L0_conv_in['vproj_w'], 'L0_conv_vproj_b': _L0_conv_in['vproj_b'], 'L0_conv_mvp_w': _L0_conv_in['mvp_w'], 'L0_conv_mvp_b': _L0_conv_in['mvp_b'], 'L0_conv_soff_w': _L0_conv_in['soff_w'], 'L0_conv_soff_b': _L0_conv_in['soff_b'], 'L0_conv_attw_w': _L0_conv_in['attw_w'], 'L0_conv_attw_b': _L0_conv_in['attw_b'], 'L0_conv_mop_w': _L0_conv_in['mop_w'], 'L0_conv_mop_b': _L0_conv_in['mop_b'], 'L0_conv_dout_w': _L0_conv_in['dout_w'], 'L0_conv_dout_b': _L0_conv_in['dout_b'], 'L0_conv_ln3_g': _L0_conv_in['ln3_g'], 'L0_conv_ln3_b': _L0_conv_in['ln3_b'], 'L0_conv_geglu_w': _L0_conv_in['geglu_w'], 'L0_conv_geglu_b': _L0_conv_in['geglu_b'], 'L0_conv_dense_w': _L0_conv_in['dense_w'], 'L0_conv_dense_b': _L0_conv_in['dense_b'], 'L0_conv_pout_w': _L0_conv_in['pout_w'], 'L0_conv_pout_b': _L0_conv_in['pout_b'], 'L1_attn_wq': _L1_attn_in['wq'], 'L1_attn_wk': _L1_attn_in['wk'], 'L1_attn_wv': _L1_attn_in['wv'], 'L1_attn_wproj': _L1_attn_in['wproj'], 'L1_ffn_gate_weight': _L1_ffn_in['gate_weight'], 'L1_ffn_w1': _L1_ffn_in['w1'], 'L1_ffn_w2': _L1_ffn_in['w2']}

def reference(x, L0_conv_gn_g, L0_conv_gn_b, L0_conv_pin_w, L0_conv_pin_b, L0_conv_ln1_g, L0_conv_ln1_b, L0_conv_vproj_w, L0_conv_vproj_b, L0_conv_mvp_w, L0_conv_mvp_b, L0_conv_soff_w, L0_conv_soff_b, L0_conv_attw_w, L0_conv_attw_b, L0_conv_mop_w, L0_conv_mop_b, L0_conv_dout_w, L0_conv_dout_b, L0_conv_ln3_g, L0_conv_ln3_b, L0_conv_geglu_w, L0_conv_geglu_b, L0_conv_dense_w, L0_conv_dense_b, L0_conv_pout_w, L0_conv_pout_b, L1_attn_wq, L1_attn_wk, L1_attn_wv, L1_attn_wproj, L1_ffn_gate_weight, L1_ffn_w1, L1_ffn_w2):
    import jax
    import jax.numpy as jnp

    def _L0_conv_ref(x, gn_g, gn_b, pin_w, pin_b, ln1_g, ln1_b, vproj_w, vproj_b, mvp_w, mvp_b, soff_w, soff_b, attw_w, attw_b, mop_w, mop_b, dout_w, dout_b, ln3_g, ln3_b, geglu_w, geglu_b, dense_w, dense_b, pout_w, pout_b):
        import jax, jax.numpy as jnp
        import numpy as np
        B, C, H, W = (4, 128, 16, 16)
        NH, DH, NP = (8, 16, 8)
        GROUPS = 8
        EPS = 1e-05

        def _linear_params(key, din, dout, scale=0.02):
            kw, kb = jax.random.split(key)
            return (jax.random.normal(kw, (din, dout), jnp.float32) * scale, jax.random.normal(kb, (dout,), jnp.float32) * scale)

        def _layernorm(x, g, b):
            mu = x.mean(-1, keepdims=True)
            var = x.var(-1, keepdims=True)
            return (x - mu) / jnp.sqrt(var + EPS) * g + b

        def _groupnorm(x, g, b):
            bsz, c, h, w = x.shape
            xg = x.reshape(bsz, GROUPS, c // GROUPS, h, w)
            mu = xg.mean((2, 3, 4), keepdims=True)
            var = xg.var((2, 3, 4), keepdims=True)
            xg = (xg - mu) / jnp.sqrt(var + EPS)
            return xg.reshape(bsz, c, h, w) * g[None, :, None, None] + b[None, :, None, None]

        def _bilinear(v, px, py, Hl, Wl):
            x0 = jnp.floor(px)
            y0 = jnp.floor(py)
            lx = px - x0
            ly = py - y0
            x0i = x0.astype(jnp.int32)
            y0i = y0.astype(jnp.int32)
            d = v.shape[-1]

            def corner(xi, yi, wgt):
                valid = (xi >= 0) & (xi < Wl) & (yi >= 0) & (yi < Hl)
                idx = jnp.clip(yi, 0, Hl - 1) * Wl + jnp.clip(xi, 0, Wl - 1)
                idx = jnp.broadcast_to(idx[..., None], idx.shape + (d,))
                g = jnp.take_along_axis(v, idx, axis=2)
                return g * (wgt * valid)[..., None]
            return corner(x0i, y0i, (1 - lx) * (1 - ly)) + corner(x0i + 1, y0i, lx * (1 - ly)) + corner(x0i, y0i + 1, (1 - lx) * ly) + corner(x0i + 1, y0i + 1, lx * ly)

        def _msda(query, value, soff_w, soff_b, attw_w, attw_b, Hl, Wl):
            bsz, L, _ = query.shape
            d = C // NH
            v = value.reshape(bsz, L, NH, d).transpose(0, 2, 1, 3)
            off = (query @ soff_w + soff_b).reshape(bsz, L, NH, 1, NP, 2)
            aw = jax.nn.softmax((query @ attw_w + attw_b).reshape(bsz, L, NH, NP), axis=-1)
            normalizer = jnp.array([Wl, Hl], jnp.float32)
            loc = 0.5 + off[:, :, :, 0] / normalizer
            grid = 2.0 * loc - 1.0
            px = ((grid[..., 0] + 1.0) * Wl - 1.0) * 0.5
            py = ((grid[..., 1] + 1.0) * Hl - 1.0) * 0.5
            px = px.transpose(0, 2, 1, 3).reshape(bsz, NH, L * NP)
            py = py.transpose(0, 2, 1, 3).reshape(bsz, NH, L * NP)
            sampled = _bilinear(v, px, py, Hl, Wl).reshape(bsz, NH, L, NP, d)
            awt = aw.transpose(0, 2, 1, 3)
            return jnp.einsum('bhqpd,bhqp->bqhd', sampled, awt).reshape(bsz, L, C)
        bsz, c, h, w = x.shape
        x_in = x
        xn = _groupnorm(x, gn_g, gn_b)
        xn = jnp.einsum('bihw,io->bohw', xn, pin_w) + pin_b[None, :, None, None]
        t = xn.reshape(bsz, c, h * w).transpose(0, 2, 1)
        L = h * w
        q = _layernorm(t, ln1_g, ln1_b)
        value = q @ vproj_w + vproj_b
        v2 = value @ mvp_w + mvp_b
        msda = _msda(q, v2, soff_w, soff_b, attw_w, attw_b, L, 1)
        msda = msda @ mop_w + mop_b + q
        attn_out = msda @ dout_w + dout_b
        t = attn_out + t
        hn = _layernorm(t, ln3_g, ln3_b)
        gp = hn @ geglu_w + geglu_b
        a, gate = (gp[..., :4 * c], gp[..., 4 * c:])
        ff = a * jax.nn.gelu(gate, approximate=False) @ dense_w + dense_b
        t = ff + t
        xo = t.transpose(0, 2, 1).reshape(bsz, c, h, w)
        return jnp.einsum('bihw,io->bohw', xo, pout_w) + pout_b[None, :, None, None] + x_in

    def _L1_attn_ref(x, wq, wk, wv, wproj):
        import jax, jax.numpy as jnp
        import numpy as np
        DIM = 128
        HEADS = 8
        HEAD_DIM = DIM // HEADS
        B, N = (2, 16 * 14 * 14)
        SCALE = HEAD_DIM ** (-0.5)
        Bs, Ns, C = x.shape

        def heads(y):
            return y.reshape(Bs, Ns, HEADS, HEAD_DIM).transpose(0, 2, 1, 3)
        q = heads(x @ wq.T)
        k = heads(x @ wk.T)
        v = heads(x @ wv.T)
        attn = jnp.einsum('bhnd,bhmd->bhnm', q, k) * SCALE
        attn = jax.nn.softmax(attn, axis=-1)
        out = jnp.einsum('bhnm,bhmd->bhnd', attn, v)
        out = out.transpose(0, 2, 1, 3).reshape(Bs, Ns, C)
        return out @ wproj.T

    def _L1_ffn_ref(hidden_states, gate_weight, w1, w2):
        import jax, jax.numpy as jnp
        import numpy as np
        TOP_K = 2
        B, S, D = hidden_states.shape
        E = gate_weight.shape[0]
        x = hidden_states.reshape(-1, D)
        gate_logits = x @ gate_weight.T
        top_vals, top_idx = jax.lax.top_k(gate_logits, TOP_K)
        routing_w = jax.nn.softmax(top_vals, axis=-1)
        mask = jnp.any(top_idx[:, :, None] == jnp.arange(E)[None, None, :], axis=1)
        h = jax.nn.silu(jnp.einsum('td,efd->tef', x, w1))
        counts = jnp.sum(mask, axis=0)
        h_sum = jnp.einsum('tef,te->ef', h, mask.astype(h.dtype))
        h_mean = h_sum / jnp.maximum(counts, 1)[:, None].astype(h.dtype)
        y_mean = jnp.einsum('ef,edf->ed', h_mean, w2)
        y_mean = jnp.where((counts > 0)[:, None], y_mean, 0.0)
        out = jnp.einsum('tk,tkd->td', routing_w, y_mean[top_idx])
        return out.reshape(B, S, D)

    def _gn(v, G=32, eps=1e-05):
        B_, C_, H_, W_ = v.shape
        g = v.reshape(B_, G, C_ // G, H_, W_)
        m = jnp.mean(g, axis=(2, 3, 4), keepdims=True)
        s = jnp.var(g, axis=(2, 3, 4), keepdims=True)
        return ((g - m) / jnp.sqrt(s + eps)).reshape(v.shape)

    def _ln_c(v, eps=1e-06):
        m = jnp.mean(v, axis=1, keepdims=True)
        s = jnp.var(v, axis=1, keepdims=True)
        return (v - m) / jnp.sqrt(s + eps)

    def _ln_t(v, eps=1e-05):
        m = jnp.mean(v, axis=-1, keepdims=True)
        s = jnp.var(v, axis=-1, keepdims=True)
        return (v - m) / jnp.sqrt(s + eps)

    def _to_tokens(v):
        B_, C_, H_, W_ = v.shape
        return v.reshape(B_, C_, H_ * W_).transpose(0, 2, 1)

    def _from_tokens(t, like):
        B_, C_, H_, W_ = like.shape
        return t.transpose(0, 2, 1).reshape(B_, C_, H_, W_)
    x = _L0_conv_ref(x, L0_conv_gn_g, L0_conv_gn_b, L0_conv_pin_w, L0_conv_pin_b, L0_conv_ln1_g, L0_conv_ln1_b, L0_conv_vproj_w, L0_conv_vproj_b, L0_conv_mvp_w, L0_conv_mvp_b, L0_conv_soff_w, L0_conv_soff_b, L0_conv_attw_w, L0_conv_attw_b, L0_conv_mop_w, L0_conv_mop_b, L0_conv_dout_w, L0_conv_dout_b, L0_conv_ln3_g, L0_conv_ln3_b, L0_conv_geglu_w, L0_conv_geglu_b, L0_conv_dense_w, L0_conv_dense_b, L0_conv_pout_w, L0_conv_pout_b)
    t = _to_tokens(x)
    t = t + _L1_attn_ref(_ln_t(t), L1_attn_wq, L1_attn_wk, L1_attn_wv, L1_attn_wproj)
    t = t + _L1_ffn_ref(_ln_t(t), L1_ffn_gate_weight, L1_ffn_w1, L1_ffn_w2)
    x = _from_tokens(t, x)
    return x

_drawn_inputs = setup_inputs


def setup_inputs(seed=0):
    import zlib

    import numpy as np

    out = dict(_drawn_inputs(seed))
    spreads = {'L0_conv_gn_g': (1.0, 0.6),
     'L0_conv_gn_b': (0.0, 0.788),
     'L0_conv_ln1_g': (1.0, 0.6),
     'L0_conv_ln1_b': (0.0, 0.8),
     'L0_conv_ln3_g': (1.0, 0.6),
     'L0_conv_ln3_b': (0.0, 0.8)}
    factors = {'L0_conv_pin_b': 5.746,
     'L0_conv_vproj_w': 8.0,
     'L0_conv_vproj_b': 8.0,
     'L0_conv_mvp_w': 8.0,
     'L0_conv_mvp_b': 8.0,
     'L0_conv_soff_w': 8.0,
     'L0_conv_soff_b': 8.0,
     'L0_conv_attw_w': 8.0,
     'L0_conv_attw_b': 8.0,
     'L0_conv_mop_w': 8.0,
     'L0_conv_mop_b': 8.0,
     'L0_conv_dout_b': 8.0,
     'L0_conv_geglu_w': 8.0,
     'L0_conv_geglu_b': 8.0,
     'L0_conv_dense_w': 8.0,
     'L0_conv_dense_b': 42.634,
     'L1_ffn_gate_weight': 8.0,
     'L1_ffn_w1': 8.0,
     'L1_ffn_w2': 7.631,
     'L0_conv_pout_b': 7.869}
    for name, (base, spread) in spreads.items():
        noise = np.random.default_rng([zlib.crc32(name.encode()), seed]).standard_normal(out[name].shape)
        drawn = base * np.exp(spread * noise) if base else spread * noise
        out[name] = jnp.asarray(drawn.astype(out[name].dtype))
    for name, factor in factors.items():
        out[name] = (out[name] * factor).astype(out[name].dtype)
    return out
```

```python
from contextlib import ExitStack

import concourse.bass as bass
from concourse import mybir

ALU = mybir.AluOpType
ACT = mybir.ActivationFunctionType
AX_X = mybir.AxisListType.X
F32 = mybir.dt.float32
BF16 = mybir.dt.bfloat16
U32 = mybir.dt.uint32
I32 = mybir.dt.int32

P = 128
B, C, HW = 4, 128, 256
T = B * HW
TILES = T // P
HALF = T // 2
NH, DH, NP = 8, 16, 8
HP = NH * NP
GROUPS = 8
NK = 3
PARTS = 3
AH, AD = 8, 16
AD1 = AD + 1
E, TOPK, F = 16, 2, 512
FT = F // P
GE = 4
EPS = 1e-5
ROUND = 1.5 * 2 ** 23

WCOLS = dict(pin=128, vprojT=128, mvp=128, soff=128, attw=64, mopT=128, dout=128,
             geglu=1024, dense=512, pout=128, wv=128, wproj=128, gate=16)
WAT, at = {}, 0
for name, n in WCOLS.items():
    WAT[name] = (at, at + n)
    at += n
WTOTAL = at
VCOLS = dict(gn_g=1, gn_b=1, pin_b=1, ln1_g=1, ln1_b=1, vproj_b=1, mop_b=1, dout_b=1,
             ln3_g=1, ln3_b=1, geglu_b=8, dense_b=1, pout_b=1)
VAT, at = {}, 0
for name, n in VCOLS.items():
    VAT[name] = (at, at + n)
    at += n
VTOTAL = at
RTOTAL = C + 2 * HP + HP


def build(nc, x, weights, vectors, rows, wq_t, wk_t, w1_t, w2_t, out):
    with ExitStack() as ctx:
        def sb(name, shape, dt=F32):
            return ctx.enter_context(nc.sbuf_tensor(name, shape, dt))

        def sem(name):
            return ctx.enter_context(nc.semaphore(name))

        ps = ctx.enter_context(nc.psum_tensor("ps", [P, 8, 512], F32))

        ones_mean = sb("ones_mean", [P, P])
        ident = sb("ident", [P, P])
        ident_b = sb("ident_b", [P, P], BF16)
        group_mean = sb("group_mean", [P, P])
        row_i = sb("row_i", [P, 1], I32)
        row_f = sb("row_f", [P, 1])
        expert_i = sb("expert_i", [P, E], I32)
        expert_f = sb("expert_f", [P, E])
        eps_c = sb("eps_c", [P, 1])
        shift_c = sb("shift_c", [P, NK])
        w_sb = sb("w_sb", [P, WTOTAL])
        v_sb = sb("v_sb", [P, VTOTAL])
        r_sb = sb("r_sb", [P, RTOTAL])
        wq_sb = sb("wq_sb", [P, AH, 32])
        wk_sb = sb("wk_sb", [P, AH, 32])
        w1_sb = sb("w1_sb", [P, 2, F])
        w2_sb = sb("w2_sb", [P, E * FT, P])

        def W(name):
            a, b = WAT[name]
            return w_sb[:, a:b]

        def V(name, j=0):
            a, _ = VAT[name]
            return v_sb[:, a + j:a + j + 1]

        x_sb = sb("x_sb", [P, T])
        xn = sb("xn", [P, T])
        t0 = sb("t0", [P, T])
        q_c = sb("q_c", [P, T])
        dev = sb("dev", [P, T])
        sq = sb("sq", [P, T])
        std = sb("std", [P, T])
        rstd = sb("rstd", [P, T])
        nrm = sb("nrm", [P, T])
        msda_c = xn
        t1 = sb("t1", [P, T])
        hn = q_c
        gelu_g = sb("gelu_g", [P, 2, HALF])
        ff = sb("ff", [P, GE, T])
        t2 = nrm
        x1 = sb("x1", [P, T])
        z1 = q_c
        x2 = t1
        z2 = t0
        y_out = sq
        gn_st = sb("gn_st", [P, B, 6])
        gn_mv = sb("gn_mv", [P, B, 2])
        gn_sq = sb("gn_sq", [P, B])
        gn_g = sb("gn_g", [P, B, 2])
        gn_var = sb("gn_var", [P, B])
        gn_std = sb("gn_std", [P, B])
        gn_scale = sb("gn_scale", [P, B])
        gn_shift = sb("gn_shift", [P, B])
        w_val = sb("w_val", [P, P])
        w_out = sb("w_out", [P, P])
        vb_bc = sb("vb_bc", [P, P])
        b_val = sb("b_val", [P, P])
        b_out = sb("b_out", [P, 1])
        proj = sb("proj", [P, TILES, 3 * HP])
        hat_x = sb("hat_x", [P, TILES, HP])
        lmax = sb("lmax", [P, TILES * NH])
        lsum = sb("lsum", [P, TILES * NH])
        aw = sb("aw", [P, TILES * NH, NP])
        y_pos = sb("y_pos", [P, TILES, HP])
        y_half = sb("y_half", [P, TILES, HP])
        pair = sb("pair", [P, TILES, HP])
        pair_b = sb("pair_b", [P, TILES, HP], BF16)
        y_rest = sb("y_rest", [P, TILES, HP])
        hat_y = sb("hat_y", [P, NK, TILES, HP])
        wk3 = sb("wk3", [P, TILES, HP, NK])
        pair_t = sb("pair_t", [P, B, P], BF16)
        val = sb("val", [P, B, NH, NK, DH])
        val_r = sb("val_r", [P, B, NH, NK, DH])
        val_p = [sb(f"val_p{i}", [P, B, NH, NK, DH], BF16) for i in range(PARTS)]
        bc_b = ff[:, 2:4, :].bitcast(BF16).rearrange("r a (b q) -> r (a b) q", q=HALF)
        hot = sb("hot", [P, 2, NP, B, P], BF16)
        prod = hat_y[:, :, :, :].rearrange("q k t r -> q (k t r)").rearrange(
            "q (s b n d) -> q s b n d", s=2, b=2, d=DH)
        msda = sb("msda", [P, TILES, NH, DH])
        zb = sb("zb", [P, HW])
        qp = sb("qp", [P, 2, HW])
        kp = sb("kp", [P, 2, HW])
        v_tok = sb("v_tok", [P, 2, AH, AD1])
        nmax = sb("nmax", [P, 2, 2])
        prob = ff[:, 0, :].rearrange("q (s t k) -> q s t k", s=2, t=2)
        prob_t = ff[:, 1, :].rearrange("k (s a q) -> k s a q", s=2, a=4)
        inv_sum = sb("inv_sum", [P, 2, AH])
        o_tok = sb("o_tok", [P, 2, AH, AD])
        o_c = msda_c
        lg = sb("lg", [P, TILES, E])
        top = sb("top", [P, TILES, 8])
        top_i = sb("top_i", [P, TILES, 8], U32)
        top_f = sb("top_f", [P, TILES, TOPK])
        oh1 = sb("oh1", [P, TILES, E])
        oh2 = sb("oh2", [P, TILES, E])
        chosen = sb("chosen", [P, TILES, E])
        chosen_b = pair[:, :, :].bitcast(BF16)
        chosen_t = aw[:, :, :].bitcast(BF16).rearrange("e a b -> e (a b)")
        gap = sb("gap", [P, TILES])
        e2 = sb("e2", [P, TILES])
        e2p = sb("e2p", [P, TILES])
        rw1 = sb("rw1", [P, TILES])
        rw2 = sb("rw2", [P, TILES])
        route = sb("route", [P, TILES, E])
        route_t = rstd[0:E, :]
        cnt = sb("cnt", [P, E])
        inv_cnt = sb("inv_cnt", [P, E])
        xm = ff[:, 0:2, :]
        silu_junk = y_half[:, :, :].bitcast(BF16).rearrange("f a b -> f (a b)")
        h_sum = sb("h_sum", [P, E, FT])
        h_mean = sb("h_mean", [P, E, FT])
        y_t = sb("y_t", [P, E])
        y_mean = sb("y_mean", [E, P])

        ld_x = [sem(f"ld_x{b}") for b in range(B)]
        ld_v, ld_r, ld_wa, ld_wb, ld_qk, ld_w2 = (sem(n) for n in (
            "ld_v", "ld_r", "ld_wa", "ld_wb", "ld_qk", "ld_w2"))
        ld_w1 = [sem("ld_w1_even"), sem("ld_w1_odd")]
        stored = sem("stored")
        pool_step, dve_step, act_step = sem("pool_step"), sem("dve_step"), sem("act_step")
        consts = sem("consts")
        dve_consts = sem("dve_consts")
        gn_moments, gn_grouped, gn_varied, gn_stded, xn_ready = (sem(n) for n in (
            "gn_moments", "gn_grouped", "gn_varied", "gn_stded", "xn_ready"))
        pin_mm, t0_ready = sem("pin_mm"), sem("t0_ready")
        fuse_mm, fuse_ready = sem("fuse_mm"), sem("fuse_ready")
        lns = {n: {k: sem(f"{n}_{k}") for k in ("mean", "dev", "sq", "var", "std", "rstd", "norm", "out")}
               for n in ("ln1", "ln3", "lna", "lnf")}
        proj_mm, proj_ready, val_mm, val_ready = (sem(n) for n in (
            "proj_mm", "proj_ready", "val_mm", "val_ready"))
        val_p0, val_r1, val_p1 = sem("val_p0"), sem("val_r1"), sem("val_p1")
        logit_sub, logit_exp, x_abs, hat_x_ready = (sem(n) for n in (
            "logit_sub", "logit_exp", "x_abs", "hat_x_ready"))
        rest_ready, y_abs, hat_y_ready, pair_ready = (sem(n) for n in (
            "rest_ready", "y_abs", "hat_y_ready", "pair_ready"))
        pair_mm, pair_t_ready, wk3_ready = sem("pair_mm"), sem("pair_t_ready"), sem("wk3_ready")
        bc_ready, bc_free, bc_copied, bc_used = (sem(n) for n in (
            "bc_ready", "bc_free", "bc_copied", "bc_used"))
        hot_ready, g_ready, g_free, prod_ready, prod_free = (sem(n) for n in (
            "hot_ready", "g_ready", "g_free", "prod_ready", "prod_free"))
        msda_mm, msda_c_ready, out_mm, t1_ready = (sem(n) for n in (
            "msda_mm", "msda_c_ready", "out_mm", "t1_ready"))
        gate_mm, lin_mm, gelu_ready, ff_ready, dense_mm, t2_ready, pout_mm, x1_ready = (sem(n) for n in (
            "gate_mm", "lin_mm", "gelu_ready", "ff_ready", "dense_mm", "t2_ready", "pout_mm", "x1_ready"))
        zb_ready, qk_mm, qk_ready, v_mm, v_ready = (sem(n) for n in (
            "zb_ready", "qk_mm", "qk_ready", "v_mm", "v_ready"))
        sc_mm, nmax_ready, prob_ready, pt_mm, pt_ready, pv_mm = (sem(n) for n in (
            "sc_mm", "nmax_ready", "prob_ready", "pt_mm", "pt_ready", "pv_mm"))
        inv_ready, o_ready, ot_mm, o_c_ready, ap_mm, x2_ready = (sem(n) for n in (
            "inv_ready", "o_ready", "ot_mm", "o_c_ready", "ap_mm", "x2_ready"))
        lg_mm, gap_ready, e2_ready, route_ready, rt_mm, route_t_ready, cnt_mm = (sem(n) for n in (
            "lg_mm", "gap_ready", "e2_ready", "route_ready", "rt_mm", "route_t_ready", "cnt_mm"))
        mb_mm, xm_ready, h_mm, h_used, hmean_ready, y_mm, y_t_ready, yt_mm, y_ready, moe_mm, y_out_ready = (
            sem(n) for n in ("mb_mm", "xm_ready", "h_mm", "h_used", "hmean_ready", "y_mm", "y_t_ready",
                             "yt_mm", "y_ready", "moe_mm", "y_out_ready"))

        def half(t, h):
            return t[:, h * HALF:(h + 1) * HALF]

        block = ctx.enter_context(nc.Block())

        @block.sync
        def _(sp):
            a = WAT["attw"][1]
            sp.dma_start(v_sb[:, :], vectors).then_inc(ld_v, 16)
            for b in range(B):
                sp.dma_start(x_sb[:, b * HW:(b + 1) * HW], x[b]).then_inc(ld_x[b], 16)
            sp.dma_start(w_sb[:, 0:a], weights[:, 0:a]).then_inc(ld_wa, 16)
            sp.dma_start(r_sb[:, :], rows.to_broadcast([P, RTOTAL])).then_inc(ld_r, 16)
            sp.dma_start(w_sb[:, a:], weights[:, a:]).then_inc(ld_wb, 16)
            sp.wait_ge(consts, 1)
            sp.dma_start(wq_sb[:, :, 0:AD], wq_t).then_inc(ld_qk, 16)
            sp.dma_start(wk_sb[:, :, 0:AD], wk_t).then_inc(ld_qk, 16)
            for n in range(2):
                sp.dma_start(w1_sb[:, n, :], w1_t[n]).then_inc(ld_w1[n], 16)
            sp.dma_start(w2_sb[:, :, :], w2_t).then_inc(ld_w2, 16)
            with sp.Fori(0, E // 2 - 1) as i:
                for n in range(2):
                    sp.wait_ge(h_mm, (2 * FT) * i + FT * (n + 1))
                    sp.dma_start(w1_sb[:, n, :], w1_t[bass.ds(2 * i + 2 + n, 1)].rearrange("e d f -> (e d) f")).then_inc(
                        ld_w1[n], 16)
            for h in range(2):
                sp.wait_ge(y_out_ready, h + 1)
                sp.dma_start(out[2 * h:2 * h + 2].rearrange("b c l -> c b l"),
                             half(y_out, h).rearrange("c (b l) -> c b l", b=2)).then_inc(stored, 16)
            sp.wait_ge(stored, 32)

        @block.gpsimd
        def _(pool):
            nc.gpsimd.memset(wq_sb[:, :, :], 0.0).then_inc(pool_step, 1)
            nc.gpsimd.memset(wk_sb[:, :, :], 0.0).then_inc(pool_step, 1)
            nc.gpsimd.memset(ident[:, :], 0.0).then_inc(pool_step, 1)
            nc.gpsimd.memset(group_mean[:, :], GROUPS / C).then_inc(pool_step, 1)
            pool.wait_ge(pool_step, 4)
            nc.gpsimd.affine_select(out=ident[:, :], in_=ident[:, :], compare_op=ALU.not_equal, fill=1.0,
                                    base=0, pattern=[[-1, P]], channel_multiplier=1).then_inc(consts, 1)
            gm = group_mean[:, :].rearrange("c (g i) -> c g i", g=GROUPS)
            per = C // GROUPS
            nc.gpsimd.affine_select(out=gm, in_=gm, compare_op=ALU.is_ge, fill=0.0, base=0,
                                    pattern=[[-per, GROUPS], [0, per]], channel_multiplier=1).then_inc(pool_step, 1)
            pool.wait_ge(pool_step, 5)
            nc.gpsimd.affine_select(out=gm, in_=gm, compare_op=ALU.is_ge, fill=0.0, base=per - 1,
                                    pattern=[[per, GROUPS], [0, per]], channel_multiplier=-1).then_inc(consts, 1)
            nc.gpsimd.iota(row_i[:, :], pattern=[[0, 1]], base=0, channel_multiplier=1).then_inc(consts, 1)
            nc.gpsimd.iota(expert_i[:, :], pattern=[[1, E]], base=0, channel_multiplier=0).then_inc(consts, 1)
            nc.gpsimd.memset(val[:, :, :, :, :], 0.0).then_inc(consts, 1)
            nc.gpsimd.memset(v_tok[:, :, :, :], 1.0).then_inc(consts, 1)
        CONSTS = 6

        @block.scalar
        def _(act):
            def ln(s, src_g=None, src_b=None, dst=None):
                for h in range(2):
                    act.wait_ge(s["dev"], h + 1)
                    nc.scalar.activation(half(sq, h), half(dev, h), ACT.Square).then_inc(s["sq"], 1)
                for h in range(2):
                    act.wait_ge(s["var"], h + 1)
                    nc.scalar.activation(half(std, h), ps[:, 2 + h, :], ACT.Sqrt,
                                         bias=eps_c[:, 0:1]).then_inc(s["std"], 1)
                if dst is not None:
                    for h in range(2):
                        act.wait_ge(s["norm"], h + 1)
                        nc.scalar.activation(half(dst, h), half(nrm, h), ACT.Identity,
                                             scale=src_g, bias=src_b).then_inc(s["out"], 1)

            act.wait_ge(dve_consts, 1)
            act.wait_ge(gn_varied, 1)
            nc.scalar.activation(gn_std[:, :], gn_var[:, :], ACT.Sqrt, bias=eps_c[:, 0:1]).then_inc(gn_stded, 1)
            for h in range(2):
                act.wait_ge(pin_mm, h + 1)
                nc.scalar.activation(half(t0, h), ps[:, h, :], ACT.Identity, bias=V("pin_b")).then_inc(t0_ready, 1)
            ln(lns["ln1"], V("ln1_g"), V("ln1_b"), q_c)

            act.wait_ge(proj_ready, TILES)
            nc.scalar.activation(hat_x[:, :, :], proj[:, :, 0:HP], ACT.Abs).then_inc(x_abs, 1)
            act.wait_ge(x_abs, 1)
            nc.scalar.activation(hat_x[:, :, :], hat_x[:, :, :], ACT.Relu, scale=-1.0, bias=1.0).then_inc(hat_x_ready, 1)
            act.wait_ge(logit_sub, 1)
            nc.scalar.activation(aw[:, :, :], aw[:, :, :], ACT.Exp).then_inc(logit_exp, 1)
            act.wait_ge(rest_ready, 1)
            for k in range(NK):
                nc.scalar.activation(hat_y[:, k, :, :], y_rest[:, :, :], ACT.Abs,
                                     bias=shift_c[:, k:k + 1]).then_inc(y_abs, 1)
            for k in range(NK):
                act.wait_ge(y_abs, k + 1)
                nc.scalar.activation(hat_y[:, k, :, :], hat_y[:, k, :, :], ACT.Relu,
                                     scale=-1.0, bias=1.0).then_inc(hat_y_ready, 1)
            act.wait_ge(val_ready, B * NK)
            nc.scalar.activation(val_p[0][:, :, :, :, :], val[:, :, :, :, :], ACT.Copy).then_inc(val_p0, 1)
            act.wait_ge(val_r1, 1)
            nc.scalar.activation(val_p[1][:, :, :, :, :], val_r[:, :, :, :, :], ACT.Copy).then_inc(val_p1, 1)
            act.wait_ge(pair_mm, B)
            nc.scalar.activation(pair_t[:, :, :], ps[:, 5, 0:256].bitcast(BF16).rearrange("r (b q) -> r b q", b=B),
                                 ACT.Copy).then_inc(pair_t_ready, 1)

            with act.Fori(0, NH) as i:
                for u in range(2):
                    for c in range(NP // 2):
                        act.wait_ge(bc_ready, 8 * i + 4 * u + c + 1)
                        act.wait_ge(bc_used, 8 * i + 4 * u + c + 1)
                        nc.scalar.activation(bc_b[:, 2 * c:2 * c + 2, :], ps[:, 2 * (c % 2):2 * (c % 2) + 2, :],
                                             ACT.Copy).then_inc(bc_copied, 1)

            for h in range(2):
                act.wait_ge(msda_mm, 4 * (h + 1))
                nc.scalar.activation(half(msda_c, h), ps[:, 4 + h, :], ACT.Copy).then_inc(msda_c_ready, 1)
            ln(lns["ln3"], V("ln3_g"), V("ln3_b"), hn)
            n = 0
            for j in range(GE):
                for h in range(2):
                    act.wait_ge(gate_mm, n + 1)
                    if n >= 2:
                        act.wait_ge(ff_ready, n - 1)
                    nc.scalar.activation(gelu_g[:, n % 2, :], ps[:, n % 2, :], ACT.Gelu,
                                         bias=V("geglu_b", GE + j)).then_inc(gelu_ready, 1)
                    n += 1
            ln(lns["lna"])

            with act.Fori(0, B) as b:
                act.wait_ge(qk_mm, b + 1)
                nc.scalar.activation(qp[:, :, :], ps[:, 0, :].rearrange("c (g l) -> c g l", g=2), ACT.Copy,
                                     scale=AD ** -0.5).then_inc(qk_ready, 1)
                nc.scalar.activation(kp[:, :, :], ps[:, 1, :].rearrange("c (g l) -> c g l", g=2),
                                     ACT.Copy).then_inc(qk_ready, 1)
                for h in range(AH):
                    act.wait_ge(nmax_ready, AH * b + h + 1)
                    act.wait_ge(pt_mm, AH * b + h + 1)
                    for qt in range(2):
                        nc.scalar.activation(prob[:, h % 2, qt, :], ps[:, h % 2, qt * HW:(qt + 1) * HW], ACT.Exp,
                                             bias=nmax[:, h % 2, qt:qt + 1]).then_inc(prob_ready, 1)
            ln(lns["lnf"])

            act.wait_ge(gap_ready, 1)
            nc.scalar.activation(e2[:, :], gap[:, :], ACT.Exp).then_inc(e2_ready, 1)
            with act.Fori(0, E // 2) as i:
                for n in range(2):
                    for f in range(FT):
                        act.wait_ge(h_mm, 2 * FT * i + FT * n + f + 1)
                        c = 2 + 2 * ((FT * n + f) % 2)
                        nc.scalar.activation(silu_junk[:, :], ps[:, c:c + 2, :].rearrange("f a t -> f (a t)"), ACT.Silu,
                                             accum_out=h_sum[:, bass.ds(2 * i + n, 1), f:f + 1].rearrange(
                                                 "p e f -> p (e f)")).then_inc(h_used, 1)
                        act.wait_ge(h_used, 2 * FT * i + FT * n + f + 1 + 2)

        @block.vector
        def _(dve):
            count = [0]

            def link(ins):
                count[0] += 1
                ins.then_inc(dve_step, 1)
                dve.wait_ge(dve_step, count[0])

            def ln(s, src, dst):
                for h in range(2):
                    dve.wait_ge(s["mean"], h + 1)
                    nc.vector.tensor_tensor(half(dev, h), half(src, h), ps[:, h, :], ALU.subtract).then_inc(s["dev"], 1)
                for h in range(2):
                    dve.wait_ge(s["std"], h + 1)
                    nc.vector.reciprocal(half(rstd, h), half(std, h)).then_inc(s["rstd"], 1)
                    dve.wait_ge(s["rstd"], h + 1)
                    nc.vector.tensor_tensor(half(dst, h), half(dev, h), half(rstd, h), ALU.mult).then_inc(s["norm"], 1)

            nc.vector.memset(ones_mean[:, :], 1.0 / P)
            for k in range(NK):
                nc.vector.memset(shift_c[:, k:k + 1], float(-k))
            nc.vector.memset(eps_c[:, :], EPS).then_inc(dve_consts, 1)
            dve.wait_ge(ld_v, 16)
            for b in range(B):
                dve.wait_ge(ld_x[b], 16)
                link(nc.vector.bn_stats(gn_st[:, b, :], x_sb[:, b * HW:(b + 1) * HW]))
                link(nc.vector.bn_aggr(gn_mv[:, b, :], gn_st[:, b, :]))
            link(nc.vector.tensor_tensor(gn_sq[:, :], gn_mv[:, :, 0], gn_mv[:, :, 0], ALU.mult))
            nc.vector.tensor_tensor(gn_mv[:, :, 1], gn_mv[:, :, 1], gn_sq[:, :], ALU.add).then_inc(gn_moments, 1)
            dve.wait_ge(gn_grouped, 1)
            link(nc.vector.tensor_copy(gn_g[:, :, :], ps[:, 0, 0:2 * B].rearrange("c (b m) -> c b m", b=B)))
            link(nc.vector.tensor_tensor(gn_sq[:, :], gn_g[:, :, 0], gn_g[:, :, 0], ALU.mult))
            nc.vector.tensor_tensor(gn_var[:, :], gn_g[:, :, 1], gn_sq[:, :], ALU.subtract).then_inc(gn_varied, 1)
            dve.wait_ge(gn_stded, 1)
            link(nc.vector.reciprocal(gn_std[:, :], gn_std[:, :]))
            link(nc.vector.tensor_scalar(gn_scale[:, :], gn_std[:, :], V("gn_g"), None, ALU.mult))
            link(nc.vector.tensor_tensor(gn_sq[:, :], gn_g[:, :, 0], gn_scale[:, :], ALU.mult))
            link(nc.vector.tensor_scalar(gn_shift[:, :], gn_sq[:, :], -1.0, V("gn_b"), ALU.mult, ALU.add))
            for b in range(B):
                cols = slice(b * HW, (b + 1) * HW)
                nc.vector.tensor_scalar(xn[:, cols], x_sb[:, cols], gn_scale[:, b:b + 1], gn_shift[:, b:b + 1],
                                        ALU.mult, ALU.add).then_inc(xn_ready, 1)
            dve.wait_ge(consts, CONSTS)
            nc.vector.tensor_copy(ident_b[:, :], ident[:, :])
            nc.vector.tensor_copy(row_f[:, :], row_i[:, :])
            nc.vector.tensor_copy(expert_f[:, :], expert_i[:, :])
            nc.vector.tensor_scalar(vb_bc[:, :], ones_mean[:, :], float(P), V("vproj_b"),
                                    ALU.mult, ALU.mult).then_inc(dve_consts, 1)
            dve.wait_ge(fuse_mm, 1)
            nc.vector.tensor_copy(w_val[:, :], ps[:, 4, 0:128]).then_inc(fuse_ready, 1)
            nc.vector.tensor_copy(w_out[:, :], ps[:, 4, 128:256]).then_inc(fuse_ready, 1)
            dve.wait_ge(ld_r, 16)
            nc.vector.tensor_tensor(b_val[:, :], ps[:, 4, 256:384], r_sb[:, 0:C], ALU.add).then_inc(fuse_ready, 1)
            nc.vector.tensor_tensor(b_out[:, :], ps[:, 4, 384:385], V("dout_b"), ALU.add).then_inc(fuse_ready, 1)

            ln(lns["ln1"], t0, nrm)
            for t in range(TILES):
                dve.wait_ge(proj_mm, 2 * (t // 2) + 2)
                nc.vector.tensor_tensor(proj[:, t, :], ps[:, 4 + t // 2, 256 * (t % 2):256 * (t % 2) + 3 * HP],
                                        r_sb[:, C:], ALU.add).then_inc(proj_ready, 1)
            dve.wait_ge(fuse_ready, 4)
            for n in range(B * NK):
                b, k = n // NK, n % NK
                rows_k = P if k < 2 else P - 1
                dve.wait_ge(val_mm, 4 * (n // 4) + 4)
                nc.vector.tensor_tensor(val[0:rows_k, b, :, k, :],
                                        ps[0:rows_k, n // 4, 128 * (n % 4):128 * (n % 4) + 128].rearrange(
                                            "p (h d) -> p h d", h=NH),
                                        b_val[0:rows_k, :].rearrange("p (h d) -> p h d", h=NH),
                                        ALU.add).then_inc(val_ready, 1)
            dve.wait_ge(proj_ready, TILES)
            nc.vector.tensor_scalar(y_pos[:, :, :], proj[:, :, HP:2 * HP], 1.0, (HW - 1) / 2, ALU.mult, ALU.add)
            link(nc.vector.tensor_scalar(y_half[:, :, :], proj[:, :, HP:2 * HP], 0.5, (HW - 3) / 4, ALU.mult, ALU.add))
            link(nc.vector.tensor_scalar(y_half[:, :, :], y_half[:, :, :], 0.0, float(HW // 2 - 1), ALU.max, ALU.min))
            link(nc.vector.tensor_scalar(pair[:, :, :], y_half[:, :, :], ROUND, -ROUND, ALU.add, ALU.add))
            nc.vector.tensor_copy(pair_b[:, :, :], pair[:, :, :]).then_inc(pair_ready, 1)
            nc.vector.scalar_tensor_tensor(out=y_rest[:, :, :], in0=pair[:, :, :], scalar=-2.0, in1=y_pos[:, :, :],
                                           op0=ALU.mult, op1=ALU.add).then_inc(rest_ready, 1)
            logits = proj[:, :, 2 * HP:].rearrange("q t (h p) -> q t h p", p=NP)
            l3 = lmax[:, :].rearrange("q (t h) -> q t h", h=NH)
            a4 = aw[:, :, :].rearrange("q (t h) p -> q t h p", h=NH)
            link(nc.vector.tensor_reduce(l3, logits, AX_X, ALU.max))
            nc.vector.tensor_tensor(a4, logits, l3.unsqueeze(3).to_broadcast([P, TILES, NH, NP]),
                                    ALU.subtract).then_inc(logit_sub, 1)
            dve.wait_ge(val_p0, 1)
            nc.vector.tensor_tensor(val_r[:, :, :, :, :], val[:, :, :, :, :], val_p[0][:, :, :, :, :],
                                    ALU.subtract).then_inc(val_r1, 1)
            dve.wait_ge(logit_exp, 1)
            link(nc.vector.tensor_reduce(lsum[:, :], aw[:, :, :], AX_X, ALU.add))
            link(nc.vector.reciprocal(lsum[:, :], lsum[:, :]))
            link(nc.vector.tensor_tensor(aw[:, :, :], aw[:, :, :],
                                         lsum[:, :].unsqueeze(2).to_broadcast([P, TILES * NH, NP]), ALU.mult))
            dve.wait_ge(hat_x_ready, 1)
            flat = aw[:, :, :].rearrange("q (t h) p -> q t (h p)", h=NH)
            link(nc.vector.tensor_tensor(hat_x[:, :, :], hat_x[:, :, :], flat, ALU.mult))
            for k in range(NK):
                dve.wait_ge(hat_y_ready, k + 1)
                nc.vector.tensor_tensor(wk3[:, :, :, k], hat_x[:, :, :], hat_y[:, k, :, :], ALU.mult).then_inc(wk3_ready, 1)
            dve.wait_ge(val_p1, 1)
            nc.vector.tensor_tensor(val_p[2][:, :, :, :, :], val_r[:, :, :, :, :], val_p[1][:, :, :, :, :],
                                    ALU.subtract).then_inc(val_p1, 1)
            nc.vector.memset(lmax[:, 0:1], 0.0).then_inc(bc_used, NP // 2)
            nc.vector.memset(lmax[:, 1:2], 0.0).then_inc(g_free, 2)
            nc.vector.memset(lmax[:, 3:4], 0.0).then_inc(prod_free, 2)
            dve.wait_ge(wk3_ready, NK)

            def one_hots(i, u):
                for c in range(NP // 2):
                    dve.wait_ge(bc_copied, 8 * i + 4 * u + c + 1)
                    nc.vector.tensor_scalar(hot[:, u, 2 * c:2 * c + 2, :, :],
                                            bc_b[:, 2 * c:2 * c + 2, :].rearrange("r c (b q) -> r c b q", b=B),
                                            row_f[:, 0:1], None, ALU.is_equal).then_inc(bc_used, 1)

            def weigh(i, u):
                for c in range(2):
                    dve.wait_ge(g_ready, 4 * i + 2 * u + c + 1)
                    dve.wait_ge(prod_free, 4 * i + 2 * u + c + 1)
                    g = ps[:, 4 + 2 * c:6 + 2 * c, 0:NP * NK * DH].rearrange("q b (n d) -> q b n d", d=DH)
                    w = wk3[:, 4 * c + u:4 * c + u + 3:2, bass.ds(i * NP, NP), :].rearrange("q b p k -> q b (p k)")
                    nc.vector.tensor_tensor(prod[:, c, :, :, :], g,
                                            w.unsqueeze(3).to_broadcast([P, 2, NP * NK, DH]),
                                            ALU.mult).then_inc(g_free, 1)
                for c in range(2):
                    dve.wait_ge(g_free, 4 * i + 2 * u + c + 1 + 2)
                    nc.vector.tensor_reduce(msda[:, 4 * c + u:4 * c + u + 3:2, bass.ds(i, 1), :].rearrange(
                                                "q b h d -> q b (h d)"),
                                            prod[:, c, :, :, :].rearrange("q b n d -> q b d n"),
                                            AX_X, ALU.add).then_inc(prod_free, 1)

            one_hots(0, 0)
            with dve.Fori(0, NH - 1) as i:
                one_hots(i, 1)
                weigh(i, 0)
                one_hots(i + 1, 0)
                weigh(i, 1)
            one_hots(NH - 1, 1)
            weigh(NH - 1, 0)
            weigh(NH - 1, 1)

            for h in range(2):
                dve.wait_ge(out_mm, h + 1)
                nc.vector.scalar_tensor_tensor(out=half(t1, h), in0=ps[:, 6 + h, :], scalar=b_out[:, 0:1],
                                               in1=half(t0, h), op0=ALU.add, op1=ALU.add).then_inc(t1_ready, 1)
            ln(lns["ln3"], t1, nrm)
            n = 0
            for j in range(GE):
                for h in range(2):
                    dve.wait_ge(gelu_ready, n + 1)
                    dve.wait_ge(lin_mm, n + 1)
                    nc.vector.scalar_tensor_tensor(out=half(ff[:, j, :], h), in0=ps[:, 2 + n % 2, :],
                                                   scalar=V("geglu_b", j), in1=gelu_g[:, n % 2, :],
                                                   op0=ALU.add, op1=ALU.mult).then_inc(ff_ready, 1)
                    n += 1
            for h in range(2):
                dve.wait_ge(dense_mm, h + 1)
                nc.vector.scalar_tensor_tensor(out=half(t2, h), in0=ps[:, 4 + h, :], scalar=V("dense_b"),
                                               in1=half(t1, h), op0=ALU.add, op1=ALU.add).then_inc(t2_ready, 1)
            for h in range(2):
                dve.wait_ge(pout_mm, h + 1)
                nc.vector.scalar_tensor_tensor(out=half(x1, h), in0=ps[:, 6 + h, :], scalar=V("pout_b"),
                                               in1=half(x_sb, h), op0=ALU.add, op1=ALU.add).then_inc(x1_ready, 1)
            ln(lns["lna"], x1, z1)

            dve.wait_ge(lns["lna"]["norm"], 2)
            nc.vector.memset(lmax[:, 4:5], 0.0).then_inc(pt_mm, 2)
            nc.vector.memset(lmax[:, 6:7], 0.0).then_inc(v_mm, 1)
            with dve.Fori(0, B) as b:
                dve.wait_ge(v_mm, b + 1)
                nc.vector.tensor_copy(zb[:, :], z1[:, bass.ds(b * HW, HW)]).then_inc(zb_ready, 1)
                dve.wait_ge(v_mm, b + 2)
                nc.vector.tensor_copy(v_tok[:, :, :, 0:AD],
                                      ps[:, 2, 0:2 * P].rearrange("t (k h d) -> t k h d", k=2, h=AH)).then_inc(v_ready, 1)

                def row_max(h):
                    dve.wait_ge(sc_mm, AH * b + h + 1)
                    nc.vector.tensor_reduce(nmax[:, h % 2, :], ps[:, h % 2, :].rearrange("q (t k) -> q t k", t=2),
                                            AX_X, ALU.max, negate=True).then_inc(nmax_ready, 1)

                row_max(0)
                for h in range(AH):
                    if h + 1 < AH:
                        row_max(h + 1)
                    dve.wait_ge(pt_mm, AH * b + h + 1 + 2)
                    if h >= 2:
                        dve.wait_ge(pv_mm, AH * b + h - 1)
                    nc.vector.tensor_copy(prob_t[:, h % 2, :, :],
                                          ps[:, 4 + h % 2, :].rearrange("k (a q) -> k a q", a=4)).then_inc(pt_ready, 1)
                dve.wait_ge(pv_mm, AH * b + AH)
                o_ps = ps[:, 6, 0:2 * AH * AD1].rearrange("q (t h d) -> q t h d", t=2, h=AH)
                nc.vector.reciprocal(inv_sum[:, :, :], o_ps[:, :, :, AD]).then_inc(inv_ready, 1)
                dve.wait_ge(inv_ready, b + 1)
                nc.vector.tensor_tensor(o_tok[:, :, :, :], o_ps[:, :, :, 0:AD],
                                        inv_sum[:, :, :].unsqueeze(3).to_broadcast([P, 2, AH, AD]),
                                        ALU.mult).then_inc(o_ready, 1)
                dve.wait_ge(ot_mm, b + 1)
                nc.vector.tensor_copy(o_c[:, bass.ds(b * HW, HW)], ps[:, 7, 0:HW]).then_inc(o_c_ready, 1)
            for h in range(2):
                dve.wait_ge(ap_mm, h + 1)
                nc.vector.tensor_tensor(half(x2, h), ps[:, 4 + h, :], half(x1, h), ALU.add).then_inc(x2_ready, 1)
            ln(lns["lnf"], x2, z2)

            link(nc.vector.memset(chosen_b, 0.0))
            dve.wait_ge(lg_mm, 1)
            link(nc.vector.tensor_copy(lg[:, :, :], ps[:, 4, 0:TILES * E].rearrange("t (n e) -> t n e", e=E)))
            for t in range(TILES):
                ins = nc.vector.max(top[:, t, :], lg[:, t, :])
            link(ins)
            nc.vector.tensor_tensor(gap[:, :], top[:, :, 1], top[:, :, 0], ALU.subtract).then_inc(gap_ready, 1)
            for t in range(TILES):
                ins = nc.vector.max_index(top_i[:, t, :], top[:, t, :], lg[:, t, :])
            link(ins)
            link(nc.vector.tensor_copy(top_f[:, :, :], top_i[:, :, 0:TOPK]))
            ex = expert_f[:, :].unsqueeze(1).to_broadcast([P, TILES, E])
            nc.vector.tensor_tensor(oh1[:, :, :], ex, top_f[:, :, 0:1].to_broadcast([P, TILES, E]), ALU.is_equal)
            link(nc.vector.tensor_tensor(oh2[:, :, :], ex, top_f[:, :, 1:2].to_broadcast([P, TILES, E]), ALU.is_equal))
            link(nc.vector.tensor_tensor(chosen[:, :, :], oh1[:, :, :], oh2[:, :, :], ALU.add))
            nc.vector.tensor_copy(chosen_b[:, :, 0:E], chosen[:, :, :]).then_inc(route_ready, 1)
            dve.wait_ge(e2_ready, 1)
            link(nc.vector.tensor_scalar(e2p[:, :], e2[:, :], 1.0, None, ALU.add))
            link(nc.vector.reciprocal(rw1[:, :], e2p[:, :]))
            link(nc.vector.tensor_tensor(rw2[:, :], e2[:, :], rw1[:, :], ALU.mult))
            nc.vector.tensor_tensor(oh1[:, :, :], oh1[:, :, :], rw1[:, :].unsqueeze(2).to_broadcast([P, TILES, E]), ALU.mult)
            link(nc.vector.tensor_tensor(oh2[:, :, :], oh2[:, :, :],
                                         rw2[:, :].unsqueeze(2).to_broadcast([P, TILES, E]), ALU.mult))
            nc.vector.tensor_tensor(route[:, :, :], oh1[:, :, :], oh2[:, :, :], ALU.add).then_inc(route_ready, 1)
            dve.wait_ge(rt_mm, TILES)
            nc.vector.tensor_copy(chosen_t[:, :], ps[:, 0, :].bitcast(BF16)).then_inc(route_t_ready, 1)
            dve.wait_ge(rt_mm, 2 * TILES)
            nc.vector.tensor_copy(route_t[:, :], ps[0:E, 6:8, :].rearrange("e a t -> e (a t)")).then_inc(route_t_ready, 1)
            dve.wait_ge(cnt_mm, 1)
            link(nc.vector.tensor_scalar(cnt[:, :], ps[:, 5, 0:E], float(P), 1.0, ALU.mult, ALU.max))
            link(nc.vector.reciprocal(inv_cnt[:, :], cnt[:, :]))

            nc.vector.memset(lmax[:, 5:6], 0.0).then_inc(h_used, 2)
            with dve.Fori(0, E // 2) as i:
                for n in range(2):
                    for h in range(2):
                        dve.wait_ge(mb_mm, 4 * i + 2 * n + h + 1)
                        nc.vector.tensor_tensor(xm[:, n, h * HALF:(h + 1) * HALF], half(z2, h), ps[:, h, :],
                                                ALU.mult).then_inc(xm_ready, 1)
            dve.wait_ge(h_used, E * FT + 2)
            nc.vector.tensor_tensor(h_mean[:, :, :], h_sum[:, :, :],
                                    inv_cnt[:, :].unsqueeze(2).to_broadcast([P, E, FT]), ALU.mult).then_inc(hmean_ready, 1)
            dve.wait_ge(y_mm, 1)
            nc.vector.tensor_copy(y_t[:, :], ps[:, 0, 0:E]).then_inc(y_t_ready, 1)
            dve.wait_ge(yt_mm, 1)
            nc.vector.tensor_copy(y_mean[:, :], ps[0:E, 1, 0:P]).then_inc(y_ready, 1)
            for h in range(2):
                dve.wait_ge(moe_mm, h + 1)
                nc.vector.tensor_tensor(half(y_out, h), half(x2, h), ps[:, 2 + h, :], ALU.add).then_inc(y_out_ready, 1)

        @block.tensor
        def _(pe):
            def ln(s, ready, src):
                for h in range(2):
                    pe.wait_ge(ready, h + 1)
                    nc.tensor.matmul(ps[:, h, :], ones_mean[:, :], half(src, h)).then_inc(s["mean"], 1)
                for h in range(2):
                    pe.wait_ge(s["sq"], h + 1)
                    nc.tensor.matmul(ps[:, 2 + h, :], ones_mean[:, :], half(sq, h)).then_inc(s["var"], 1)

            pe.wait_ge(dve_consts, 1)
            pe.wait_ge(consts, CONSTS)
            pe.wait_ge(gn_moments, 1)
            nc.tensor.matmul(ps[:, 0, 0:2 * B], group_mean[:, :],
                             gn_mv[:, :, :].rearrange("c b m -> c (b m)")).then_inc(gn_grouped, 1)
            pe.wait_ge(ld_wa, 16)
            for h in range(2):
                pe.wait_ge(xn_ready, 2 * h + 2)
                nc.tensor.matmul(ps[:, h, :], W("pin"), half(xn, h)).then_inc(pin_mm, 1)
            pe.wait_ge(ld_wb, 16)
            pe.wait_ge(dve_consts, 2)
            nc.tensor.matmul(ps[:, 4, 0:128], W("vprojT"), W("mvp"))
            nc.tensor.matmul(ps[:, 4, 128:256], W("mopT"), W("dout"))
            nc.tensor.matmul(ps[:, 4, 256:384], vb_bc[:, :], W("mvp"))
            nc.tensor.matmul(ps[:, 4, 384:385], W("dout"), V("mop_b")).then_inc(fuse_mm, 1)
            ln(lns["ln1"], t0_ready, t0)
            pe.wait_ge(fuse_ready, 4)
            soff_attw = w_sb[:, WAT["soff"][0]:WAT["attw"][1]]
            for t in range(TILES):
                pe.wait_ge(lns["ln1"]["out"], t // (TILES // 2) + 1)
                nc.tensor.matmul(ps[:, 4 + t // 2, 256 * (t % 2):256 * (t % 2) + 3 * HP], q_c[:, t * P:(t + 1) * P],
                                 soff_attw).then_inc(proj_mm, 1)
            for n in range(B * NK):
                b, k = n // NK, n % NK
                rows_k = P if k < 2 else P - 1
                first = b * HW + k
                nc.tensor.matmul(ps[0:rows_k, n // 4, 128 * (n % 4):128 * (n % 4) + 128],
                                 q_c[:, first:first + 2 * rows_k - 1:2], w_val[:, :]).then_inc(val_mm, 1)
            pe.wait_ge(pair_ready, 1)
            pe.wait_ge(proj_ready, TILES)
            for b in range(B):
                nc.tensor.transpose(ps[:, 5, 64 * b:64 * b + 64].bitcast(BF16),
                                    pair_b[:, 2 * b:2 * b + 2, :].rearrange("q t r -> q (t r)"),
                                    ident_b[:, :]).then_inc(pair_mm, 1)
            pe.wait_ge(pair_t_ready, 1)
            pe.wait_ge(val_p1, 2)
            pe.wait_ge(val_ready, B * NK)
            pe.wait_ge(g_free, 2)

            def broadcast(i, u):
                for p in range(NP):
                    c = p // 2
                    if p % 2 == 0 and not (isinstance(i, int) and u == 0 and i == 0 and c < 2):
                        pe.wait_ge(bc_copied, 8 * i + 4 * u + c - 1)
                    row = ident_b[:, bass.ds(i * NP + (u * HP + p), 1)].to_broadcast([P, P])
                    ins = nc.tensor.matmul(ps[:, 2 * (c % 2) + p % 2, :], row,
                                           pair_t[:, :, :].rearrange("r b q -> r (b q)"))
                    if p % 2:
                        ins.then_inc(bc_ready, 1)

            def gather(i, u):
                pe.wait_ge(bc_used, 8 * i + 4 * u + 4 + NP // 2)
                for b in range(B):
                    if b % 2 == 0:
                        pe.wait_ge(g_free, 4 * i + 2 * u + b // 2 + 1)
                    for p in range(NP):
                        for s in range(PARTS):
                            rhs = val_p[s][:, b, bass.ds(i, 1), :, :].rearrange("r h k d -> r (h k d)")
                            ins = nc.tensor.matmul(ps[:, 4 + b, p * NK * DH:(p + 1) * NK * DH], hot[:, u, p, b, :], rhs,
                                                   start=(s == 0), stop=(s == PARTS - 1))
                    if b == 1:
                        ins.then_inc(g_ready, 1)
                ins.then_inc(g_ready, 1)

            broadcast(0, 0)
            with pe.Fori(0, NH - 1) as i:
                broadcast(i, 1)
                gather(i, 0)
                broadcast(i + 1, 0)
                gather(i, 1)
            broadcast(NH - 1, 1)
            gather(NH - 1, 0)
            gather(NH - 1, 1)

            pe.wait_ge(prod_free, 4 * NH + 2)
            for t in range(TILES):
                nc.tensor.transpose(ps[:, 4 + t // 4, P * (t % 4):P * (t % 4) + P],
                                    msda[:, t, :, :].rearrange("q h d -> q (h d)"), ident[:, :]).then_inc(msda_mm, 1)
            for h in range(2):
                nc.tensor.matmul(ps[:, 6 + h, :], W("dout"), half(q_c, h), start=True, stop=False)
                pe.wait_ge(msda_c_ready, h + 1)
                nc.tensor.matmul(ps[:, 6 + h, :], w_out[:, :], half(msda_c, h), start=False, stop=True).then_inc(out_mm, 1)
            ln(lns["ln3"], t1_ready, t1)
            n = 0
            geglu = W("geglu")
            for j in range(GE):
                for h in range(2):
                    pe.wait_ge(lns["ln3"]["out"], h + 1)
                    if n == 0:
                        pe.wait_ge(lns["ln3"]["std"], 2)
                    if n >= 2:
                        pe.wait_ge(gelu_ready, n - 1)
                    nc.tensor.matmul(ps[:, n % 2, :], geglu[:, (GE + j) * P:(GE + j + 1) * P], half(hn, h)).then_inc(gate_mm, 1)
                    if n >= 2:
                        pe.wait_ge(ff_ready, n - 1)
                    nc.tensor.matmul(ps[:, 2 + n % 2, :], geglu[:, j * P:(j + 1) * P], half(hn, h)).then_inc(lin_mm, 1)
                    n += 1
            dense = W("dense")
            for h in range(2):
                for j in range(GE):
                    pe.wait_ge(ff_ready, 2 * j + h + 1)
                    ins = nc.tensor.matmul(ps[:, 4 + h, :], dense[:, j * P:(j + 1) * P], half(ff[:, j, :], h),
                                           start=(j == 0), stop=(j == GE - 1))
                ins.then_inc(dense_mm, 1)
            for h in range(2):
                pe.wait_ge(t2_ready, h + 1)
                nc.tensor.matmul(ps[:, 6 + h, :], W("pout"), half(t2, h)).then_inc(pout_mm, 1)
            ln(lns["lna"], x1_ready, x1)

            pe.wait_ge(ld_qk, 32)
            pe.wait_ge(lns["lna"]["std"], 2)
            with pe.Fori(0, B) as b:
                pe.wait_ge(zb_ready, b + 1)
                for g in range(2):
                    nc.tensor.matmul(ps[:, 0, g * HW:(g + 1) * HW],
                                     wq_sb[:, 4 * g:4 * g + 4, :].rearrange("c h d -> c (h d)"), zb[:, :])
                for g in range(2):
                    ins = nc.tensor.matmul(ps[:, 1, g * HW:(g + 1) * HW],
                                           wk_sb[:, 4 * g:4 * g + 4, :].rearrange("c h d -> c (h d)"), zb[:, :])
                ins.then_inc(qk_mm, 1)
                for t in range(2):
                    ins = nc.tensor.matmul(ps[:, 2, t * P:(t + 1) * P], zb[:, t * P:(t + 1) * P], W("wv"))
                ins.then_inc(v_mm, 1)

                def scores(h):
                    if h >= 2:
                        pe.wait_ge(prob_ready, 2 * AH * b + 2 * (h - 1))
                    r = 32 * (h % 4)
                    for t in range(2):
                        ins = nc.tensor.matmul(ps[:, h % 2, t * HW:(t + 1) * HW],
                                               qp[r:r + AD, h // 4, t * P:(t + 1) * P], kp[r:r + AD, h // 4, :])
                    ins.then_inc(sc_mm, 1)

                pe.wait_ge(qk_ready, 2 * b + 2)
                scores(0)
                scores(1)
                for h in range(AH):
                    pe.wait_ge(prob_ready, 2 * AH * b + 2 * (h + 1))
                    if h >= 2:
                        pe.wait_ge(pt_ready, AH * b + h - 1)
                    for a in range(4):
                        kt, qt = a // 2, a % 2
                        ins = nc.tensor.transpose(ps[:, 4 + h % 2, a * P:(a + 1) * P],
                                                  prob[:, h % 2, qt, kt * P:(kt + 1) * P], ident[:, :])
                    ins.then_inc(pt_mm, 1)
                    if h + 2 < AH:
                        scores(h + 2)
                    pe.wait_ge(pt_ready, AH * b + h + 1)
                    if h == 0:
                        pe.wait_ge(v_ready, b + 1)
                    for qt in range(2):
                        at_o = (qt * AH + h) * AD1
                        for kt in range(2):
                            ins = nc.tensor.matmul(ps[:, 6, at_o:at_o + AD1], prob_t[:, h % 2, 2 * kt + qt, :],
                                                   v_tok[:, kt, h, :], start=(kt == 0), stop=(kt == 1))
                    ins.then_inc(pv_mm, 1)
                pe.wait_ge(o_ready, b + 1)
                for t in range(2):
                    ins = nc.tensor.transpose(ps[:, 7, t * P:(t + 1) * P],
                                              o_tok[:, t, :, :].rearrange("q h d -> q (h d)"), ident[:, :])
                ins.then_inc(ot_mm, 1)
            for h in range(2):
                pe.wait_ge(o_c_ready, 2 * h + 2)
                nc.tensor.matmul(ps[:, 4 + h, :], W("wproj"), half(o_c, h)).then_inc(ap_mm, 1)
            ln(lns["lnf"], x2_ready, x2)

            pe.wait_ge(x2_ready, 2)
            for t in range(TILES):
                pe.wait_ge(lns["lnf"]["norm"], t // (TILES // 2) + 1)
                ins = nc.tensor.matmul(ps[:, 4, t * E:(t + 1) * E], z2[:, t * P:(t + 1) * P], W("gate"))
            ins.then_inc(lg_mm, 1)
            pe.wait_ge(route_ready, 1)
            for t in range(TILES):
                nc.tensor.transpose(ps[:, 0, 64 * t:64 * t + 64].bitcast(BF16), chosen_b[:, t, :],
                                    ident_b[:, :]).then_inc(rt_mm, 1)
            for t in range(TILES):
                ins = nc.tensor.matmul(ps[:, 5, 0:E], ones_mean[:, :], chosen[:, t, :], start=(t == 0), stop=(t == TILES - 1))
            ins.then_inc(cnt_mm, 1)
            pe.wait_ge(route_ready, 2)
            for t in range(TILES):
                nc.tensor.transpose(ps[0:E, 6 + t // 4, P * (t % 4):P * (t % 4) + P], route[:, t, :],
                                    ident[:, :]).then_inc(rt_mm, 1)
            pe.wait_ge(route_t_ready, 2)
            pe.wait_ge(lns["lnf"]["std"], 2)
            pe.wait_ge(h_used, 2)

            def choose(e, first=False):
                for h in range(2):
                    if not first:
                        pe.wait_ge(xm_ready, 2 * e + h - 1)
                    nc.tensor.matmul(ps[:, h, :], ident_b[:, bass.ds(e, 1)].to_broadcast([P, P]),
                                     half(chosen_t, h)).then_inc(mb_mm, 1)

            def hidden(i, n):
                pe.wait_ge(ld_w1[n], 16 * i + 16)
                pe.wait_ge(xm_ready, 4 * i + 2 * n + 2)
                for f in range(FT):
                    pe.wait_ge(h_used, 2 * FT * i + FT * n + f + 1)
                    c = 2 + 2 * ((FT * n + f) % 2)
                    for h in range(2):
                        ins = nc.tensor.matmul(ps[:, c + h, :], w1_sb[:, n, f * P:(f + 1) * P],
                                               xm[:, n, h * HALF:(h + 1) * HALF])
                    ins.then_inc(h_mm, 1)

            choose(0, first=True)
            with pe.Fori(0, E // 2 - 1) as i:
                choose(2 * i + 1)
                hidden(i, 0)
                choose(2 * i + 2)
                hidden(i, 1)
            choose(E - 1)
            hidden(E // 2 - 1, 0)
            hidden(E // 2 - 1, 1)
            pe.wait_ge(hmean_ready, 1)
            pe.wait_ge(ld_w2, 16)
            for e in range(E):
                for f in range(FT):
                    ins = nc.tensor.matmul(ps[:, 0, e:e + 1], w2_sb[:, e * FT + f, :], h_mean[:, e, f:f + 1],
                                           start=(f == 0), stop=(f == FT - 1))
            ins.then_inc(y_mm, 1)
            pe.wait_ge(y_t_ready, 1)
            nc.tensor.transpose(ps[0:E, 1, 0:P], y_t[:, :], ident[:, :]).then_inc(yt_mm, 1)
            pe.wait_ge(y_ready, 1)
            for h in range(2):
                nc.tensor.matmul(ps[:, 2 + h, :], y_mean[:, :], half(route_t, h)).then_inc(moe_mm, 1)


def kernel(**inputs):
    import numpy as np
    import concourse.bacc as bacc
    from concourse.bass_utils import run_bass_kernel_spmd as run

    a = {n: np.asarray(v) for n, v in inputs.items()}

    def L(n):
        return a["L0_conv_" + n]

    soff_w = L("soff_w").reshape(C, HP, 2).transpose(0, 2, 1).reshape(C, 2 * HP)
    soff_b = L("soff_b").reshape(HP, 2).transpose(1, 0).reshape(2 * HP)
    parts = dict(pin=L("pin_w"), vprojT=L("vproj_w").T, mvp=L("mvp_w"), soff=soff_w, attw=L("attw_w"),
                 mopT=L("mop_w").T, dout=L("dout_w"), geglu=L("geglu_w"),
                 dense=L("dense_w").reshape(GE, P, C).transpose(1, 0, 2).reshape(P, GE * C),
                 pout=L("pout_w"), wv=a["L1_attn_wv"].T, wproj=a["L1_attn_wproj"].T, gate=a["L1_ffn_gate_weight"].T)
    vecs = {n: L(n).reshape(-1, P).T for n in VCOLS}
    arrays = dict(
        x=a["x"].reshape(B, C, HW),
        weights=np.concatenate([parts[n] for n in WCOLS], axis=1),
        vectors=np.concatenate([vecs[n] for n in VCOLS], axis=1),
        rows=np.concatenate([L("mvp_b"), soff_b, L("attw_b")]).reshape(1, RTOTAL),
        wq_t=a["L1_attn_wq"].T.reshape(C, AH, AD),
        wk_t=a["L1_attn_wk"].T.reshape(C, AH, AD),
        w1_t=a["L1_ffn_w1"].transpose(0, 2, 1),
        w2_t=a["L1_ffn_w2"].transpose(2, 0, 1).reshape(FT, P, E, C).transpose(1, 2, 0, 3).reshape(P, E * FT, C),
    )
    nc = bacc.Bacc("TRN2", target_bir_lowering=False, num_devices=1)
    feeds, args = {}, []
    for name, v in arrays.items():
        v = np.ascontiguousarray(v)
        feeds[f"in_{name}"] = v
        args.append(nc.dram_tensor(f"in_{name}", v.shape, F32, kind="ExternalInput").ap())
    out = nc.dram_tensor("out", (B, C, HW), F32, kind="ExternalOutput").ap()
    build(nc, *args, out)
    r = run(nc, [feeds], core_ids=[0])
    return r.results[0]["out"].reshape(B, C, 16, 16)
```

```python
from contextlib import ExitStack

import concourse.bass as bass
from concourse import mybir

ALU = mybir.AluOpType
ACT = mybir.ActivationFunctionType
AX_X = mybir.AxisListType.X
F32 = mybir.dt.float32
BF16 = mybir.dt.bfloat16
F32R = mybir.dt.float32r
U32 = mybir.dt.uint32
I32 = mybir.dt.int32

P = 128
B, C, HW = 4, 128, 256
T = B * HW
TILES = T // P
HALF = T // 2
NH, DH, NP = 8, 16, 8
HP = NH * NP
GROUPS = 8
NK = 3
PARTS = 3
AH, AD = 8, 16
AD1 = AD + 1
E, TOPK, F = 16, 2, 512
FT = F // P
GE = 4
EPS = 1e-5
ROUND = 1.5 * 2 ** 23

def columns(**widths):
    at, where = 0, {}
    for name, n in widths.items():
        where[name] = (at, at + n)
        at += n
    return where, at


WAT, WTOTAL = columns(pin=C, vprojT=C, mvp=C, soff=2 * HP, attw=HP, mopT=C, dout=C,
                      geglu=2 * GE * P, denseT=GE * P, pout=C, wv=C, wproj=C, gate=E)
VAT, VTOTAL = columns(gn_g=1, gn_b=1, ln1_g=1, ln1_b=1, vproj_b=1, mop_b=1,
                      ln3_g=1, ln3_b=1, geglu_b=2 * GE, dense_b=1)
RAT, RTOTAL = columns(mvp_b=C, soff_b=2 * HP, attw_b=HP, pin_b=C, dout_b=C, pout_b=C)


def build(nc, x, weights, vectors, rows, wq_t, wk_t, w1_t, w2_t, out):
    with ExitStack() as ctx:
        def sb(name, shape, dt=F32):
            return ctx.enter_context(nc.sbuf_tensor(name, shape, dt))

        def sem(name):
            return ctx.enter_context(nc.semaphore(name))

        ps = ctx.enter_context(nc.psum_tensor("ps", [P, 8, 512], F32))

        ones_mean = sb("ones_mean", [P, P])
        ident = sb("ident", [P, P])
        ident_b = sb("ident_b", [P, P], BF16)
        group_mean = sb("group_mean", [P, P])
        row_i = sb("row_i", [P, 1], I32)
        row_f = sb("row_f", [P, 1])
        one_less_sq = sb("one_less_sq", [P, 1])
        expert_i = sb("expert_i", [P, E], I32)
        expert_f = sb("expert_f", [P, E])
        own_i = sb("own_i", [P, E, E], I32)
        own_f = sb("own_f", [P, E, E])
        eps_c = sb("eps_c", [P, 1])
        one_c = sb("one_c", [P, 1])
        zero_c = sb("zero_c", [P, E])
        shift_c = sb("shift_c", [P, NK])
        sel = sb("sel", [P, 4, NP, P], BF16)
        w_sb = sb("w_sb", [P, WTOTAL])
        v_sb = sb("v_sb", [P, VTOTAL])
        r_sb = sb("r_sb", [P, RTOTAL])
        wq_sb = sb("wq_sb", [P, AH, 32])
        wk_sb = sb("wk_sb", [P, AH, 32])
        w1_sb = sb("w1_sb", [P, 2, F])
        w1_h = sb("w1_h", [P, 2, F], F32R)
        w1_l = sb("w1_l", [P, 2, F], F32R)
        arena = sb("arena", [P, E * FT * P])
        w2_sb = arena[:, :].rearrange("f (n d) -> f n d", d=P)

        def W(name):
            a, b = WAT[name]
            return w_sb[:, a:b]

        def V(name, j=0):
            a, _ = VAT[name]
            return v_sb[:, a + j:a + j + 1]

        def R(name):
            a, b = RAT[name]
            return r_sb[:, a:b]

        def tok(name):
            return sb(name, [P, TILES, C])

        x_sb = sb("x_sb", [P, T])
        xn = sb("xn", [P, T])
        t0_k = tok("t0_k")
        nrm = tok("nrm")
        q_c = sb("q_c", [P, T])
        msda_c = xn
        t1_k = tok("t1_k")
        t1_c = sb("t1_c", [P, T])
        hn = q_c
        gelu_g = sb("gelu_g", [P, 2, HALF])
        ff = sb("ff", [P, GE, T])
        x1_k = tok("x1_k")
        z1 = q_c
        o_c = xn
        x2_k = t1_k
        z2 = q_c
        x2_c = t1_c
        y_out = xn
        gn_st = sb("gn_st", [P, B, 6])
        gn_mv = sb("gn_mv", [P, B, 2])
        gn_sq = sb("gn_sq", [P, B])
        gn_g = sb("gn_g", [P, B, 2])
        gn_var = sb("gn_var", [P, B])
        gn_std = sb("gn_std", [P, B])
        gn_scale = sb("gn_scale", [P, B])
        gn_shift = sb("gn_shift", [P, B])
        ln_st = sb("ln_st", [P, TILES, 6])
        ln_mv = sb("ln_mv", [P, TILES, 2])
        ln_std = sb("ln_std", [P, TILES])
        ln_rstd = sb("ln_rstd", [P, TILES])
        w_val = sb("w_val", [P, P])
        w_out = sb("w_out", [P, P])
        w_dp = sb("w_dp", [P, GE, P])
        bias_c = sb("bias_c", [P, 3, P])
        b_val = sb("b_val", [P, P])
        b_out = sb("b_out", [P, P])
        b_dp = sb("b_dp", [P, P])
        proj = sb("proj", [P, TILES, 3 * HP])
        hat_x = sb("hat_x", [P, TILES, HP])
        lmax = sb("lmax", [P, TILES * NH])
        lsum = sb("lsum", [P, TILES * NH])
        aw = sb("aw", [P, TILES * NH, NP])
        y_pos = sb("y_pos", [P, TILES, HP])
        y_half = sb("y_half", [P, TILES, HP])
        pair = sb("pair", [P, TILES, HP])
        pair_sq = sb("pair_sq", [P, TILES, HP])
        terms = sb("terms", [P, TILES, NH, 4, NP], BF16)
        y_rest = sb("y_rest", [P, TILES, HP])
        hat_y = sb("hat_y", [P, NK, TILES, HP])
        wk3 = sb("wk3", [P, TILES, HP, NK])
        terms_t = sb("terms_t", [P, 2, T], BF16)
        val = sb("val", [P, B, NH, NK, DH])
        n_val = B * NH * NK * DH
        hot_words = 2 * NP * HALF // 2
        hot = arena[:, 0:hot_words].bitcast(BF16).rearrange("r (u p b q) -> r u p b q", u=2, p=NP, b=B)
        val_p = [arena[:, hot_words + i * n_val // 2:hot_words + (i + 1) * n_val // 2].bitcast(BF16).rearrange(
            "r (b h k d) -> r b h k d", b=B, h=NH, k=NK) for i in range(PARTS)]
        at_r = hot_words + PARTS * n_val // 2
        val_r = arena[:, at_r:at_r + n_val].rearrange("r (b h k d) -> r b h k d", b=B, h=NH, k=NK)
        prod = hat_y[:, :, :, :].rearrange("q k t r -> q (k t r)").rearrange(
            "q (s b n d) -> q s b n d", s=2, b=2, d=DH)
        msda = sb("msda", [P, TILES, NH, DH])
        qp = ff[:, 0:2, :]
        kp = ff[:, 2:4, :]
        qb = gelu_g[:, :, :].rearrange("c s (g t) -> c s g t", g=2)
        kb = x_sb[:, :].rearrange("c (s g t) -> c s g t", s=2, g=2)
        v_tok = sb("v_tok", [P, TILES, AH, AD1])
        nmax = sb("nmax", [P, 4, 2])
        prob = proj[:, :, :].rearrange("q t n -> q (t n)")[:, 0:2 * 2 * HW].rearrange(
            "q (s t k) -> q s t k", s=2, t=2)
        prob_t = wk3[:, :, :, :].rearrange("q t n k -> q (t n k)")[:, 0:2 * 4 * P].rearrange(
            "k (s a q) -> k s a q", s=2, a=4)
        inv_sum = sb("inv_sum", [P, 2, AH])
        o_tok = msda
        lg = sb("lg", [P, TILES, E])
        top = sb("top", [P, TILES, 8])
        top_i = sb("top_i", [P, TILES, 8], U32)
        top_f = sb("top_f", [P, TILES, TOPK])
        oh1 = sb("oh1", [P, TILES, E])
        oh2 = sb("oh2", [P, TILES, E])
        chosen = sb("chosen", [P, TILES, E])
        chosen_b = pair_sq[:, :, :].rearrange("t a b -> t (a b)").bitcast(BF16).rearrange(
            "t (a e) -> t a e", a=TILES)
        chosen_t = pair[:, :, :].rearrange("e a b -> e (a b)").bitcast(BF16)
        gap = sb("gap", [P, TILES])
        e2 = sb("e2", [P, TILES])
        e2p = sb("e2p", [P, TILES])
        rw1 = sb("rw1", [P, TILES])
        rw2 = sb("rw2", [P, TILES])
        route = sb("route", [P, TILES, E])
        route_t = val[0:E, :, :, :, :].rearrange("e b h k d -> e (b h k d)")[:, 0:T]
        cnt = sb("cnt", [P, E])
        inv_cnt = sb("inv_cnt", [P, E])
        z2_h = nrm[:, :, :].rearrange("c t k -> c (t k)")
        z2_l = t0_k[:, :, :].rearrange("c t k -> c (t k)")
        xm_h = sb("xm_h", [P, 2, T], F32R)
        xm_l = sb("xm_l", [P, 2, T], F32R)
        silu_junk = y_half[:, :, :].bitcast(BF16).rearrange("f a b -> f (a b)")
        h_sum = sb("h_sum", [P, E, FT])
        h_mean = sb("h_mean", [P, 2, FT])
        h_col = sb("h_col", [P, 2, FT, E])
        y_mean = sb("y_mean", [E, P])

        def sems(names):
            return [sem(n) for n in names.split()]

        ld_x = [sem(f"ld_x{b}") for b in range(B)]
        ld_v, ld_r, ld_wa, ld_wb, ld_qk, ld_w2 = sems("ld_v ld_r ld_wa ld_wb ld_qk ld_w2")
        ld_w1 = sems("ld_w1_even ld_w1_odd")
        stored, pool_step, dve_step, consts, sel_ready, dve_consts = sems(
            "stored pool_step dve_step consts sel_ready dve_consts")
        gn_moments, gn_grouped, gn_varied, gn_stded, xn_ready = sems(
            "gn_moments gn_grouped gn_varied gn_stded xn_ready")
        pin_mm, t0_ready, fuse_mm, fuse_ready = sems("pin_mm t0_ready fuse_mm fuse_ready")
        lns = {n: {k: sem(f"{n}_{k}") for k in ("var", "std", "rstd", "norm", "turned", "out")}
               for n in ("ln1", "ln3", "lna", "lnf")}
        proj_mm, proj_ready, val_mm, val_ready, val_p0, val_r1, val_p1 = sems(
            "proj_mm proj_ready val_mm val_ready val_p0 val_r1 val_p1")
        logit_sub, logit_exp, x_abs, hat_x_ready, rest_ready, y_abs, hat_y_ready = sems(
            "logit_sub logit_exp x_abs hat_x_ready rest_ready y_abs hat_y_ready")
        terms_ready, terms_mm, terms_t_ready, wk3_ready = sems("terms_ready terms_mm terms_t_ready wk3_ready")
        dist_mm, hot_ready, g_ready, g_free, prod_free = sems("dist_mm hot_ready g_ready g_free prod_free")
        msda_mm, msda_c_ready, out_mm, t1_ready, t1_mm, t1_c_ready = sems(
            "msda_mm msda_c_ready out_mm t1_ready t1_mm t1_c_ready")
        gate_mm, lin_mm, gelu_ready, ff_ready, x1_mm, x1_ready = sems(
            "gate_mm lin_mm gelu_ready ff_ready x1_mm x1_ready")
        q_mm, k_mm, q_ready, k_ready, v_mm, v_ready, qb_ready = sems(
            "q_mm k_mm q_ready k_ready v_mm v_ready qb_ready")
        sc_mm, nmax_ready, prob_ready, pt_mm, pt_ready, pv_mm = sems(
            "sc_mm nmax_ready prob_ready pt_mm pt_ready pv_mm")
        inv_ready, o_ready, ot_mm, o_c_ready, ap_mm, x2_ready, x2_mm, x2_c_ready = sems(
            "inv_ready o_ready ot_mm o_c_ready ap_mm x2_ready x2_mm x2_c_ready")
        lg_mm, gap_ready, e2_ready, route_ready, rt_mm, route_t_ready, cnt_mm = sems(
            "lg_mm gap_ready e2_ready route_ready rt_mm route_t_ready cnt_mm")
        z2_parted, w1h_ready, w1_parted, mb_mm, xm_ready, h_mm, h_used = sems(
            "z2_parted w1h_ready w1_parted mb_mm xm_ready h_mm h_used")
        hmean_ready, hcol_ready, y_mm, y_ready, moe_mm, y_out_ready = sems(
            "hmean_ready hcol_ready y_mm y_ready moe_mm y_out_ready")

        def half(t, h):
            return t[:, h * HALF:(h + 1) * HALF]

        def four(t, h):
            return t[:, 4 * h:4 * h + 4, :].rearrange("k t c -> k (t c)")

        def rows4(t):
            return t.unsqueeze(1).to_broadcast([P, 4, P])

        def psum4(bank):
            return ps[:, bank, :].rearrange("k (t c) -> k t c", t=4)

        HOT_CREDIT, G_CREDIT, FREE_CREDIT, H_CREDIT, Y_CREDIT = 2, 3, 2, 2 * FT, 2

        block = ctx.enter_context(nc.Block())

        @block.sync
        def _(sp):
            a = WAT["attw"][1]
            for b in range(B):
                sp.dma_start(x_sb[:, b * HW:(b + 1) * HW], x[b]).then_inc(ld_x[b], 16)
            sp.dma_start(v_sb[:, :], vectors).then_inc(ld_v, 16)
            sp.dma_start(w_sb[:, 0:a], weights[:, 0:a]).then_inc(ld_wa, 16)
            sp.dma_start(r_sb[:, :], rows.to_broadcast([P, RTOTAL])).then_inc(ld_r, 16)
            sp.dma_start(w_sb[:, a:], weights[:, a:]).then_inc(ld_wb, 16)
            sp.wait_ge(pool_step, 2)
            sp.dma_start(wq_sb[:, :, 0:AD], wq_t).then_inc(ld_qk, 16)
            sp.dma_start(wk_sb[:, :, 0:AD], wk_t).then_inc(ld_qk, 16)
            for n in range(2):
                sp.dma_start(w1_sb[:, n, :], w1_t[n]).then_inc(ld_w1[n], 16)
            sp.wait_ge(g_ready, 4 * NH + G_CREDIT)
            sp.dma_start(w2_sb, w2_t).then_inc(ld_w2, 16)
            with sp.Fori(0, E // 2 - 1) as i:
                for n in range(2):
                    sp.wait_ge(w1_parted, 2 * i + n + 1)
                    sp.dma_start(w1_sb[:, n, :], w1_t[bass.ds(2 * i + 2 + n, 1)].rearrange("e d f -> (e d) f")).then_inc(
                        ld_w1[n], 16)
            for h in range(2):
                sp.wait_ge(y_out_ready, h + 1)
                sp.dma_start(out[2 * h:2 * h + 2].rearrange("b c l -> c b l"),
                             half(y_out, h).rearrange("c (b l) -> c b l", b=2)).then_inc(stored, 16)
            sp.wait_ge(stored, 32)

        @block.gpsimd
        def _(pool):
            nc.gpsimd.memset(wq_sb[:, :, :], 0.0).then_inc(pool_step, 1)
            nc.gpsimd.memset(wk_sb[:, :, :], 0.0).then_inc(pool_step, 1)
            nc.gpsimd.memset(one_c[:, :], 1.0)
            nc.gpsimd.memset(ident[:, :], 0.0).then_inc(pool_step, 1)
            nc.gpsimd.memset(group_mean[:, :], GROUPS / C).then_inc(pool_step, 1)
            pool.wait_ge(pool_step, 4)
            gm = group_mean[:, :].rearrange("c (g i) -> c g i", g=GROUPS)
            per = C // GROUPS
            nc.gpsimd.affine_select(out=gm, in_=gm, compare_op=ALU.is_ge, fill=0.0, base=0,
                                    pattern=[[-per, GROUPS], [0, per]], channel_multiplier=1).then_inc(pool_step, 1)
            pool.wait_ge(pool_step, 5)
            nc.gpsimd.affine_select(out=gm, in_=gm, compare_op=ALU.is_ge, fill=0.0, base=per - 1,
                                    pattern=[[per, GROUPS], [0, per]], channel_multiplier=-1).then_inc(consts, 1)
            nc.gpsimd.affine_select(out=ident[:, :], in_=ident[:, :], compare_op=ALU.not_equal, fill=1.0,
                                    base=0, pattern=[[-1, P]], channel_multiplier=1).then_inc(consts, 1)
            nc.gpsimd.iota(row_i[:, :], pattern=[[0, 1]], base=0, channel_multiplier=1).then_inc(consts, 1)
            nc.gpsimd.iota(expert_i[:, :], pattern=[[1, E]], base=0, channel_multiplier=0).then_inc(consts, 1)
            nc.gpsimd.iota(own_i[:, :, :], pattern=[[1, E], [-1, E]], base=0, channel_multiplier=0).then_inc(consts, 1)
            nc.gpsimd.memset(terms[:, :, :, :, :], 0.0).then_inc(consts, 1)
            nc.gpsimd.memset(val[:, :, :, :, :], 0.0).then_inc(consts, 1)
            s3 = sel[:, :, :, :].rearrange("k h p j -> k (h p) j")
            nc.gpsimd.iota(s3, pattern=[[0, 4 * NP], [-2, P]], base=0, channel_multiplier=0,
                           allow_small_or_imprecise_dtypes=True).then_inc(sel_ready, 1)
            for k, (op, fill) in enumerate([(ALU.is_equal, 0.0), (ALU.not_equal, 1.0), (ALU.not_equal, 1.0)]):
                pool.wait_ge(sel_ready, k + 1)
                nc.gpsimd.affine_select(out=sel[:, :, :, :], in_=sel[:, :, :, :], compare_op=op, fill=fill, base=-NP * k,
                                        pattern=[[-32, 4], [-1, NP], [0, P]], channel_multiplier=1).then_inc(sel_ready, 1)
            nc.gpsimd.memset(v_tok[:, :, :, :], 1.0).then_inc(pool_step, 1)
            def stage(b, slot):
                nc.gpsimd.tensor_tensor(qb[:, slot, :, :], qp[:, :, bass.ds(b * HW, HW)],
                                        one_c[:, 0:1].unsqueeze(2).to_broadcast([P, 2, HW]), ALU.mult)
                nc.gpsimd.tensor_tensor(kb[:, slot, :, :], kp[:, :, bass.ds(b * HW, HW)],
                                        one_c[:, 0:1].unsqueeze(2).to_broadcast([P, 2, HW]), ALU.mult).then_inc(qb_ready, 1)

            pool.wait_ge(q_ready, 4)
            pool.wait_ge(k_ready, 4)
            stage(0, 0)
            stage(1, 1)
            with pool.Fori(1, B // 2) as i:
                for n in range(2):
                    pool.wait_ge(sc_mm, 2 * AH * i + AH * n - AH)
                    stage(2 * i + n, n)
            nc.gpsimd.memset(chosen_b[:, :, :], 0.0).then_inc(pool_step, 1)
            for h in range(2):
                pool.wait_ge(lns["lnf"]["out"], h + 1)
                nc.gpsimd.tensor_copy(half(z2_h, h).bitcast(F32R), half(z2, h)).then_inc(z2_parted, 1)
            for h in range(2):
                pool.wait_ge(z2_parted, h + 1)
                nc.gpsimd.tensor_tensor(half(z2_l, h), half(z2, h), half(z2_h, h), ALU.subtract).then_inc(z2_parted, 1)
            with pool.Fori(0, E // 2) as i:
                for n in range(2):
                    pool.wait_ge(ld_w1[n], 16 * i + 16)
                    pool.wait_ge(h_mm, 2 * FT * i + FT * n + FT)
                    nc.gpsimd.tensor_tensor(w1_h[:, n, :], w1_sb[:, n, :],
                                            one_c[:, 0:1].to_broadcast([P, F]), ALU.mult).then_inc(w1h_ready, 1)
                    pool.wait_ge(w1h_ready, 2 * i + n + 1)
                    nc.gpsimd.tensor_tensor(w1_l[:, n, :], w1_sb[:, n, :], w1_h[:, n, :].bitcast(F32),
                                            ALU.subtract).then_inc(w1_parted, 1)
        CONSTS = 7

        @block.scalar
        def _(act):
            def ln_std_of(s):
                for h in range(2):
                    act.wait_ge(s["var"], h + 1)
                    nc.scalar.activation(ln_std[:, 4 * h:4 * h + 4], ln_mv[:, 4 * h:4 * h + 4, 1], ACT.Sqrt,
                                         bias=eps_c[:, 0:1]).then_inc(s["std"], 1)

            def ln_out(s, bank, dst, gain=1.0, bias=0.0):
                for h in range(2):
                    act.wait_ge(s["turned"], 4 * (h + 1))
                    nc.scalar.activation(half(dst, h), ps[:, bank + h, :], ACT.Identity,
                                         scale=gain, bias=bias).then_inc(s["out"], 1)

            act.wait_ge(dve_consts, 1)
            act.wait_ge(gn_varied, 1)
            nc.scalar.activation(gn_std[:, :], gn_var[:, :], ACT.Sqrt, bias=eps_c[:, 0:1]).then_inc(gn_stded, 1)
            ln_std_of(lns["ln1"])
            act.wait_ge(ld_v, 16)
            ln_out(lns["ln1"], 2, q_c, V("ln1_g"), V("ln1_b"))

            act.wait_ge(proj_ready, TILES)
            nc.scalar.activation(hat_x[:, :, :], proj[:, :, 0:HP], ACT.Abs).then_inc(x_abs, 1)
            act.wait_ge(x_abs, 1)
            nc.scalar.activation(hat_x[:, :, :], hat_x[:, :, :], ACT.Relu, scale=-1.0, bias=1.0).then_inc(hat_x_ready, 1)
            act.wait_ge(val_ready, B * NK)
            nc.scalar.activation(val_p[0], val[:, :, :, :, :], ACT.Copy).then_inc(val_p0, 1)
            for g in range(2):
                act.wait_ge(terms_mm, TILES * (g + 1))
                nc.scalar.activation(terms_t[:, g, :], ps[:, 3 + g, :].bitcast(BF16), ACT.Copy).then_inc(terms_t_ready, 1)
            act.wait_ge(rest_ready, 1)
            for k in range(NK):
                nc.scalar.activation(hat_y[:, k, :, :], y_rest[:, :, :], ACT.Abs,
                                     bias=shift_c[:, k:k + 1]).then_inc(y_abs, 1)
            for k in range(NK):
                act.wait_ge(y_abs, k + 1)
                nc.scalar.activation(hat_y[:, k, :, :], hat_y[:, k, :, :], ACT.Relu,
                                     scale=-1.0, bias=1.0).then_inc(hat_y_ready, 1)
            act.wait_ge(val_r1, 1)
            nc.scalar.activation(val_p[1], val_r, ACT.Copy).then_inc(val_p1, 1)
            act.wait_ge(logit_sub, 1)
            nc.scalar.activation(aw[:, :, :], aw[:, :, :], ACT.Exp).then_inc(logit_exp, 1)

            def one_hots(i, u):
                act.wait_ge(g_ready, 4 * i + 2 * u + 1)
                for c in range(NP // 2):
                    act.wait_ge(dist_mm, 8 * i + 4 * u + c + 1)
                    nc.scalar.activation(hot[:, u, 2 * c:2 * c + 2, :, :],
                                         ps[:, 2 * (c % 2):2 * (c % 2) + 2, :].rearrange("r p (b q) -> r p b q", b=B),
                                         ACT.Relu, scale=-1.0, bias=one_less_sq[:, 0:1]).then_inc(hot_ready, 1)

            with act.Fori(0, NH) as i:
                for u in range(2):
                    one_hots(i, u)

            for h in range(2):
                act.wait_ge(msda_mm, 4 * (h + 1))
                nc.scalar.activation(half(msda_c, h), ps[:, h, :], ACT.Copy).then_inc(msda_c_ready, 1)
            ln_std_of(lns["ln3"])
            ln_out(lns["ln3"], 4, hn, V("ln3_g"), V("ln3_b"))
            n = 0
            for j in range(GE):
                for h in range(2):
                    act.wait_ge(gate_mm, n + 1)
                    if n >= 2:
                        act.wait_ge(ff_ready, n - 1)
                    nc.scalar.activation(gelu_g[:, n % 2, :], ps[:, n % 2, :], ACT.Gelu,
                                         bias=V("geglu_b", GE + j)).then_inc(gelu_ready, 1)
                    n += 1
            for h in range(2):
                act.wait_ge(t1_mm, 4 * (h + 1))
                nc.scalar.activation(half(t1_c, h), ps[:, 6 + h, :], ACT.Copy).then_inc(t1_c_ready, 1)
            ln_std_of(lns["lna"])
            ln_out(lns["lna"], 6, z1)

            for n in range(4):
                act.wait_ge(q_mm, n + 1)
                if n == 0:
                    act.wait_ge(x1_mm, TILES)
                nc.scalar.activation(half(qp[:, n % 2, :], n // 2), ps[:, n, :], ACT.Copy,
                                     scale=AD ** -0.5).then_inc(q_ready, 1)
            with act.Fori(0, B) as b:
                for h in range(AH):
                    act.wait_ge(nmax_ready, AH * b + h + 1)
                    for qt in range(2):
                        nc.scalar.activation(prob[:, h % 2, qt, :], ps[:, h % 4, qt * HW:(qt + 1) * HW], ACT.Exp,
                                             bias=nmax[:, h % 4, qt:qt + 1]).then_inc(prob_ready, 1)
            for h in range(2):
                act.wait_ge(ot_mm, 4 * (h + 1))
                nc.scalar.activation(half(o_c, h), ps[:, 4 + h, :], ACT.Copy).then_inc(o_c_ready, 1)
            ln_std_of(lns["lnf"])
            ln_out(lns["lnf"], 2, z2)
            for h in range(2):
                act.wait_ge(x2_mm, 4 * (h + 1))
                nc.scalar.activation(half(x2_c, h), ps[:, 6 + h, :], ACT.Copy).then_inc(x2_c_ready, 1)

            act.wait_ge(gap_ready, 1)
            nc.scalar.activation(e2[:, :], gap[:, :], ACT.Exp).then_inc(e2_ready, 1)
            with act.Fori(0, E // 2) as i:
                for n in range(2):
                    for f in range(FT):
                        act.wait_ge(h_mm, 2 * FT * i + FT * n + f + 1 + H_CREDIT)
                        c = 2 + 2 * (f % 2)
                        nc.scalar.activation(silu_junk[:, :], ps[:, c:c + 2, :].rearrange("f a t -> f (a t)"), ACT.Silu,
                                             accum_out=h_sum[:, bass.ds(2 * i + n, 1), f:f + 1].rearrange(
                                                 "p e f -> p (e f)")).then_inc(h_used, 1)
                        act.wait_ge(h_used, 2 * FT * i + FT * n + f + 1 + FREE_CREDIT)

        @block.vector
        def _(dve):
            count = [0]

            def link(ins):
                count[0] += 1
                ins.then_inc(dve_step, 1)
                dve.wait_ge(dve_step, count[0])

            def ln_stats(s, src, h):
                for t in range(4 * h, 4 * h + 4):
                    ins = nc.vector.bn_stats(ln_st[:, t, :], src[:, t, :])
                link(ins)
                for t in range(4 * h, 4 * h + 4):
                    ins = nc.vector.bn_aggr(ln_mv[:, t, :], ln_st[:, t, :])
                ins.then_inc(s["var"], 1)

            def ln_apply(s, src):
                for h in range(2):
                    dve.wait_ge(s["std"], h + 1)
                    nc.vector.reciprocal(ln_rstd[:, 4 * h:4 * h + 4], ln_std[:, 4 * h:4 * h + 4]).then_inc(s["rstd"], 1)
                    dve.wait_ge(s["rstd"], h + 1)
                    dve.wait_ge(s["var"], h + 1)
                    for t in range(4 * h, 4 * h + 4):
                        nc.vector.tensor_scalar(nrm[:, t, :], src[:, t, :], ln_mv[:, t, 0:1], ln_rstd[:, t:t + 1],
                                                ALU.subtract, ALU.mult).then_inc(s["norm"], 1)

            nc.vector.memset(ones_mean[:, :], 1.0 / P)
            nc.vector.memset(zero_c[:, :], 0.0)
            for k in range(NK):
                nc.vector.memset(shift_c[:, k:k + 1], float(-k))
            nc.vector.memset(eps_c[:, :], EPS).then_inc(dve_consts, 1)
            for b in range(B):
                dve.wait_ge(ld_x[b], 16)
                ins = nc.vector.bn_stats(gn_st[:, b, :], x_sb[:, b * HW:(b + 1) * HW])
            link(ins)
            for b in range(B):
                ins = nc.vector.bn_aggr(gn_mv[:, b, :], gn_st[:, b, :])
            link(ins)
            link(nc.vector.tensor_tensor(gn_sq[:, :], gn_mv[:, :, 0], gn_mv[:, :, 0], ALU.mult))
            nc.vector.tensor_tensor(gn_mv[:, :, 1], gn_mv[:, :, 1], gn_sq[:, :], ALU.add).then_inc(gn_moments, 1)
            dve.wait_ge(gn_grouped, 1)
            link(nc.vector.tensor_copy(gn_g[:, :, :], ps[:, 0, 0:2 * B].rearrange("c (b m) -> c b m", b=B)))
            link(nc.vector.tensor_tensor(gn_sq[:, :], gn_g[:, :, 0], gn_g[:, :, 0], ALU.mult))
            nc.vector.tensor_tensor(gn_var[:, :], gn_g[:, :, 1], gn_sq[:, :], ALU.subtract).then_inc(gn_varied, 1)
            dve.wait_ge(gn_stded, 1)
            link(nc.vector.reciprocal(gn_std[:, :], gn_std[:, :]))
            dve.wait_ge(ld_v, 16)
            link(nc.vector.tensor_scalar(gn_scale[:, :], gn_std[:, :], V("gn_g"), None, ALU.mult))
            link(nc.vector.tensor_tensor(gn_sq[:, :], gn_g[:, :, 0], gn_scale[:, :], ALU.mult))
            link(nc.vector.tensor_scalar(gn_shift[:, :], gn_sq[:, :], -1.0, V("gn_b"), ALU.mult, ALU.add))
            for b in range(B):
                cols = slice(b * HW, (b + 1) * HW)
                nc.vector.tensor_scalar(xn[:, cols], x_sb[:, cols], gn_scale[:, b:b + 1], gn_shift[:, b:b + 1],
                                        ALU.mult, ALU.add).then_inc(xn_ready, 1)
            for n, name in enumerate(("vproj_b", "mop_b", "dense_b")):
                nc.vector.tensor_scalar(bias_c[:, n, :], ones_mean[:, :], float(P), V(name),
                                        ALU.mult, ALU.mult).then_inc(dve_consts, 1)
            dve.wait_ge(ld_r, 16)
            for h in range(2):
                dve.wait_ge(pin_mm, 4 * (h + 1))
                nc.vector.tensor_tensor(t0_k[:, 4 * h:4 * h + 4, :], psum4(h), rows4(R("pin_b")), ALU.add).then_inc(t0_ready, 1)
                dve.wait_ge(t0_ready, h + 1)
                ln_stats(lns["ln1"], t0_k, h)
            dve.wait_ge(consts, CONSTS)
            nc.vector.tensor_copy(ident_b[:, :], ident[:, :])
            nc.vector.tensor_copy(expert_f[:, :], expert_i[:, :])
            nc.vector.tensor_scalar(own_f[:, :, :], own_i[:, :, :], 0.0, None, ALU.is_equal)
            link(nc.vector.tensor_copy(row_f[:, :], row_i[:, :]))
            link(nc.vector.tensor_tensor(one_less_sq[:, :], row_f[:, :], row_f[:, :], ALU.mult))
            nc.vector.tensor_scalar(one_less_sq[:, :], one_less_sq[:, :], -1.0, 1.0, ALU.mult, ALU.add).then_inc(dve_consts, 1)
            ln_apply(lns["ln1"], t0_k)
            dve.wait_ge(fuse_mm, 1)
            nc.vector.tensor_copy(w_val[:, :], ps[:, 4, 0:128]).then_inc(fuse_ready, 1)
            nc.vector.tensor_copy(w_out[:, :], ps[:, 4, 128:256]).then_inc(fuse_ready, 1)
            nc.vector.tensor_tensor(b_val[:, :], ps[:, 4, 256:384], R("mvp_b"), ALU.add).then_inc(fuse_ready, 1)
            nc.vector.tensor_tensor(b_out[:, :], ps[:, 4, 384:512], R("dout_b"), ALU.add).then_inc(fuse_ready, 1)
            nc.vector.tensor_copy(w_dp[:, :, :], psum4(5)).then_inc(fuse_ready, 1)
            nc.vector.tensor_tensor(b_dp[:, :], ps[:, 6, 0:128], R("pout_b"), ALU.add).then_inc(fuse_ready, 1)

            for t in range(TILES):
                dve.wait_ge(proj_mm, 2 * (t // 2) + 2)
                nc.vector.tensor_tensor(proj[:, t, :], ps[:, 4 + t // 2, 256 * (t % 2):256 * (t % 2) + 3 * HP],
                                        r_sb[:, RAT["soff_b"][0]:RAT["attw_b"][1]], ALU.add).then_inc(proj_ready, 1)
            dve.wait_ge(proj_ready, TILES)
            link(nc.vector.tensor_scalar(y_half[:, :, :], proj[:, :, HP:2 * HP], 0.5, (HW - 3) / 4, ALU.mult, ALU.add))
            link(nc.vector.tensor_scalar(y_half[:, :, :], y_half[:, :, :], 0.0, float(HW // 2 - 1), ALU.max, ALU.min))
            link(nc.vector.tensor_scalar(pair[:, :, :], y_half[:, :, :], ROUND, -ROUND, ALU.add, ALU.add))

            def by_head(t):
                return t[:, :, :].rearrange("q t (h p) -> q t h p", p=NP)

            link(nc.vector.tensor_tensor(pair_sq[:, :, :], pair[:, :, :], pair[:, :, :], ALU.mult))
            nc.vector.tensor_copy(terms[:, :, :, 0, :], by_head(pair))
            link(nc.vector.tensor_copy(terms[:, :, :, 1, :], by_head(pair_sq)))
            nc.vector.tensor_tensor(terms[:, :, :, 2, :], by_head(pair_sq), terms[:, :, :, 1, :],
                                    ALU.subtract).then_inc(terms_ready, 1)
            for n in range(B * NK):
                b, k = n // NK, n % NK
                rows_k = P if k < 2 else P - 1
                dve.wait_ge(val_mm, 4 * (n // 4) + 4)
                nc.vector.tensor_tensor(val[0:rows_k, b, :, k, :],
                                        ps[0:rows_k, n // 4, 128 * (n % 4):128 * (n % 4) + 128].rearrange(
                                            "p (h d) -> p h d", h=NH),
                                        b_val[0:rows_k, :].rearrange("p (h d) -> p h d", h=NH),
                                        ALU.add).then_inc(val_ready, 1)
            link(nc.vector.tensor_scalar(y_pos[:, :, :], proj[:, :, HP:2 * HP], 1.0, (HW - 1) / 2, ALU.mult, ALU.add))
            nc.vector.scalar_tensor_tensor(out=y_rest[:, :, :], in0=pair[:, :, :], scalar=-2.0, in1=y_pos[:, :, :],
                                           op0=ALU.mult, op1=ALU.add).then_inc(rest_ready, 1)
            dve.wait_ge(val_p0, 1)
            nc.vector.tensor_tensor(val_r, val[:, :, :, :, :], val_p[0], ALU.subtract).then_inc(val_r1, 1)
            logits = proj[:, :, 2 * HP:].rearrange("q t (h p) -> q t h p", p=NP)
            l3 = lmax[:, :].rearrange("q (t h) -> q t h", h=NH)
            a4 = aw[:, :, :].rearrange("q (t h) p -> q t h p", h=NH)
            link(nc.vector.tensor_reduce(l3, logits, AX_X, ALU.max))
            nc.vector.tensor_tensor(a4, logits, l3.unsqueeze(3).to_broadcast([P, TILES, NH, NP]),
                                    ALU.subtract).then_inc(logit_sub, 1)
            dve.wait_ge(val_p1, 1)
            nc.vector.tensor_tensor(val_p[2], val_r, val_p[1], ALU.subtract).then_inc(val_p1, 1)
            nc.vector.memset(gap[:, 0:1], 0.0).then_inc(hot_ready, HOT_CREDIT)
            nc.vector.memset(gap[:, 1:2], 0.0).then_inc(g_ready, G_CREDIT)
            nc.vector.memset(gap[:, 2:3], 0.0).then_inc(g_free, FREE_CREDIT)
            nc.vector.memset(gap[:, 3:4], 0.0).then_inc(prod_free, FREE_CREDIT)
            dve.wait_ge(logit_exp, 1)
            link(nc.vector.tensor_reduce(lsum[:, :], aw[:, :, :], AX_X, ALU.add))
            link(nc.vector.reciprocal(lsum[:, :], lsum[:, :]))
            link(nc.vector.tensor_tensor(aw[:, :, :], aw[:, :, :],
                                         lsum[:, :].unsqueeze(2).to_broadcast([P, TILES * NH, NP]), ALU.mult))
            dve.wait_ge(hat_x_ready, 1)
            flat = aw[:, :, :].rearrange("q (t h) p -> q t (h p)", h=NH)
            link(nc.vector.tensor_tensor(hat_x[:, :, :], hat_x[:, :, :], flat, ALU.mult))
            for k in range(NK):
                dve.wait_ge(hat_y_ready, k + 1)
                nc.vector.tensor_tensor(wk3[:, :, :, k], hat_x[:, :, :], hat_y[:, k, :, :], ALU.mult).then_inc(wk3_ready, 1)
            dve.wait_ge(wk3_ready, NK)

            with dve.Fori(0, NH) as i:
                for u in range(2):
                    for c in range(2):
                        dve.wait_ge(g_ready, 4 * i + 2 * u + c + 1 + G_CREDIT)
                        dve.wait_ge(prod_free, 4 * i + 2 * u + c + 1)
                        g = ps[:, 4 + 2 * c:6 + 2 * c, 0:NP * NK * DH].rearrange("q b (n d) -> q b n d", d=DH)
                        w = wk3[:, 4 * c + u:4 * c + u + 3:2, bass.ds(i * NP, NP), :].rearrange("q b p k -> q b (p k)")
                        nc.vector.tensor_tensor(prod[:, c, :, :, :], g,
                                                w.unsqueeze(3).to_broadcast([P, 2, NP * NK, DH]),
                                                ALU.mult).then_inc(g_free, 1)
                    for c in range(2):
                        dve.wait_ge(g_free, 4 * i + 2 * u + c + 1 + FREE_CREDIT)
                        nc.vector.tensor_reduce(msda[:, 4 * c + u:4 * c + u + 3:2, bass.ds(i, 1), :].rearrange(
                                                    "q b h d -> q b (h d)"),
                                                prod[:, c, :, :, :].rearrange("q b n d -> q b d n"),
                                                AX_X, ALU.add).then_inc(prod_free, 1)

            for h in range(2):
                nc.vector.tensor_tensor(t0_k[:, 4 * h:4 * h + 4, :], t0_k[:, 4 * h:4 * h + 4, :], rows4(b_out[:, :]),
                                        ALU.add).then_inc(t0_ready, 1)
            for h in range(2):
                dve.wait_ge(out_mm, 4 * (h + 1))
                dve.wait_ge(t0_ready, 3 + h)
                nc.vector.tensor_tensor(t1_k[:, 4 * h:4 * h + 4, :], psum4(2 + h), t0_k[:, 4 * h:4 * h + 4, :],
                                        ALU.add).then_inc(t1_ready, 1)
                dve.wait_ge(t1_ready, h + 1)
                ln_stats(lns["ln3"], t1_k, h)
            ln_apply(lns["ln3"], t1_k)
            n = 0
            for j in range(GE):
                for h in range(2):
                    dve.wait_ge(gelu_ready, n + 1)
                    dve.wait_ge(lin_mm, n + 1)
                    nc.vector.scalar_tensor_tensor(out=half(ff[:, j, :], h), in0=ps[:, 2 + n % 2, :],
                                                   scalar=V("geglu_b", j), in1=gelu_g[:, n % 2, :],
                                                   op0=ALU.add, op1=ALU.mult).then_inc(ff_ready, 1)
                    n += 1
            for h in range(2):
                dve.wait_ge(x1_mm, 4 * (h + 1))
                nc.vector.tensor_tensor(x1_k[:, 4 * h:4 * h + 4, :], psum4(4 + h), rows4(b_dp[:, :]), ALU.add).then_inc(x1_ready, 1)
                dve.wait_ge(x1_ready, h + 1)
                ln_stats(lns["lna"], x1_k, h)
            ln_apply(lns["lna"], x1_k)

            for n in range(4):
                dve.wait_ge(k_mm, n + 1)
                nc.vector.tensor_copy(half(kp[:, n % 2, :], n // 2), ps[:, 4 + n, :]).then_inc(k_ready, 1)
            dve.wait_ge(pool_step, 6)
            for h in range(2):
                dve.wait_ge(v_mm, 4 * (h + 1))
                nc.vector.tensor_copy(v_tok[:, 4 * h:4 * h + 4, :, 0:AD],
                                      ps[:, h, :].rearrange("t (k h d) -> t k h d", k=4, h=AH)).then_inc(v_ready, 1)
            nc.vector.memset(gap[:, 4:5], 0.0).then_inc(o_ready, 1)

            def row_max(b, h):
                dve.wait_ge(sc_mm, AH * b + h + 1)
                nc.vector.tensor_reduce(nmax[:, h % 4, :], ps[:, h % 4, :].rearrange("q (t k) -> q t k", t=2),
                                        AX_X, ALU.max, negate=True).then_inc(nmax_ready, 1)

            def attend(b, last):
                for h in range(AH):
                    dve.wait_ge(pt_mm, AH * b + h + 1)
                    nc.vector.tensor_copy(prob_t[:, h % 2, :, :],
                                          ps[:, 4 + h % 2, :].rearrange("k (a q) -> k a q", a=4)).then_inc(pt_ready, 1)
                    if h + 2 < AH:
                        row_max(b, h + 2)
                    elif not last:
                        row_max(b + 1, h + 2 - AH)
                dve.wait_ge(pv_mm, AH * b + AH)
                o_ps = ps[:, 6, 0:2 * AH * AD1].rearrange("q (t h d) -> q t h d", t=2, h=AH)
                nc.vector.reciprocal(inv_sum[:, :, :], o_ps[:, :, :, AD]).then_inc(inv_ready, 1)
                dve.wait_ge(inv_ready, b + 1)
                nc.vector.tensor_tensor(o_tok[:, bass.ds(2 * b, 2), :, :], o_ps[:, :, :, 0:AD],
                                        inv_sum[:, :, :].unsqueeze(3).to_broadcast([P, 2, AH, AD]),
                                        ALU.mult).then_inc(o_ready, 1)

            row_max(0, 0)
            row_max(0, 1)
            with dve.Fori(0, B - 1) as b:
                attend(b, False)
            attend(B - 1, True)
            for h in range(2):
                dve.wait_ge(ap_mm, 4 * (h + 1))
                nc.vector.tensor_tensor(x2_k[:, 4 * h:4 * h + 4, :], psum4(h), x1_k[:, 4 * h:4 * h + 4, :],
                                        ALU.add).then_inc(x2_ready, 1)
                dve.wait_ge(x2_ready, h + 1)
                ln_stats(lns["lnf"], x2_k, h)
            ln_apply(lns["lnf"], x2_k)

            dve.wait_ge(lg_mm, 1)
            link(nc.vector.tensor_copy(lg[:, :, :], ps[:, 4, 0:TILES * E].rearrange("t (n e) -> t n e", e=E)))
            for t in range(TILES):
                ins = nc.vector.max(top[:, t, :], lg[:, t, :])
            link(ins)
            nc.vector.tensor_tensor(gap[:, :], top[:, :, 1], top[:, :, 0], ALU.subtract).then_inc(gap_ready, 1)
            for t in range(TILES):
                ins = nc.vector.max_index(top_i[:, t, :], top[:, t, :], lg[:, t, :])
            link(ins)
            link(nc.vector.tensor_copy(top_f[:, :, :], top_i[:, :, 0:TOPK]))
            ex = expert_f[:, :].unsqueeze(1).to_broadcast([P, TILES, E])
            nc.vector.tensor_tensor(oh1[:, :, :], ex, top_f[:, :, 0:1].to_broadcast([P, TILES, E]), ALU.is_equal)
            link(nc.vector.tensor_tensor(oh2[:, :, :], ex, top_f[:, :, 1:2].to_broadcast([P, TILES, E]), ALU.is_equal))
            link(nc.vector.tensor_tensor(chosen[:, :, :], oh1[:, :, :], oh2[:, :, :], ALU.add))
            dve.wait_ge(pool_step, 7)
            nc.vector.tensor_copy(chosen_b[:, :, 0:E], chosen[:, :, :]).then_inc(route_ready, 1)
            dve.wait_ge(rt_mm, TILES)
            nc.vector.tensor_copy(chosen_t[:, :], ps[:, 5, :].bitcast(BF16)).then_inc(route_t_ready, 1)
            nc.vector.memset(lmax[:, 0:1], 0.0).then_inc(h_mm, H_CREDIT)
            nc.vector.memset(lmax[:, 1:2], 0.0).then_inc(h_used, FREE_CREDIT)
            nc.vector.memset(lmax[:, 2:3], 0.0).then_inc(y_mm, Y_CREDIT)

            def masked(e, n):
                dve.wait_ge(h_mm, FT * e + FT)
                for h in range(2):
                    dve.wait_ge(mb_mm, 2 * e + h + 1)
                    nc.vector.tensor_tensor(half(xm_h[:, n, :], h), half(z2_h, h), ps[:, h, :], ALU.mult)
                    nc.vector.tensor_tensor(half(xm_l[:, n, :], h), half(z2_l, h), ps[:, h, :],
                                            ALU.mult).then_inc(xm_ready, 1)

            def means(e, n):
                dve.wait_ge(h_used, FT * e + FT + FREE_CREDIT)
                dve.wait_ge(y_mm, e + 1)
                nc.vector.tensor_scalar(h_mean[:, n, :], h_sum[:, bass.ds(e, 1), :].rearrange("p e f -> p (e f)"),
                                        inv_cnt[:, bass.ds(e, 1)], None, ALU.mult).then_inc(hmean_ready, 1)
                dve.wait_ge(hmean_ready, e + 1)
                nc.vector.tensor_tensor(h_col[:, n, :, :], h_mean[:, n, :].unsqueeze(2).to_broadcast([P, FT, E]),
                                        own_f[:, bass.ds(e, 1), :].to_broadcast([P, FT, E]),
                                        ALU.mult).then_inc(hcol_ready, 1)

            def expert_pair(i, first, last):
                masked(2 * i + 1, 1)
                if not first:
                    means(2 * i - 1, 1)
                if not last:
                    masked(2 * i + 2, 0)
                means(2 * i, 0)

            dve.wait_ge(z2_parted, 4)
            masked(0, 0)
            dve.wait_ge(e2_ready, 1)
            link(nc.vector.tensor_scalar(e2p[:, :], e2[:, :], 1.0, None, ALU.add))
            link(nc.vector.reciprocal(rw1[:, :], e2p[:, :]))
            link(nc.vector.tensor_tensor(rw2[:, :], e2[:, :], rw1[:, :], ALU.mult))
            nc.vector.tensor_tensor(oh1[:, :, :], oh1[:, :, :], rw1[:, :].unsqueeze(2).to_broadcast([P, TILES, E]), ALU.mult)
            link(nc.vector.tensor_tensor(oh2[:, :, :], oh2[:, :, :],
                                         rw2[:, :].unsqueeze(2).to_broadcast([P, TILES, E]), ALU.mult))
            nc.vector.tensor_tensor(route[:, :, :], oh1[:, :, :], oh2[:, :, :], ALU.add).then_inc(route_ready, 1)
            dve.wait_ge(cnt_mm, 1)
            link(nc.vector.tensor_scalar(cnt[:, :], ps[:, 7, 0:E], float(P), 1.0, ALU.mult, ALU.max))
            link(nc.vector.reciprocal(inv_cnt[:, :], cnt[:, :]))
            expert_pair(0, True, False)
            with dve.Fori(1, E // 2 - 1) as i:
                expert_pair(i, False, False)
            expert_pair(E // 2 - 1, False, True)
            means(E - 1, 1)
            dve.wait_ge(rt_mm, 2 * TILES)
            nc.vector.tensor_copy(route_t[:, :], ps[0:E, 0:2, :].rearrange("e a t -> e (a t)")).then_inc(route_t_ready, 1)
            dve.wait_ge(y_mm, E + Y_CREDIT)
            nc.vector.tensor_copy(y_mean[:, :], ps[0:E, 6, 0:P]).then_inc(y_ready, 1)
            for h in range(2):
                dve.wait_ge(moe_mm, h + 1)
                dve.wait_ge(x2_c_ready, h + 1)
                nc.vector.tensor_tensor(half(y_out, h), half(x2_c, h), ps[:, 2 + h, :], ALU.add).then_inc(y_out_ready, 1)

        @block.tensor
        def _(pe):
            def turn(s, bank):
                for t in range(TILES):
                    pe.wait_ge(s["norm"], t + 1)
                    nc.tensor.transpose(ps[:, bank + t // 4, P * (t % 4):P * (t % 4) + P], nrm[:, t, :],
                                        ident[:, :]).then_inc(s["turned"], 1)

            def tile_of(bank, t):
                return ps[:, bank + t // 4, P * (t % 4):P * (t % 4) + P]

            pe.wait_ge(dve_consts, 1)
            pe.wait_ge(consts, CONSTS)
            pe.wait_ge(gn_moments, 1)
            nc.tensor.matmul(ps[:, 0, 0:2 * B], group_mean[:, :],
                             gn_mv[:, :, :].rearrange("c b m -> c (b m)")).then_inc(gn_grouped, 1)
            pe.wait_ge(ld_wa, 16)
            pe.wait_ge(ld_wb, 16)
            nc.tensor.matmul(ps[:, 4, 0:128], W("vprojT"), W("mvp"))
            nc.tensor.matmul(ps[:, 4, 128:256], W("mopT"), W("dout"))
            for j in range(GE):
                nc.tensor.matmul(ps[:, 5, j * P:(j + 1) * P], W("denseT")[:, j * P:(j + 1) * P], W("pout"))
            for t in range(TILES):
                pe.wait_ge(xn_ready, t // 2 + 1)
                nc.tensor.matmul(tile_of(0, t), xn[:, t * P:(t + 1) * P], W("pin")).then_inc(pin_mm, 1)
            pe.wait_ge(dve_consts, 4)
            nc.tensor.matmul(ps[:, 4, 256:384], bias_c[:, 0, :], W("mvp"))
            nc.tensor.matmul(ps[:, 4, 384:512], bias_c[:, 1, :], W("dout"))
            nc.tensor.matmul(ps[:, 6, 0:128], bias_c[:, 2, :], W("pout")).then_inc(fuse_mm, 1)
            turn(lns["ln1"], 2)
            pe.wait_ge(fuse_ready, 6)
            soff_attw = w_sb[:, WAT["soff"][0]:WAT["attw"][1]]
            for t in range(TILES):
                pe.wait_ge(lns["ln1"]["out"], t // (TILES // 2) + 1)
                nc.tensor.matmul(ps[:, 4 + t // 2, 256 * (t % 2):256 * (t % 2) + 3 * HP], q_c[:, t * P:(t + 1) * P],
                                 soff_attw).then_inc(proj_mm, 1)
            for n in range(B * NK):
                b, k = n // NK, n % NK
                rows_k = P if k < 2 else P - 1
                first = b * HW + k
                nc.tensor.matmul(ps[0:rows_k, n // 4, 128 * (n % 4):128 * (n % 4) + 128],
                                 q_c[:, first:first + 2 * rows_k - 1:2], w_val[:, :]).then_inc(val_mm, 1)
            pe.wait_ge(terms_ready, 1)
            pe.wait_ge(dve_consts, 5)
            for g in range(2):
                for n in range(TILES):
                    t = 2 * (n % B) + n // B
                    nc.tensor.transpose(ps[:, 3 + g, 64 * n:64 * n + 64].bitcast(BF16),
                                        terms[:, t, 4 * g:4 * g + 4, :, :].rearrange("q h c p -> q (h c p)"),
                                        ident_b[:, :]).then_inc(terms_mm, 1)
            pe.wait_ge(terms_t_ready, 2)
            pe.wait_ge(sel_ready, 4)
            pe.wait_ge(val_ready, B * NK)
            pe.wait_ge(g_ready, G_CREDIT)

            def distances(i, u, c):
                pe.wait_ge(hot_ready, 8 * i + 4 * u + c + 1)
                for p in (2 * c, 2 * c + 1):
                    ins = nc.tensor.matmul(ps[:, 2 * (c % 2) + p % 2, :],
                                           sel[:, bass.ds(i % 4, 1), p, :].rearrange("k h j -> k (h j)"),
                                           terms_t[:, bass.ds(i // 4, 1), u * HALF:(u + 1) * HALF].rearrange(
                                               "k g q -> k (g q)"))
                ins.then_inc(dist_mm, 1)

            def gather(i, u, b):
                if b == 0:
                    pe.wait_ge(hot_ready, 8 * i + 4 * u + 4 + HOT_CREDIT)
                if b % 2 == 0:
                    pe.wait_ge(g_free, 4 * i + 2 * u + b // 2 + 1)
                for p in range(NP):
                    for s in range(PARTS):
                        rhs = val_p[s][:, b, bass.ds(i, 1), :, :].rearrange("r h k d -> r (h k d)")
                        ins = nc.tensor.matmul(ps[:, 4 + b, p * NK * DH:(p + 1) * NK * DH], hot[:, u, p, b, :], rhs,
                                               start=(s == 0), stop=(s == PARTS - 1))
                if b % 2:
                    ins.then_inc(g_ready, 1)

            def sample(i, last):
                for c in range(NP // 2):
                    distances(i, 1, c)
                    if c == 0 and isinstance(i, int) and i == 0:
                        pe.wait_ge(val_p1, 2)
                    gather(i, 0, c)
                for c in range(NP // 2):
                    if not last:
                        distances(i + 1, 0, c)
                    gather(i, 1, c)

            pe.wait_ge(val_p1, 2)
            for c in range(NP // 2):
                distances(0, 0, c)
            with pe.Fori(0, NH - 1) as i:
                sample(i, False)
            sample(NH - 1, True)

            for t in range(TILES):
                nc.tensor.matmul(tile_of(2, t), q_c[:, t * P:(t + 1) * P], W("dout"), start=(t % 4 == 0), stop=False,
                                 skip_group_check=True)
            for t in range(TILES):
                if t == 0:
                    pe.wait_ge(prod_free, 4 * NH + FREE_CREDIT)
                nc.tensor.transpose(tile_of(0, t), msda[:, t, :, :].rearrange("q h d -> q (h d)"),
                                    ident[:, :]).then_inc(msda_mm, 1)
            for t in range(TILES):
                pe.wait_ge(msda_c_ready, t // 4 + 1)
                nc.tensor.matmul(tile_of(2, t), msda_c[:, t * P:(t + 1) * P], w_out[:, :], start=False, stop=True,
                                 skip_group_check=True).then_inc(out_mm, 1)
            for t in range(TILES):
                pe.wait_ge(t1_ready, t // 4 + 1)
                nc.tensor.transpose(tile_of(6, t), t1_k[:, t, :], ident[:, :]).then_inc(t1_mm, 1)
            turn(lns["ln3"], 4)
            n = 0
            geglu = W("geglu")
            for j in range(GE):
                for h in range(2):
                    pe.wait_ge(lns["ln3"]["out"], h + 1)
                    if n >= 2:
                        pe.wait_ge(gelu_ready, n - 1)
                    nc.tensor.matmul(ps[:, n % 2, :], geglu[:, (GE + j) * P:(GE + j + 1) * P], half(hn, h)).then_inc(gate_mm, 1)
                    if n >= 2:
                        pe.wait_ge(ff_ready, n - 1)
                    nc.tensor.matmul(ps[:, 2 + n % 2, :], geglu[:, j * P:(j + 1) * P], half(hn, h)).then_inc(lin_mm, 1)
                    n += 1
            for t in range(TILES):
                cols = slice(t * P, (t + 1) * P)
                nc.tensor.matmul(tile_of(4, t), x_sb[:, cols], ident[:, :], start=True, stop=False)
                pe.wait_ge(t1_c_ready, t // 4 + 1)
                nc.tensor.matmul(tile_of(4, t), t1_c[:, cols], W("pout"), start=False, stop=False)
                for j in range(GE):
                    pe.wait_ge(ff_ready, 2 * j + t // 4 + 1)
                    ins = nc.tensor.matmul(tile_of(4, t), ff[:, j, cols], w_dp[:, j, :], start=False, stop=(j == GE - 1))
                ins.then_inc(x1_mm, 1)
            turn(lns["lna"], 6)

            pe.wait_ge(ld_qk, 32)
            for w, bank, done in ((wq_sb, 0, q_mm), (wk_sb, 4, k_mm)):
                for n in range(4):
                    g, h = n % 2, n // 2
                    pe.wait_ge(lns["lna"]["out"], 2 if bank else h + 1)
                    nc.tensor.matmul(ps[:, bank + n, :], w[:, 4 * g:4 * g + 4, :].rearrange("c h d -> c (h d)"),
                                     half(z1, h)).then_inc(done, 1)
            for t in range(TILES):
                pe.wait_ge(q_ready, t // 4 + 1)
                nc.tensor.matmul(tile_of(0, t), z1[:, t * P:(t + 1) * P], W("wv")).then_inc(v_mm, 1)

            def scores(b, slot, h):
                r = 32 * (h % 4)
                if h == 0:
                    pe.wait_ge(qb_ready, b + 1)
                for t in range(2):
                    ins = nc.tensor.matmul(ps[:, h % 4, t * HW:(t + 1) * HW], qb[r:r + AD, slot, h // 4, t * P:(t + 1) * P],
                                           kb[r:r + AD, slot, h // 4, :])
                ins.then_inc(sc_mm, 1)

            def turn_probs(b, h):
                pe.wait_ge(prob_ready, 2 * AH * b + 2 * (h + 1))
                for a in range(4):
                    kt, qt = a // 2, a % 2
                    ins = nc.tensor.transpose(ps[:, 4 + h % 2, a * P:(a + 1) * P],
                                              prob[:, h % 2, qt, kt * P:(kt + 1) * P], ident[:, :])
                ins.then_inc(pt_mm, 1)

            def weigh_values(b, h):
                pe.wait_ge(pt_ready, AH * b + h + 1)
                if h == 0:
                    pe.wait_ge(o_ready, b + 1)
                for qt in range(2):
                    at_o = (qt * AH + h) * AD1
                    for kt in range(2):
                        ins = nc.tensor.matmul(ps[:, 6, at_o:at_o + AD1], prob_t[:, h % 2, 2 * kt + qt, :],
                                               v_tok[:, bass.ds(2 * b + kt, 1), h, :].rearrange("k t d -> k (t d)"),
                                               start=(kt == 0), stop=(kt == 1))
                ins.then_inc(pv_mm, 1)

            def attend(b, slot, last):
                for h in range(AH):
                    turn_probs(b, h)
                    if h + 2 < AH:
                        scores(b, slot, h + 2)
                    elif not last:
                        scores(b + 1, 1 - slot, h + 2 - AH)
                    if h > 0:
                        weigh_values(b, h - 1)
                weigh_values(b, AH - 1)

            pe.wait_ge(v_ready, 2)
            pe.wait_ge(q_ready, 4)
            pe.wait_ge(k_ready, 4)
            scores(0, 0, 0)
            scores(0, 0, 1)
            with pe.Fori(0, B // 2 - 1) as i:
                attend(2 * i, 0, False)
                attend(2 * i + 1, 1, False)
            attend(B - 2, 0, False)
            attend(B - 1, 1, True)
            pe.wait_ge(o_ready, B + 1)
            for t in range(TILES):
                nc.tensor.transpose(tile_of(4, t), o_tok[:, t, :, :].rearrange("q h d -> q (h d)"),
                                    ident[:, :]).then_inc(ot_mm, 1)
            for t in range(TILES):
                pe.wait_ge(o_c_ready, t // 4 + 1)
                nc.tensor.matmul(tile_of(0, t), o_c[:, t * P:(t + 1) * P], W("wproj")).then_inc(ap_mm, 1)
            turn(lns["lnf"], 2)
            for t in range(TILES):
                pe.wait_ge(x2_ready, t // 4 + 1)
                nc.tensor.transpose(tile_of(6, t), x2_k[:, t, :], ident[:, :]).then_inc(x2_mm, 1)

            for t in range(TILES):
                pe.wait_ge(lns["lnf"]["out"], t // 4 + 1)
                ins = nc.tensor.matmul(ps[:, 4, t * E:(t + 1) * E], z2[:, t * P:(t + 1) * P], W("gate"))
            ins.then_inc(lg_mm, 1)
            pe.wait_ge(route_ready, 1)
            pe.wait_ge(pool_step, 7)
            for t in range(TILES):
                nc.tensor.transpose(ps[:, 5, 64 * t:64 * t + 64].bitcast(BF16), chosen_b[:, t, :],
                                    ident_b[:, :]).then_inc(rt_mm, 1)
            pe.wait_ge(x2_c_ready, 2)
            for t in range(TILES):
                ins = nc.tensor.matmul(ps[:, 7, 0:E], ones_mean[:, :], chosen[:, t, :], start=(t == 0), stop=(t == TILES - 1))
            ins.then_inc(cnt_mm, 1)
            nc.tensor.matmul(ps[0:E, 6, 0:P], zero_c[:, :], ident[:, :], start=True, stop=False, skip_group_check=True)

            def choose(e):
                for h in range(2):
                    if not (isinstance(e, int) and e == 0):
                        pe.wait_ge(xm_ready, 2 * e + h - 1)
                    nc.tensor.matmul(ps[:, h, :], ident_b[:, bass.ds(e, 1)].to_broadcast([P, P]),
                                     half(chosen_t, h)).then_inc(mb_mm, 1)

            def hidden(e, n):
                pe.wait_ge(w1_parted, e + 1)
                pe.wait_ge(xm_ready, 2 * e + 2)
                for f in range(FT):
                    pe.wait_ge(h_used, FT * e + f + 1)
                    c = 2 + 2 * (f % 2)
                    cols = slice(f * P, (f + 1) * P)
                    for h in range(2):
                        o = ps[:, c + h, :]
                        nc.tensor.matmul(o, w1_h[:, n, cols], half(xm_h[:, n, :], h), start=True, stop=False)
                        nc.tensor.matmul(o, w1_h[:, n, cols], half(xm_l[:, n, :], h), start=False, stop=False)
                        ins = nc.tensor.matmul(o, w1_l[:, n, cols], half(xm_h[:, n, :], h), start=False, stop=True)
                    ins.then_inc(h_mm, 1)

            def mean_out(e, n):
                pe.wait_ge(hcol_ready, e + 1)
                for f in range(FT):
                    ins = nc.tensor.matmul(ps[0:E, 6, 0:P], h_col[:, n, f, :],
                                           w2_sb[:, bass.ds(FT * e + f, 1), :].rearrange("f n d -> f (n d)"),
                                           start=False, stop=False, skip_group_check=True)
                ins.then_inc(y_mm, 1)

            def expert_pair(i, first, last):
                choose(2 * i + 1)
                hidden(2 * i, 0)
                if not first:
                    mean_out(2 * i - 2, 0)
                if not last:
                    choose(2 * i + 2)
                hidden(2 * i + 1, 1)
                if not first:
                    mean_out(2 * i - 1, 1)

            pe.wait_ge(route_t_ready, 1)
            choose(0)
            pe.wait_ge(ld_w2, 16)
            expert_pair(0, True, False)
            with pe.Fori(1, E // 2 - 1) as i:
                expert_pair(i, False, False)
            expert_pair(E // 2 - 1, False, True)
            pe.wait_ge(route_ready, 2)
            pe.wait_ge(xm_ready, 2 * E)
            for t in range(TILES):
                nc.tensor.transpose(ps[0:E, t // 4, P * (t % 4):P * (t % 4) + P], route[:, t, :],
                                    ident[:, :]).then_inc(rt_mm, 1)
            mean_out(E - 2, 0)
            mean_out(E - 1, 1)
            pe.wait_ge(y_ready, 1)
            pe.wait_ge(route_t_ready, 2)
            pe.wait_ge(h_used, E * FT + FREE_CREDIT)
            for h in range(2):
                nc.tensor.matmul(ps[:, 2 + h, :], y_mean[:, :], half(route_t, h)).then_inc(moe_mm, 1)


def kernel(**inputs):
    import numpy as np
    import concourse.bacc as bacc
    from concourse.bass_utils import run_bass_kernel_spmd as run

    a = {n: np.asarray(v) for n, v in inputs.items()}

    def L(n):
        return a["L0_conv_" + n]

    soff_w = L("soff_w").reshape(C, HP, 2).transpose(0, 2, 1).reshape(C, 2 * HP)
    soff_b = L("soff_b").reshape(HP, 2).transpose(1, 0).reshape(2 * HP)
    parts = dict(pin=L("pin_w"), vprojT=L("vproj_w").T, mvp=L("mvp_w"), soff=soff_w, attw=L("attw_w"),
                 mopT=L("mop_w").T, dout=L("dout_w"), geglu=L("geglu_w"),
                 denseT=L("dense_w").T,
                 pout=L("pout_w"), wv=a["L1_attn_wv"].T, wproj=a["L1_attn_wproj"].T, gate=a["L1_ffn_gate_weight"].T)
    vecs = {n: L(n).reshape(-1, P).T for n in VAT}
    rows = dict(mvp_b=L("mvp_b"), soff_b=soff_b, attw_b=L("attw_b"), pin_b=L("pin_b"), dout_b=L("dout_b"),
                pout_b=L("pout_b"))
    arrays = dict(
        x=a["x"].reshape(B, C, HW),
        weights=np.concatenate([parts[n] for n in WAT], axis=1),
        vectors=np.concatenate([vecs[n] for n in VAT], axis=1),
        rows=np.concatenate([rows[n] for n in RAT]).reshape(1, RTOTAL),
        wq_t=a["L1_attn_wq"].T.reshape(C, AH, AD),
        wk_t=a["L1_attn_wk"].T.reshape(C, AH, AD),
        w1_t=a["L1_ffn_w1"].transpose(0, 2, 1),
        w2_t=a["L1_ffn_w2"].transpose(2, 0, 1).reshape(FT, P, E, C).transpose(1, 2, 0, 3).reshape(P, E * FT, C),
    )
    nc = bacc.Bacc("TRN2", target_bir_lowering=False, num_devices=1)
    feeds, args = {}, []
    for name, v in arrays.items():
        v = np.ascontiguousarray(v)
        feeds[f"in_{name}"] = v
        args.append(nc.dram_tensor(f"in_{name}", v.shape, F32, kind="ExternalInput").ap())
    out = nc.dram_tensor("out", (B, C, HW), F32, kind="ExternalOutput").ap()
    build(nc, *args, out)
    r = run(nc, [feeds], core_ids=[0])
    return r.results[0]["out"].reshape(B, C, 16, 16)
```

```python
from contextlib import ExitStack

import concourse.bass as bass
from concourse import mybir

ALU = mybir.AluOpType
ACT = mybir.ActivationFunctionType
AX_X = mybir.AxisListType.X
F32 = mybir.dt.float32
BF16 = mybir.dt.bfloat16
F32R = mybir.dt.float32r
U32 = mybir.dt.uint32
I32 = mybir.dt.int32

P = 128
B, C, HW = 4, 128, 256
T = B * HW
TILES = T // P
HALF = T // 2
NH, DH, NP = 8, 16, 8
HP = NH * NP
GROUPS = 8
NK = 3
PARTS = 3
AH, AD = 8, 16
HROWS = 64
SPLIT = 3 * AD
PAIRS = AH // 2
E, TOPK, F = 16, 2, 512
FT = F // P
GE = 4
EPS = 1e-5
ROUND = 1.5 * 2 ** 23

def columns(**widths):
    at, where = 0, {}
    for name, n in widths.items():
        where[name] = (at, at + n)
        at += n
    return where, at


WAT, WTOTAL = columns(pin=C, vprojT=C, mvp=C, mopT=C, dout=C, soff=2 * HP, attw=HP,
                      geglu=2 * GE * P, denseT=GE * P, pout=C, wq=AH * HROWS, wk=AH * HROWS, wv=C, wproj=C, gate=E)
VAT, VTOTAL = columns(gn_g=1, gn_b=1, ln1_g=1, ln1_b=1, vproj_b=1, mop_b=1,
                      ln3_g=1, ln3_b=1, geglu_b=2 * GE, dense_b=1, pout_b=1)
RAT, RTOTAL = columns(mvp_b=C, soff_b=2 * HP, attw_b=HP, pin_b=C, dout_b=C)


def build(nc, x, weights, vectors, rows, w1_t, w2_t, out):
    with ExitStack() as ctx:
        def sb(name, shape, dt=F32):
            return ctx.enter_context(nc.sbuf_tensor(name, shape, dt))

        def sem(name):
            return ctx.enter_context(nc.semaphore(name))

        ps = ctx.enter_context(nc.psum_tensor("ps", [P, 8, 512], F32))

        ones_mean = sb("ones_mean", [P, P])
        ident = sb("ident", [P, P])
        ident_b = sb("ident_b", [P, P], BF16)
        ident_less = sb("ident_less", [P, P])
        group_mean = sb("group_mean", [P, P])
        row_i = sb("row_i", [P, 1], I32)
        row_f = sb("row_f", [P, 1])
        one_less_sq = sb("one_less_sq", [P, 1])
        expert_i = sb("expert_i", [P, E], I32)
        expert_f = sb("expert_f", [P, E])
        own_i = sb("own_i", [P, E, E], I32)
        own_f = sb("own_f", [P, E, E])
        eps_c = sb("eps_c", [P, 1])
        one_c = sb("one_c", [P, 1])
        zero_c = sb("zero_c", [P, E])
        ones_b = sb("ones_b", [P, P], BF16)
        shift_c = sb("shift_c", [P, NK])
        row_groups = sb("row_groups", [P, 2, 4])
        row_group = sb("row_group", [P, 4])
        raw_by = sb("raw_by", [P, 2])
        high_by = sb("high_by", [P, 2])
        pick = sb("pick", [AH, AH], F32R)
        sel = sb("sel", [P, 4, NP, P], BF16)
        w_sb = sb("w_sb", [P, WTOTAL])
        v_sb = sb("v_sb", [P, VTOTAL])
        r_sb = sb("r_sb", [P, RTOTAL])
        w1_sb = sb("w1_sb", [P, 2, F])
        w1_h = sb("w1_h", [P, 2, F], F32R)
        w1_l = sb("w1_l", [P, 2, F], F32R)
        arena = sb("arena", [P, E * FT * P])
        w2_sb = arena[:, :].rearrange("f (n d) -> f n d", d=P)

        def W(name):
            a, b = WAT[name]
            return w_sb[:, a:b]

        def V(name, j=0):
            a, _ = VAT[name]
            return v_sb[:, a + j:a + j + 1]

        def R(name):
            a, b = RAT[name]
            return r_sb[:, a:b]

        def tok(name):
            return sb(name, [P, TILES, C])

        x_sb = sb("x_sb", [P, T])
        xn = sb("xn", [P, T])
        t0_k = tok("t0_k")
        nrm = tok("nrm")
        q_c = sb("q_c", [P, T])
        msda_c = xn
        t1_k = tok("t1_k")
        t1_c = sb("t1_c", [P, T])
        hn = q_c
        gelu_g = sb("gelu_g", [P, 2, HALF])
        ff = sb("ff", [P, GE, T])
        x1_k = tok("x1_k")
        z1 = q_c
        o_c = xn
        x2_k = t1_k
        z2 = q_c
        x2_c = t1_c
        y_out = xn
        gn_st = sb("gn_st", [P, B, 6])
        gn_mv = sb("gn_mv", [P, B, 2])
        gn_sq = sb("gn_sq", [P, B])
        gn_g = sb("gn_g", [P, B, 2])
        gn_var = sb("gn_var", [P, B])
        gn_std = sb("gn_std", [P, B])
        gn_scale = sb("gn_scale", [P, B])
        gn_shift = sb("gn_shift", [P, B])
        ln_st = sb("ln_st", [P, TILES, 6])
        ln_mv = sb("ln_mv", [P, TILES, 2])
        ln_std = sb("ln_std", [P, TILES])
        ln_rstd = sb("ln_rstd", [P, TILES])
        fused = sb("fused", [P, 4, P])
        w_val = fused[:, 0, :]
        w_out = fused[:, 1, :]
        w_dp = sb("w_dp", [P, GE, P])
        bias_c = sb("bias_c", [P, 2, P])
        b_val = fused[:, 2, :]
        b_out = fused[:, 3, :]
        b_dp = sb("b_dp", [P, 1])
        proj = sb("proj", [P, TILES, 3 * HP])
        hat_x = sb("hat_x", [P, TILES, HP])
        lmax = sb("lmax", [P, TILES * NH])
        lsum = sb("lsum", [P, TILES * NH])
        aw = sb("aw", [P, TILES * NH, NP])
        y_pos = sb("y_pos", [P, TILES, HP])
        y_half = sb("y_half", [P, TILES, HP])
        pair = sb("pair", [P, TILES, HP])
        pair_sq = sb("pair_sq", [P, TILES, HP])
        terms = sb("terms", [P, TILES, NH, 4, NP], BF16)
        y_rest = sb("y_rest", [P, TILES, HP])
        hat_y = sb("hat_y", [P, NK, TILES, HP])
        wk3 = sb("wk3", [P, TILES, HP, NK])
        terms_t = sb("terms_t", [P, 2, T], BF16)
        n_val = B * NH * NK * DH
        hot_words = 2 * NP * HALF // 2
        hot = arena[:, 0:hot_words].bitcast(BF16).rearrange("r (u p b q) -> r u p b q", u=2, p=NP, b=B)
        val_p = [arena[:, hot_words + i * n_val // 2:hot_words + (i + 1) * n_val // 2].bitcast(BF16).rearrange(
            "r (b h k d) -> r b h k d", b=B, h=NH, k=NK) for i in range(PARTS)]
        at_r = hot_words + PARTS * n_val // 2
        val_r = arena[:, at_r:at_r + n_val].rearrange("r (b h k d) -> r b h k d", b=B, h=NH, k=NK)
        prod = hat_y[:, :, :, :].rearrange("q k t r -> q (k t r)").rearrange(
            "q (s b n d) -> q s b n d", s=2, b=2, d=DH)
        msda = sb("msda", [P, TILES, NH, DH])
        xm_h = sb("xm_h", [P, 2, T], F32R)
        xm_l = sb("xm_l", [P, 2, T], F32R)
        qkp = [t[:, :, :].rearrange("c s (n t) -> c s n t", n=PAIRS) for t in (xm_h, xm_l)]
        hn_h, hn_l = xm_h[:, 0, :], xm_l[:, 0, :]
        geglu_h, geglu_l = xm_h[:, 1, :], xm_l[:, 1, :]
        wqk_h = sb("wqk_h", [P, 2 * AH * HROWS], F32R)
        wqk_l = sb("wqk_l", [P, 2 * AH * HROWS], F32R)
        z1_h, z1_l = (w[:, :, :].rearrange("c a t -> c (a t)") for w in (w1_h, w1_l))
        v_k = sel[:, :, :, :].rearrange("k h p j -> k (h p j)").bitcast(F32)[:, 0:T].rearrange(
            "k (t c) -> k t c", c=C)
        v_wide = ff[:, :, :].rearrange("k a t -> k (a t)").rearrange("k (s t h c) -> k s t h c", s=2, t=2, h=AH)
        nmax = sb("nmax", [P, 2, AH])
        nmax_t = sb("nmax_t", [AH, 2, HW], F32R)
        prob_t = wk3[:, :, :, :].rearrange("q t n k -> q (t n k)")[:, 0:2 * 2 * HW].rearrange(
            "k (s c) -> k s c", s=2)
        o_raw = proj[:, :, :].rearrange("q t n -> q (t n)")[:, 0:2 * HW]
        inv_sum = sb("inv_sum", [P, 2, AH])
        o_tok = msda
        lg = sb("lg", [P, TILES, E])
        top = sb("top", [P, TILES, 8])
        top_i = sb("top_i", [P, TILES, 8], U32)
        top_f = sb("top_f", [P, TILES, TOPK])
        oh1 = sb("oh1", [P, TILES, E])
        oh2 = sb("oh2", [P, TILES, E])
        chosen = sb("chosen", [P, TILES, E])
        chosen_b = pair_sq[:, :, :].rearrange("t a b -> t (a b)").bitcast(BF16).rearrange(
            "t (a e) -> t a e", a=TILES)
        chosen_t = pair[:, :, :].rearrange("e a b -> e (a b)").bitcast(BF16)
        gap = sb("gap", [P, TILES])
        e2 = sb("e2", [P, TILES])
        e2p = sb("e2p", [P, TILES])
        rw1 = sb("rw1", [P, TILES])
        rw2 = sb("rw2", [P, TILES])
        route = sb("route", [P, TILES, E])
        route_t = terms[0:E, :, :, :, :].rearrange("e t h c p -> e (t h c p)").bitcast(F32)
        cnt = sb("cnt", [P, E])
        inv_cnt = sb("inv_cnt", [P, E])
        z2_h = nrm[:, :, :].rearrange("c t k -> c (t k)")
        z2_l = t0_k[:, :, :].rearrange("c t k -> c (t k)")
        silu_junk = y_half[:, :, :].bitcast(BF16).rearrange("f a b -> f (a b)")
        h_sum = sb("h_sum", [P, E, FT])
        h_mean = sb("h_mean", [P, 2, FT])
        y_rows = sb("y_rows", [P, 2, P])
        own_col = sb("own_col", [P, 2, E])
        y_mean = sb("y_mean", [E, P])
        table_junk = sb("table_junk", [P, 1])

        def sems(names):
            return [sem(n) for n in names.split()]

        ld_x = [sem(f"ld_x{b}") for b in range(B)]
        ld_v, ld_r, ld_wa, ld_wb, ld_wc, ld_w2 = sems("ld_v ld_r ld_wa ld_wb ld_wc ld_w2")
        ld_w1 = sems("ld_w1_even ld_w1_odd")
        stored, pool_step, dve_step, consts, sel_ready, dve_consts = sems(
            "stored pool_step dve_step consts sel_ready dve_consts")
        bias_ready, x_biased = sems("bias_ready x_biased")
        gn_moments, gn_grouped, gn_varied, gn_stded, xn_ready = sems(
            "gn_moments gn_grouped gn_varied gn_stded xn_ready")
        pin_mm, t0_ready, fuse_mm, fuse_ready = sems("pin_mm t0_ready fuse_mm fuse_ready")
        lns = {n: {k: sem(f"{n}_{k}") for k in ("var", "std", "rstd", "norm", "turned", "out")}
               for n in ("ln1", "ln3", "lna", "lnf")}
        proj_mm, proj_ready, val_mm, val_p0, val_r1, val_p1 = sems(
            "proj_mm proj_ready val_mm val_p0 val_r1 val_p1")
        y_halved, pair_ready, sq_ready, logit_sub, logit_exp = sems("y_halved pair_ready sq_ready logit_sub logit_exp")
        x_sided, hat_x_ready, rest_ready, y_sided, y_abs, hat_y_ready, hat_y2_ready = sems(
            "x_sided hat_x_ready rest_ready y_sided y_abs hat_y_ready hat_y2_ready")
        terms_ready, terms_mm, terms_t_ready, wk3_ready = sems("terms_ready terms_mm terms_t_ready wk3_ready")
        dist_mm, hot_ready, g_ready, g_free, prod_free = sems("dist_mm hot_ready g_ready g_free prod_free")
        msda_mm, msda_c_ready, out_mm, t1_ready, t1_mm, t1_c_ready = sems(
            "msda_mm msda_c_ready out_mm t1_ready t1_mm t1_c_ready")
        geglu_parted, hn_h_ready, hn_l_ready, wqk_parted, z1_h_ready, z1_l_ready = sems(
            "geglu_parted hn_h_ready hn_l_ready wqk_parted z1_h_ready z1_l_ready")
        gate_mm, lin_mm, gelu_ready, ff_ready, x1_mm, x1_ready = sems(
            "gate_mm lin_mm gelu_ready ff_ready x1_mm x1_ready")
        qk_mm, high_ready, qk_ready, v_mm, v_ready, v_zeroed, v_placed = sems(
            "qk_mm high_ready qk_ready v_mm v_ready v_zeroed v_placed")
        sc_mm, nmax_ready, nt_mm, nmax_t_ready, st_mm, prob_ready, pv_mm = sems(
            "sc_mm nmax_ready nt_mm nmax_t_ready st_mm prob_ready pv_mm")
        o_raw_ready, turn_mm = sems("o_raw_ready turn_mm")
        inv_ready, o_ready, ot_mm, o_c_ready, ap_mm, x2_ready, x2_mm, x2_c_ready = sems(
            "inv_ready o_ready ot_mm o_c_ready ap_mm x2_ready x2_mm x2_c_ready")
        lg_mm, gap_ready, e2_ready, route_ready, rt_mm, route_t_ready, cnt_mm, cnt_read = sems(
            "lg_mm gap_ready e2_ready route_ready rt_mm route_t_ready cnt_mm cnt_read")
        z2_parted, w1h_ready, w1_parted, mb_mm, xm_ready, h_mm, h_used = sems(
            "z2_parted w1h_ready w1_parted mb_mm xm_ready h_mm h_used")
        hmean_ready, y_summed, y_rows_ready, y_mm, y_ready, moe_mm, y_out_ready = sems(
            "hmean_ready y_summed y_rows_ready y_mm y_ready moe_mm y_out_ready")

        def half(t, h):
            return t[:, h * HALF:(h + 1) * HALF]

        def four(t, h):
            return t[:, 4 * h:4 * h + 4, :].rearrange("k t c -> k (t c)")

        def rows4(t):
            return t.unsqueeze(1).to_broadcast([P, 4, P])

        def proj_ps(h):
            return ps[:, 4 * h:4 * h + 2, :].rearrange("k a (t n) -> k (a t) n", t=2)[:, :, 0:3 * HP]

        def val_ps(b):
            return ps[:, (6, 7, 2, 3)[b], 0:NK * C]

        HOT_CREDIT, G_CREDIT, FREE_CREDIT, H_CREDIT, Y_CREDIT, O_CREDIT = 2, 3, 2, 2 * FT, 2, 1
        U_CREDIT = 5
        CONSTS = 7
        VALUE_ORDER = (2, 3, 0, 1)
        SLOTS = (6, 2, 4, 6, 2, 4, 2, 4)
        BACK = (5, 3, 3, 3, 3, 3, 2, 2)

        block = ctx.enter_context(nc.Block())

        @block.sync
        def _(sp):
            a, b1 = WAT["mvp"][1], WAT["attw"][1]
            for b in range(B):
                sp.dma_start(x_sb[:, b * HW:(b + 1) * HW], x[b]).then_inc(ld_x[b], 16)
            sp.dma_start(v_sb[:, :], vectors).then_inc(ld_v, 16)
            sp.dma_start(w_sb[:, 0:a], weights[:, 0:a]).then_inc(ld_wa, 16)
            sp.dma_start(r_sb[:, :], rows.to_broadcast([P, RTOTAL])).then_inc(ld_r, 16)
            sp.dma_start(w_sb[:, a:b1], weights[:, a:b1]).then_inc(ld_wb, 16)
            sp.dma_start(w_sb[:, b1:], weights[:, b1:]).then_inc(ld_wc, 16)
            for n in range(2):
                sp.dma_start(w1_sb[:, n, :], w1_t[n]).then_inc(ld_w1[n], 16)
            sp.wait_ge(g_ready, 4 * NH + G_CREDIT)
            sp.dma_start(w2_sb, w2_t).then_inc(ld_w2, 16)
            with sp.Fori(0, E // 2 - 1) as i:
                for n in range(2):
                    sp.wait_ge(w1_parted, 2 * i + n + 1)
                    sp.dma_start(w1_sb[:, n, :], w1_t[bass.ds(2 * i + 2 + n, 1)].rearrange("e d f -> (e d) f")).then_inc(
                        ld_w1[n], 16)
            for h in range(2):
                sp.wait_ge(y_out_ready, h + 1)
                sp.dma_start(out[2 * h:2 * h + 2].rearrange("b c l -> c b l"),
                             half(y_out, h).rearrange("c (b l) -> c b l", b=2)).then_inc(stored, 16)
            sp.wait_ge(stored, 32)

        @block.gpsimd
        def _(pool):
            nc.gpsimd.memset(one_c[:, :], 1.0)
            nc.gpsimd.memset(ident[:, :], 0.0).then_inc(pool_step, 1)
            nc.gpsimd.memset(group_mean[:, :], GROUPS / C).then_inc(pool_step, 1)
            pool.wait_ge(pool_step, 2)
            gm = group_mean[:, :].rearrange("c (g i) -> c g i", g=GROUPS)
            per = C // GROUPS
            nc.gpsimd.affine_select(out=gm, in_=gm, compare_op=ALU.is_ge, fill=0.0, base=0,
                                    pattern=[[-per, GROUPS], [0, per]], channel_multiplier=1).then_inc(pool_step, 1)
            pool.wait_ge(pool_step, 3)
            nc.gpsimd.affine_select(out=gm, in_=gm, compare_op=ALU.is_ge, fill=0.0, base=per - 1,
                                    pattern=[[per, GROUPS], [0, per]], channel_multiplier=-1).then_inc(consts, 1)
            nc.gpsimd.affine_select(out=ident[:, :], in_=ident[:, :], compare_op=ALU.not_equal, fill=1.0,
                                    base=0, pattern=[[-1, P]], channel_multiplier=1).then_inc(consts, 1)
            nc.gpsimd.iota(row_i[:, :], pattern=[[0, 1]], base=0, channel_multiplier=1).then_inc(consts, 1)
            nc.gpsimd.iota(expert_i[:, :], pattern=[[1, E]], base=0, channel_multiplier=0).then_inc(consts, 1)
            nc.gpsimd.iota(own_i[:, :, :], pattern=[[1, E], [-1, E]], base=0, channel_multiplier=0).then_inc(consts, 1)
            nc.gpsimd.memset(terms[:, :, :, :, :], 0.0).then_inc(consts, 1)
            nc.gpsimd.affine_select(out=ident_less[:, :], in_=one_c[:, 0:1].to_broadcast([P, P]), compare_op=ALU.is_equal,
                                    fill=0.0, base=0, pattern=[[-1, P]], channel_multiplier=1).then_inc(pool_step, 1)
            pool.wait_ge(pool_step, 4)
            nc.gpsimd.memset(ident_less[:, P - 1:P], 0.0).then_inc(consts, 1)
            s3 = sel[:, :, :, :].rearrange("k h p j -> k (h p) j")
            nc.gpsimd.iota(s3, pattern=[[0, 4 * NP], [-2, P]], base=0, channel_multiplier=0,
                           allow_small_or_imprecise_dtypes=True).then_inc(sel_ready, 1)
            for k, (op, fill) in enumerate([(ALU.is_equal, 0.0), (ALU.not_equal, 1.0), (ALU.not_equal, 1.0)]):
                pool.wait_ge(sel_ready, k + 1)
                nc.gpsimd.affine_select(out=sel[:, :, :, :], in_=sel[:, :, :, :], compare_op=op, fill=fill, base=-NP * k,
                                        pattern=[[-32, 4], [-1, NP], [0, P]], channel_multiplier=1).then_inc(sel_ready, 1)
            def hat(out, at, k, spare, sided, ready):
                nc.gpsimd.tensor_scalar(out, at, 1.0 - k, 1.0, ALU.add, ALU.min)
                nc.gpsimd.tensor_scalar(spare, at, float(-k), 0.0, ALU.add, ALU.max).then_inc(sided, 1)
                pool.wait_ge(sided, 1)
                nc.gpsimd.tensor_tensor(out, out, spare, ALU.subtract).then_inc(ready, 1)

            spare = t1_k[:, :, 0:HP]
            pool.wait_ge(proj_ready, 4)
            hat(hat_x[:, :, :], proj[:, :, 0:HP], 0, spare, x_sided, hat_x_ready)
            pool.wait_ge(hat_x_ready, 1)
            pool.wait_ge(rest_ready, 1)
            hat(hat_y[:, 2, :, :], y_rest[:, :, :], 2, spare, y_sided, hat_y2_ready)
            pool.wait_ge(ld_wc, 16)
            wqk = w_sb[:, WAT["wq"][0]:WAT["wk"][1]]
            for w, high, low, parted in ((W("geglu"), geglu_h, geglu_l, geglu_parted),
                                         (wqk, wqk_h[:, :], wqk_l[:, :], wqk_parted)):
                nc.gpsimd.tensor_tensor(high, w, one_c[:, 0:1].to_broadcast([P, 2 * GE * P]), ALU.mult).then_inc(parted, 1)
                pool.wait_ge(parted, 1)
                nc.gpsimd.tensor_tensor(low, w, high.bitcast(F32), ALU.subtract).then_inc(parted, 1)
            pool.wait_ge(x1_mm, TILES)
            for slot in range(2):
                nc.gpsimd.memset(v_wide[:, slot, :, :, :], 0.0).then_inc(v_zeroed, 1)
                pool.wait_ge(v_zeroed, slot + 1)
                for i in range(4):
                    nc.gpsimd.memset(v_wide[:, slot, :, i::4, 32 * i + AD:32 * i + AD + 1], 1.0)

            def place_values(b, slot):
                for i in range(4):
                    ins = nc.gpsimd.tensor_tensor(
                        v_wide[:, slot, :, i::4, 32 * i:32 * i + AD],
                        v_k[:, bass.ds(2 * b, 2), :].rearrange("k t (h d) -> k t h d", h=AH)[:, :, i::4, :],
                        one_c[:, 0:1].unsqueeze(2).unsqueeze(3).to_broadcast([P, 2, 2, AD]), ALU.mult)
                ins.then_inc(v_placed, 1)

            pool.wait_ge(v_ready, 2)
            place_values(0, 0)
            place_values(1, 1)
            with pool.Fori(1, B // 2) as i:
                for n in range(2):
                    pool.wait_ge(pv_mm, 2 * AH * i + AH * n - AH + FREE_CREDIT)
                    place_values(2 * i + n, n)
            nc.gpsimd.memset(chosen_b[:, :, :], 0.0).then_inc(pool_step, 1)
            for h in range(2):
                pool.wait_ge(lns["lnf"]["out"], h + 1)
                nc.gpsimd.tensor_copy(half(z2_h, h).bitcast(F32R), half(z2, h)).then_inc(z2_parted, 1)
            for h in range(2):
                pool.wait_ge(z2_parted, h + 1)
                nc.gpsimd.tensor_tensor(half(z2_l, h), half(z2, h), half(z2_h, h), ALU.subtract).then_inc(z2_parted, 1)
            with pool.Fori(0, E // 2) as i:
                for n in range(2):
                    pool.wait_ge(ld_w1[n], 16 * i + 16)
                    pool.wait_ge(h_mm, 2 * FT * i + FT * n + FT)
                    nc.gpsimd.tensor_tensor(w1_h[:, n, :], w1_sb[:, n, :],
                                            one_c[:, 0:1].to_broadcast([P, F]), ALU.mult).then_inc(w1h_ready, 1)
                    pool.wait_ge(w1h_ready, 2 * i + n + 1)
                    nc.gpsimd.tensor_tensor(w1_l[:, n, :], w1_sb[:, n, :], w1_h[:, n, :].bitcast(F32),
                                            ALU.subtract).then_inc(w1_parted, 1)

        @block.scalar
        def _(act):
            def ln_std_of(s, halves=(0, 1)):
                for h in halves:
                    act.wait_ge(s["var"], h + 1)
                    nc.scalar.activation(ln_std[:, 4 * h:4 * h + 4], ln_mv[:, 4 * h:4 * h + 4, 1], ACT.Sqrt,
                                         bias=eps_c[:, 0:1]).then_inc(s["std"], 1)

            def ln_out(s, bank, dst, gain=1.0, bias=0.0, halves=(0, 1)):
                for h in halves:
                    act.wait_ge(s["turned"], 4 * (h + 1))
                    nc.scalar.activation(half(dst, h), ps[:, bank + h, :], ACT.Identity,
                                         scale=gain, bias=bias).then_inc(s["out"], 1)

            act.wait_ge(dve_consts, 1)
            nc.scalar.activation(table_junk[:, :], eps_c[:, :], ACT.Sqrt)
            act.wait_ge(gn_varied, 1)
            nc.scalar.activation(gn_std[:, :], gn_var[:, :], ACT.Sqrt, bias=eps_c[:, 0:1]).then_inc(gn_stded, 1)
            for h in range(2):
                ln_std_of(lns["ln1"], (h,))
                nc.scalar.activation(four(t0_k, h), ps[:, h, :], ACT.Copy).then_inc(t0_ready, 1)
            act.wait_ge(fuse_mm, 1)
            nc.scalar.activation(fused[:, :, :].rearrange("c n k -> c (n k)"), ps[:, 4, :], ACT.Copy).then_inc(fuse_ready, 1)
            act.wait_ge(fuse_mm, 2)
            nc.scalar.activation(w_dp[:, :, :].rearrange("c n k -> c (n k)"), ps[:, 5, :], ACT.Copy).then_inc(fuse_ready, 1)
            nc.scalar.activation(b_dp[:, :], ps[:, 6, 0:1], ACT.Copy).then_inc(fuse_ready, 1)
            act.wait_ge(ld_v, 16)
            ln_out(lns["ln1"], 2, q_c, V("ln1_g"), V("ln1_b"))
            act.wait_ge(fuse_ready, 3)
            act.wait_ge(xn_ready, B)
            nc.scalar.activation(x_sb[:, :], x_sb[:, :], ACT.Identity, bias=b_dp[:, 0:1]).then_inc(x_biased, 1)
            for h in range(2):
                act.wait_ge(y_halved, h + 1)
                for j in range(2):
                    t = 4 * h + 2 * j
                    nc.scalar.activation(proj[:, t:t + 2, :], proj_ps(h)[:, 2 * j:2 * j + 2, :], ACT.Copy).then_inc(
                        proj_ready, 1)
            act.wait_ge(pair_ready, 1)
            nc.scalar.activation(pair_sq[:, :, :], pair[:, :, :], ACT.Square).then_inc(sq_ready, 1)

            def value_rows(s, b):
                return s[:, b, :, :, :].rearrange("r h k d -> r k h d")

            def first_part(n, b):
                act.wait_ge(val_mm, n + 1)
                nc.scalar.activation(value_rows(val_p[0], b), val_ps(b).rearrange("r (k h d) -> r k h d", k=NK, h=NH),
                                     ACT.Copy).then_inc(val_p0, 1)

            for n, b in enumerate(VALUE_ORDER[:3]):
                first_part(n, b)
            for g in range(2):
                act.wait_ge(terms_mm, TILES * (g + 1))
                nc.scalar.activation(terms_t[:, g, :], ps[:, g, :].bitcast(BF16), ACT.Copy).then_inc(terms_t_ready, 1)
            first_part(3, VALUE_ORDER[3])

            def one_hots(i, u, which=range(NP // 2)):
                act.wait_ge(g_ready, 4 * i + 2 * u + 1)
                for c in which:
                    act.wait_ge(dist_mm, 8 * i + 4 * u + c + 1)
                    nc.scalar.activation(hot[:, u, 2 * c:2 * c + 2, :, :],
                                         ps[:, 2 * (c % 2):2 * (c % 2) + 2, :].rearrange("r p (b q) -> r p b q", b=B),
                                         ACT.Relu, scale=-1.0, bias=one_less_sq[:, 0:1]).then_inc(hot_ready, 1)

            act.wait_ge(val_r1, B)
            nc.scalar.activation(val_p[1], val_r, ACT.Copy).then_inc(val_p1, 1)
            act.wait_ge(rest_ready, 1)
            for k in range(2):
                nc.scalar.activation(hat_y[:, k, :, :], y_rest[:, :, :], ACT.Abs,
                                     bias=shift_c[:, k:k + 1]).then_inc(y_abs, 1)
            one_hots(0, 0, range(0, 1))
            act.wait_ge(logit_sub, 1)
            nc.scalar.activation(aw[:, :, :], aw[:, :, :], ACT.Exp).then_inc(logit_exp, 1)
            one_hots(0, 0, range(1, 4))

            with act.Fori(0, NH - 1) as i:
                one_hots(i, 1)
                one_hots(i + 1, 0)
            one_hots(NH - 1, 1)

            def keep(src_bank, dst, normed, ready):
                for h in range(2):
                    act.wait_ge(normed, 4 * (h + 1))
                    nc.scalar.activation(four(dst, h), ps[:, src_bank + h, :], ACT.Copy).then_inc(ready, 1)

            for h in range(2):
                act.wait_ge(msda_mm, 4 * (h + 1))
                nc.scalar.activation(half(msda_c, h), ps[:, h, :], ACT.Copy).then_inc(msda_c_ready, 1)
            ln_std_of(lns["ln3"])
            for h in range(2):
                act.wait_ge(lns["ln3"]["turned"], 4 * (h + 1))
                nc.scalar.activation(half(hn_h, h), ps[:, 4 + h, :], ACT.Identity,
                                     scale=V("ln3_g"), bias=V("ln3_b")).then_inc(hn_h_ready, 1)
                ln_out(lns["ln3"], 4, hn, V("ln3_g"), V("ln3_b"), (h,))
            for n in range(2 * GE):
                h, j = n // GE, n % GE
                act.wait_ge(gate_mm, n + 1)
                if n >= 2:
                    act.wait_ge(ff_ready, n - 1)
                nc.scalar.activation(gelu_g[:, n % 2, :], ps[:, n % 2, :], ACT.Gelu,
                                     bias=V("geglu_b", GE + j)).then_inc(gelu_ready, 1)
                if n == 1:
                    keep(2, t1_k, lns["ln3"]["norm"], t1_ready)
                if n == 3:
                    for g in range(2):
                        act.wait_ge(t1_mm, 4 * (g + 1))
                        nc.scalar.activation(half(t1_c, g), ps[:, 4 + g, :], ACT.Copy).then_inc(t1_c_ready, 1)
            def high_parts(b, slot, n):
                act.wait_ge(qk_mm, 4 * b + n + 1)
                q_or_k, pairs = n % 2, slice(2 * (n // 2), 2 * (n // 2) + 2)
                nc.scalar.activation(qkp[q_or_k][:, slot, pairs, :],
                                     ps[:, 6 + n % 2, :].rearrange("c (n t) -> c n t", n=2), ACT.Identity,
                                     scale=high_by[:, q_or_k:q_or_k + 1]).then_inc(high_ready, 1)

            def exp_scores(b, h):
                act.wait_ge(st_mm, AH * b + h + 1)
                act.wait_ge(pv_mm, AH * b + h + 1)
                nc.scalar.activation(prob_t[:, h % 2, :], ps[:, 2 + h % 2, :], ACT.Exp).then_inc(prob_ready, 1)

            def outputs_out(h):
                act.wait_ge(ot_mm, 4 * (h + 1))
                nc.scalar.activation(half(o_c, h), ps[:, 6 + h, :], ACT.Copy).then_inc(o_c_ready, 1)

            def attend(b, slot, last):
                for h in range(AH):
                    exp_scores(b, h)
                    if last and h == 5:
                        outputs_out(0)
                    if h in (0, 1) and not last:
                        for n in (2 * h, 2 * h + 1):
                            high_parts(b + 1, 1 - slot, n)
                act.wait_ge(pv_mm, AH * b + AH + FREE_CREDIT)
                nc.scalar.activation(o_raw, ps[:, 4, :], ACT.Copy).then_inc(o_raw_ready, 1)

            def z1_out(h):
                act.wait_ge(lns["lna"]["turned"], 4 * (h + 1))
                nc.scalar.activation(half(z1_h, h), ps[:, 4 + h, :], ACT.Identity).then_inc(z1_h_ready, 1)
                ln_out(lns["lna"], 4, z1, halves=(h,))

            ln_std_of(lns["lna"], (0,))
            z1_out(0)
            act.wait_ge(dve_consts, 2)
            high_parts(0, 0, 0)
            high_parts(0, 0, 1)
            ln_std_of(lns["lna"], (1,))
            high_parts(0, 0, 2)
            high_parts(0, 0, 3)
            z1_out(1)
            for h in range(2):
                act.wait_ge(v_mm, 4 * (h + 1))
                nc.scalar.activation(v_k[:, 4 * h:4 * h + 4, :].rearrange("k t c -> k (t c)"), ps[:, 4 + h, :],
                                     ACT.Copy).then_inc(v_ready, 1)
            keep(2, x1_k, lns["lna"]["norm"], x1_ready)
            with act.Fori(0, B // 2 - 1) as i:
                attend(2 * i, 0, False)
                attend(2 * i + 1, 1, False)
            attend(B - 2, 0, False)
            attend(B - 1, 1, True)
            ln_std_of(lns["lnf"], (0,))
            outputs_out(1)
            ln_out(lns["lnf"], 2, z2, halves=(0,))
            ln_std_of(lns["lnf"], (1,))
            ln_out(lns["lnf"], 2, z2, halves=(1,))
            for h in range(2):
                act.wait_ge(x2_mm, 4 * (h + 1))
                nc.scalar.activation(half(x2_c, h), ps[:, 6 + h, :], ACT.Copy).then_inc(x2_c_ready, 1)

            act.wait_ge(gap_ready, 2)
            nc.scalar.activation(e2[:, :], gap[:, :], ACT.Exp).then_inc(e2_ready, 1)
            nc.scalar.activation(table_junk[:, :], eps_c[:, :], ACT.Silu)
            with act.Fori(0, E // 2) as i:
                for n in range(2):
                    for f in range(FT):
                        act.wait_ge(h_mm, 2 * FT * i + FT * n + f + 1 + H_CREDIT)
                        c = SLOTS[FT * n + f]
                        nc.scalar.activation(silu_junk[:, :], ps[:, c:c + 2, :].rearrange("f a t -> f (a t)"), ACT.Silu,
                                             accum_out=h_sum[:, bass.ds(2 * i + n, 1), f:f + 1].rearrange(
                                                 "p e f -> p (e f)")).then_inc(h_used, 1)
                        act.wait_ge(h_used, 2 * FT * i + FT * n + f + 1 + U_CREDIT)

        @block.vector
        def _(dve):
            count = [0]

            def link(ins):
                count[0] += 1
                ins.then_inc(dve_step, 1)
                dve.wait_ge(dve_step, count[0])

            def ln_stats(s, src, h):
                for t in range(4 * h, 4 * h + 4):
                    ins = nc.vector.bn_stats(ln_st[:, t, :], src[:, t, :])
                link(ins)
                for t in range(4 * h, 4 * h + 4):
                    ins = nc.vector.bn_aggr(ln_mv[:, t, :], ln_st[:, t, :])
                ins.then_inc(s["var"], 1)

            def summed(bank):
                return ps[:, bank:bank + 2, :].rearrange("k a (t c) -> k (a t) c", c=C)

            def norm(s, bank, done):
                for h in range(2):
                    dve.wait_ge(done, 4 * (h + 1))
                    ln_stats(s, summed(bank), h)
                ln_apply(s, summed(bank))

            def ln_apply(s, src, halves=(0, 1)):
                for h in halves:
                    dve.wait_ge(s["std"], h + 1)
                    nc.vector.reciprocal(ln_rstd[:, 4 * h:4 * h + 4], ln_std[:, 4 * h:4 * h + 4]).then_inc(s["rstd"], 1)
                    dve.wait_ge(s["rstd"], h + 1)
                    dve.wait_ge(s["var"], h + 1)
                    for t in range(4 * h, 4 * h + 4):
                        nc.vector.tensor_scalar(nrm[:, t, :], src[:, t, :], ln_mv[:, t, 0:1], ln_rstd[:, t:t + 1],
                                                ALU.subtract, ALU.mult).then_inc(s["norm"], 1)

            nc.vector.memset(ones_mean[:, :], 1.0 / P)
            nc.vector.memset(zero_c[:, :], 0.0)
            nc.vector.memset(ones_b[:, :], 1.0 / P)
            for k in range(NK):
                nc.vector.memset(shift_c[:, k:k + 1], float(-k))
            nc.vector.memset(eps_c[:, :], EPS).then_inc(dve_consts, 1)
            for b in range(B):
                dve.wait_ge(ld_x[b], 16)
                ins = nc.vector.bn_stats(gn_st[:, b, :], x_sb[:, b * HW:(b + 1) * HW])
            link(ins)
            for b in range(B):
                ins = nc.vector.bn_aggr(gn_mv[:, b, :], gn_st[:, b, :])
            link(ins)
            link(nc.vector.tensor_tensor(gn_sq[:, :], gn_mv[:, :, 0], gn_mv[:, :, 0], ALU.mult))
            nc.vector.tensor_tensor(gn_mv[:, :, 1], gn_mv[:, :, 1], gn_sq[:, :], ALU.add).then_inc(gn_moments, 1)
            dve.wait_ge(gn_grouped, 1)
            link(nc.vector.tensor_copy(gn_g[:, :, :], ps[:, 7, 0:2 * B].rearrange("c (b m) -> c b m", b=B)))
            link(nc.vector.tensor_tensor(gn_sq[:, :], gn_g[:, :, 0], gn_g[:, :, 0], ALU.mult))
            nc.vector.tensor_tensor(gn_var[:, :], gn_g[:, :, 1], gn_sq[:, :], ALU.subtract).then_inc(gn_varied, 1)
            dve.wait_ge(ld_v, 16)
            dve.wait_ge(dve_consts, 1)
            for n, name in enumerate(("vproj_b", "mop_b")):
                nc.vector.tensor_scalar(bias_c[:, n, :], ones_mean[:, :], float(P), V(name),
                                        ALU.mult, ALU.mult).then_inc(bias_ready, 1)
            dve.wait_ge(gn_stded, 1)
            link(nc.vector.reciprocal(gn_std[:, :], gn_std[:, :]))
            link(nc.vector.tensor_scalar(gn_scale[:, :], gn_std[:, :], V("gn_g"), None, ALU.mult))
            link(nc.vector.tensor_tensor(gn_sq[:, :], gn_g[:, :, 0], gn_scale[:, :], ALU.mult))
            link(nc.vector.tensor_scalar(gn_shift[:, :], gn_sq[:, :], -1.0, V("gn_b"), ALU.mult, ALU.add))
            for b in range(B):
                cols = slice(b * HW, (b + 1) * HW)
                nc.vector.tensor_scalar(xn[:, cols], x_sb[:, cols], gn_scale[:, b:b + 1], gn_shift[:, b:b + 1],
                                        ALU.mult, ALU.add).then_inc(xn_ready, 1)
            dve.wait_ge(consts, CONSTS)
            nc.vector.tensor_copy(ident_b[:, :], ident[:, :])
            nc.vector.tensor_copy(expert_f[:, :], expert_i[:, :])
            nc.vector.tensor_scalar(own_f[:, :, :], own_i[:, :, :], 0.0, None, ALU.is_equal)
            link(nc.vector.tensor_copy(row_f[:, :], row_i[:, :]))
            link(nc.vector.tensor_tensor(one_less_sq[:, :], row_f[:, :], row_f[:, :], ALU.mult))
            nc.vector.tensor_scalar(one_less_sq[:, :], one_less_sq[:, :], -1.0, 1.0, ALU.mult, ALU.add)
            link(nc.vector.tensor_reduce(row_groups[:, :, :], ident[:, :].rearrange("p (u g i) -> p u g i", u=2, g=4),
                                         AX_X, ALU.add))
            link(nc.vector.tensor_tensor(row_group[:, :], row_groups[:, 0, :], row_groups[:, 1, :], ALU.add))
            for n, scale in enumerate((AD ** -0.5, 1.0)):
                low = row_group[:, n + 1:n + 2]
                nc.vector.tensor_scalar(raw_by[:, n:n + 1], low, scale, None, ALU.mult)
                nc.vector.tensor_scalar(high_by[:, n:n + 1], low, -2.0 * scale, scale, ALU.mult, ALU.add)
            nc.vector.tensor_copy(pick[:, :], ident[0:AH, 0:AH]).then_inc(dve_consts, 1)
            nc.vector.memset(gap[:, 0:1], 0.0).then_inc(hot_ready, HOT_CREDIT)
            nc.vector.memset(gap[:, 1:2], 0.0).then_inc(g_ready, G_CREDIT)
            nc.vector.memset(gap[:, 2:3], 0.0).then_inc(g_free, FREE_CREDIT)
            nc.vector.memset(gap[:, 3:4], 0.0).then_inc(prod_free, FREE_CREDIT)
            for h in range(2):
                dve.wait_ge(pin_mm, 4 * (h + 1))
                ln_stats(lns["ln1"], ps[:, 0:2, :].rearrange("k a (t c) -> k (a t) c", c=C), h)
            dve.wait_ge(t0_ready, 2)
            ln_apply(lns["ln1"], t0_k)

            for h in range(2):
                tiles = slice(4 * h, 4 * h + 4)
                dve.wait_ge(proj_mm, 4 * (h + 1))
                nc.vector.tensor_scalar(y_half[:, tiles, :], proj_ps(h)[:, :, HP:2 * HP], 0.5, (HW - 3) / 4,
                                        ALU.mult, ALU.add).then_inc(y_halved, 1)
            dve.wait_ge(y_halved, 2)
            link(nc.vector.tensor_scalar(y_half[:, :, :], y_half[:, :, :], 0.0, float(HW // 2 - 1), ALU.max, ALU.min))
            nc.vector.tensor_scalar(pair[:, :, :], y_half[:, :, :], ROUND, -ROUND, ALU.add, ALU.add).then_inc(pair_ready, 1)

            def by_head(t):
                return t[:, :, :].rearrange("q t (h p) -> q t h p", p=NP)

            dve.wait_ge(pair_ready, 1)
            link(nc.vector.tensor_tensor(terms[:, :, :, 1, :], by_head(pair), by_head(pair), ALU.mult))
            nc.vector.tensor_copy(terms[:, :, :, 0, :], by_head(pair))
            dve.wait_ge(sq_ready, 1)
            nc.vector.tensor_tensor(terms[:, :, :, 2, :], by_head(pair_sq), terms[:, :, :, 1, :],
                                    ALU.subtract).then_inc(terms_ready, 1)
            dve.wait_ge(proj_ready, 4)
            link(nc.vector.tensor_scalar(y_pos[:, :, :], proj[:, :, HP:2 * HP], 1.0, (HW - 1) / 2, ALU.mult, ALU.add))
            nc.vector.scalar_tensor_tensor(out=y_rest[:, :, :], in0=pair[:, :, :], scalar=-2.0, in1=y_pos[:, :, :],
                                           op0=ALU.mult, op1=ALU.add).then_inc(rest_ready, 1)
            for n, b in enumerate(VALUE_ORDER):
                dve.wait_ge(val_p0, n + 1)
                nc.vector.tensor_tensor(val_r[:, b, :, :, :].rearrange("r h k d -> r k h d"),
                                        val_ps(b).rearrange("r (k h d) -> r k h d", k=NK, h=NH),
                                        val_p[0][:, b, :, :, :].rearrange("r h k d -> r k h d"),
                                        ALU.subtract).then_inc(val_r1, 1)
            logits = proj[:, :, 2 * HP:].rearrange("q t (h p) -> q t h p", p=NP)
            l3 = lmax[:, :].rearrange("q (t h) -> q t h", h=NH)
            a4 = aw[:, :, :].rearrange("q (t h) p -> q t h p", h=NH)
            link(nc.vector.tensor_reduce(l3, logits, AX_X, ALU.max))
            nc.vector.tensor_tensor(a4, logits, l3.unsqueeze(3).to_broadcast([P, TILES, NH, NP]),
                                    ALU.subtract).then_inc(logit_sub, 1)
            dve.wait_ge(val_p1, 1)
            nc.vector.tensor_tensor(val_p[2], val_r, val_p[1], ALU.subtract).then_inc(val_p1, 1)
            for k in range(2):
                dve.wait_ge(y_abs, k + 1)
                nc.vector.tensor_scalar(hat_y[:, k, :, :], hat_y[:, k, :, :], -1.0, 1.0, ALU.mult, ALU.add).then_inc(
                    hat_y_ready, 1)
            dve.wait_ge(logit_exp, 1)
            link(nc.vector.tensor_reduce(lsum[:, :], aw[:, :, :], AX_X, ALU.add))
            link(nc.vector.reciprocal(lsum[:, :], lsum[:, :]))
            link(nc.vector.tensor_tensor(aw[:, :, :], aw[:, :, :],
                                         lsum[:, :].unsqueeze(2).to_broadcast([P, TILES * NH, NP]), ALU.mult))
            dve.wait_ge(hat_x_ready, 1)
            flat = aw[:, :, :].rearrange("q (t h) p -> q t (h p)", h=NH)
            link(nc.vector.scalar_tensor_tensor(out=hat_x[:, :, :], in0=hat_x[:, :, :], scalar=0.0, in1=flat,
                                                op0=ALU.max, op1=ALU.mult))
            for k in range(NK):
                if k < 2:
                    dve.wait_ge(hat_y_ready, k + 1)
                else:
                    dve.wait_ge(hat_y2_ready, 1)
                nc.vector.scalar_tensor_tensor(out=wk3[:, :, :, k], in0=hat_y[:, k, :, :], scalar=0.0, in1=hat_x[:, :, :],
                                               op0=ALU.max, op1=ALU.mult).then_inc(wk3_ready, 1)
            dve.wait_ge(t0_ready, 2)
            nc.vector.tensor_tensor(t0_k[:, :, :], t0_k[:, :, :], b_out.unsqueeze(1).to_broadcast([P, TILES, C]),
                                    ALU.add).then_inc(t0_ready, 1)
            dve.wait_ge(wk3_ready, NK)

            with dve.Fori(0, NH) as i:
                for u in range(2):
                    for c in range(2):
                        dve.wait_ge(g_ready, 4 * i + 2 * u + c + 1 + G_CREDIT)
                        dve.wait_ge(prod_free, 4 * i + 2 * u + c + 1)
                        g = ps[:, 4 + 2 * c:6 + 2 * c, 0:NP * NK * DH].rearrange("q b (n d) -> q b n d", d=DH)
                        w = wk3[:, 4 * c + u:4 * c + u + 3:2, bass.ds(i * NP, NP), :].rearrange("q b p k -> q b (p k)")
                        nc.vector.tensor_tensor(prod[:, c, :, :, :], g,
                                                w.unsqueeze(3).to_broadcast([P, 2, NP * NK, DH]),
                                                ALU.mult).then_inc(g_free, 1)
                    for c in range(2):
                        dve.wait_ge(g_free, 4 * i + 2 * u + c + 1 + FREE_CREDIT)
                        nc.vector.tensor_reduce(msda[:, 4 * c + u:4 * c + u + 3:2, bass.ds(i, 1), :].rearrange(
                                                    "q b h d -> q b (h d)"),
                                                prod[:, c, :, :, :].rearrange("q b n d -> q b d n"),
                                                AX_X, ALU.add).then_inc(prod_free, 1)

            norm(lns["ln3"], 2, out_mm)
            for n in range(2 * GE):
                h, j = n // GE, n % GE
                if n < 2:
                    dve.wait_ge(lns["ln3"]["out"], n + 1)
                    nc.vector.tensor_tensor(half(hn_l, n), half(hn, n), half(hn_h, n).bitcast(F32),
                                            ALU.subtract).then_inc(hn_l_ready, 1)
                dve.wait_ge(gelu_ready, n + 1)
                dve.wait_ge(lin_mm, n + 1)
                nc.vector.scalar_tensor_tensor(out=half(ff[:, j, :], h), in0=ps[:, 6 + n % 2, :],
                                               scalar=V("geglu_b", j), in1=gelu_g[:, n % 2, :],
                                               op0=ALU.add, op1=ALU.mult).then_inc(ff_ready, 1)
            dve.wait_ge(x1_mm, 4)
            ln_stats(lns["lna"], summed(2), 0)
            ln_apply(lns["lna"], summed(2), (0,))

            def z1_rest(h):
                dve.wait_ge(lns["lna"]["out"], h + 1)
                nc.vector.tensor_tensor(half(z1_l, h), half(z1, h), half(z1_h, h).bitcast(F32),
                                        ALU.subtract).then_inc(z1_l_ready, 1)

            nc.vector.memset(gap[:, 4:5], 0.0).then_inc(prob_ready, FREE_CREDIT)
            nc.vector.memset(gap[:, 5:6], 0.0).then_inc(pv_mm, FREE_CREDIT)
            nc.vector.memset(gap[:, 6:7], 0.0).then_inc(o_raw_ready, O_CREDIT)
            nc.vector.memset(gap[:, 7:8], 0.0).then_inc(o_ready, O_CREDIT)

            def parts(b, slot, n):
                dve.wait_ge(high_ready, 4 * b + n + 1)
                q_or_k, pairs = n % 2, slice(2 * (n // 2), 2 * (n // 2) + 2)
                to = qkp[q_or_k][:, slot, pairs, :]
                nc.vector.scalar_tensor_tensor(out=to, in0=ps[:, 6 + n % 2, :].rearrange("c (n t) -> c n t", n=2),
                                               scalar=raw_by[:, q_or_k:q_or_k + 1], in1=to.bitcast(F32),
                                               op0=ALU.mult, op1=ALU.add).then_inc(qk_ready, 1)

            def row_max(b, h):
                dve.wait_ge(sc_mm, AH * b + h + 1)
                nc.vector.tensor_reduce(nmax[:, :, h], ps[:, h % 2, :].rearrange("q (t k) -> q t k", t=2),
                                        AX_X, ALU.max, negate=True).then_inc(nmax_ready, 1)

            def max_rows(b, slot):
                dve.wait_ge(nt_mm, b + 1)
                nc.vector.tensor_copy(nmax_t[:, slot, :], ps[0:AH, 0, 0:HW]).then_inc(nmax_t_ready, 1)

            def residual_stats(h):
                dve.wait_ge(ap_mm, 4 * (h + 1))
                nc.vector.tensor_tensor(four(x2_k, h), four(x1_k, h), ps[:, h, :], ALU.add).then_inc(x2_ready, 1)
                dve.wait_ge(x2_ready, h + 1)
                ln_stats(lns["lnf"], x2_k, h)

            def attend(b, slot, last):
                if not last:
                    for n in range(4):
                        parts(b + 1, 1 - slot, n)
                    for h in range(AH):
                        row_max(b + 1, h)
                    max_rows(b + 1, 1 - slot)
                else:
                    residual_stats(0)
                dve.wait_ge(turn_mm, b + 1)
                o_ps = ps[:, 5, :].rearrange("q (t h c) -> q t h c", t=2, h=AH)
                nc.vector.reciprocal(inv_sum[:, :, :], o_ps[:, :, :, AD]).then_inc(inv_ready, 1)
                dve.wait_ge(inv_ready, b + 1)
                nc.vector.tensor_tensor(o_tok[:, bass.ds(2 * b, 2), :, :], o_ps[:, :, :, 0:AD],
                                        inv_sum[:, :, :].unsqueeze(3).to_broadcast([P, 2, AH, AD]),
                                        ALU.mult).then_inc(o_ready, 1)

            z1_rest(0)
            dve.wait_ge(x1_mm, 8)
            ln_stats(lns["lna"], summed(2), 1)
            dve.wait_ge(dve_consts, 2)
            parts(0, 0, 0)
            parts(0, 0, 1)
            ln_apply(lns["lna"], summed(2), (1,))
            row_max(0, 0)
            row_max(0, 1)
            parts(0, 0, 2)
            parts(0, 0, 3)
            for h in range(2, AH):
                row_max(0, h)
            max_rows(0, 0)
            z1_rest(1)
            with dve.Fori(0, B // 2 - 1) as i:
                attend(2 * i, 0, False)
                attend(2 * i + 1, 1, False)
            attend(B - 2, 0, False)
            attend(B - 1, 1, True)
            nc.vector.memset(lmax[:, 0:1], 0.0).then_inc(h_mm, H_CREDIT)
            nc.vector.memset(lmax[:, 1:2], 0.0).then_inc(h_used, U_CREDIT)
            nc.vector.memset(lmax[:, 2:3], 0.0).then_inc(y_mm, Y_CREDIT)
            ln_apply(lns["lnf"], x2_k, (0,))
            residual_stats(1)
            ln_apply(lns["lnf"], x2_k, (1,))

            for h in range(2):
                tiles = slice(4 * h, 4 * h + 4)
                dve.wait_ge(lg_mm, 4 * (h + 1))
                link(nc.vector.tensor_copy(lg[:, tiles, :], ps[:, 4 + h, 0:4 * E].rearrange(
                    "t (n e) -> t n e", e=E)))
                for t in range(4 * h, 4 * h + 4):
                    ins = nc.vector.max(top[:, t, :], lg[:, t, :])
                link(ins)
                nc.vector.tensor_tensor(gap[:, tiles], top[:, tiles, 1], top[:, tiles, 0], ALU.subtract).then_inc(gap_ready, 1)
                for t in range(4 * h, 4 * h + 4):
                    ins = nc.vector.max_index(top_i[:, t, :], top[:, t, :], lg[:, t, :])
            link(ins)
            link(nc.vector.tensor_copy(top_f[:, :, :], top_i[:, :, 0:TOPK]))
            ex = expert_f[:, :].unsqueeze(1).to_broadcast([P, TILES, E])
            nc.vector.tensor_tensor(oh1[:, :, :], ex, top_f[:, :, 0:1].to_broadcast([P, TILES, E]), ALU.is_equal)
            link(nc.vector.tensor_tensor(oh2[:, :, :], ex, top_f[:, :, 1:2].to_broadcast([P, TILES, E]), ALU.is_equal))
            link(nc.vector.tensor_tensor(chosen[:, :, :], oh1[:, :, :], oh2[:, :, :], ALU.add))
            dve.wait_ge(pool_step, 5)
            nc.vector.tensor_copy(chosen_b[:, :, 0:E], chosen[:, :, :]).then_inc(route_ready, 1)
            dve.wait_ge(rt_mm, TILES)
            nc.vector.tensor_copy(chosen_t[:, :], ps[:, 5, :].bitcast(BF16)).then_inc(route_t_ready, 1)

            def masked(e, n):
                dve.wait_ge(h_mm, FT * e + FT)
                for h in range(2):
                    dve.wait_ge(mb_mm, 2 * e + h + 1)
                    mask = ps[:, 2 * h if isinstance(e, int) and e == 0 else 0, :]
                    nc.vector.tensor_tensor(half(xm_h[:, n, :], h), half(z2_h, h), mask, ALU.mult)
                    nc.vector.tensor_tensor(half(xm_l[:, n, :], h), half(z2_l, h), mask,
                                            ALU.mult).then_inc(xm_ready, 1)

            def means(e, n):
                dve.wait_ge(h_used, FT * e + FT + U_CREDIT)
                dve.wait_ge(y_mm, e + 1)
                nc.vector.tensor_scalar(h_mean[:, n, :], h_sum[:, bass.ds(e, 1), :].rearrange("p e f -> p (e f)"),
                                        inv_cnt[:, bass.ds(e, 1)], None, ALU.mult).then_inc(hmean_ready, 1)
                nc.vector.tensor_copy(own_col[:, n, :], own_f[:, bass.ds(e, 1), :].rearrange("p a e -> p (a e)"))
                dve.wait_ge(hmean_ready, e + 1)
                w2_of = [w2_sb[:, bass.ds(FT * e + f, 1), :].rearrange("f n d -> f (n d)") for f in range(FT)]
                nc.vector.tensor_scalar(y_rows[:, n, :], w2_of[0], h_mean[:, n, 0:1], None, ALU.mult).then_inc(y_summed, 1)
                for f in range(1, FT):
                    dve.wait_ge(y_summed, (FT - 1) * e + f)
                    nc.vector.scalar_tensor_tensor(out=y_rows[:, n, :], in0=w2_of[f], scalar=h_mean[:, n, f:f + 1],
                                                   in1=y_rows[:, n, :], op0=ALU.mult, op1=ALU.add).then_inc(
                        y_summed if f < FT - 1 else y_rows_ready, 1)

            def expert_pair(i, first, last):
                masked(2 * i + 1, 1)
                if not first:
                    means(2 * i - 1, 1)
                if not last:
                    masked(2 * i + 2, 0)
                means(2 * i, 0)

            dve.wait_ge(z2_parted, 4)
            dve.wait_ge(ld_w2, 16)
            dve.wait_ge(cnt_mm, 1)
            nc.vector.tensor_scalar(cnt[:, :], ps[:, 1, 2 * P:2 * P + E], float(P), 1.0, ALU.mult, ALU.max).then_inc(cnt_read, 1)
            masked(0, 0)
            dve.wait_ge(cnt_read, 1)
            dve.wait_ge(e2_ready, 1)
            link(nc.vector.tensor_scalar(e2p[:, :], e2[:, :], 1.0, None, ALU.add))
            link(nc.vector.reciprocal(rw1[:, :], e2p[:, :]))
            link(nc.vector.tensor_tensor(rw2[:, :], e2[:, :], rw1[:, :], ALU.mult))
            nc.vector.tensor_tensor(oh1[:, :, :], oh1[:, :, :], rw1[:, :].unsqueeze(2).to_broadcast([P, TILES, E]), ALU.mult)
            link(nc.vector.tensor_tensor(oh2[:, :, :], oh2[:, :, :],
                                         rw2[:, :].unsqueeze(2).to_broadcast([P, TILES, E]), ALU.mult))
            nc.vector.tensor_tensor(route[:, :, :], oh1[:, :, :], oh2[:, :, :], ALU.add).then_inc(route_ready, 1)
            link(nc.vector.reciprocal(inv_cnt[:, :], cnt[:, :]))
            expert_pair(0, True, False)
            with dve.Fori(1, E // 2 - 1) as i:
                expert_pair(i, False, False)
            expert_pair(E // 2 - 1, False, True)
            dve.wait_ge(rt_mm, 2 * TILES)
            nc.vector.tensor_copy(route_t[:, :], ps[0:E, 6:8, :].rearrange("e a t -> e (a t)")).then_inc(route_t_ready, 1)
            means(E - 1, 1)
            dve.wait_ge(y_mm, E + Y_CREDIT)
            nc.vector.tensor_copy(y_mean[:, :], ps[0:E, 1, 0:P]).then_inc(y_ready, 1)
            for h in range(2):
                dve.wait_ge(moe_mm, h + 1)
                dve.wait_ge(x2_c_ready, h + 1)
                nc.vector.tensor_tensor(half(y_out, h), half(x2_c, h), ps[:, 2 + h, :], ALU.add).then_inc(y_out_ready, 1)

        @block.tensor
        def _(pe):
            def turn(s, bank, halves=(0, 1)):
                for t in range(4 * halves[0], 4 * halves[-1] + 4):
                    pe.wait_ge(s["norm"], t + 1)
                    nc.tensor.transpose(ps[:, bank + t // 4, P * (t % 4):P * (t % 4) + P], nrm[:, t, :],
                                        ident[:, :]).then_inc(s["turned"], 1)

            def tile_of(bank, t):
                return ps[:, bank + t // 4, P * (t % 4):P * (t % 4) + P]

            pe.wait_ge(dve_consts, 1)
            pe.wait_ge(consts, CONSTS)
            pe.wait_ge(gn_moments, 1)
            nc.tensor.matmul(ps[:, 7, 0:2 * B], group_mean[:, :],
                             gn_mv[:, :, :].rearrange("c b m -> c (b m)")).then_inc(gn_grouped, 1)
            pe.wait_ge(ld_r, 16)
            for h in range(2):
                nc.tensor.matmul(ps[:, h, :], ident[:, :], rows4(R("pin_b")), start=True, stop=False, skip_group_check=True)
            pe.wait_ge(ld_wa, 16)
            for t in range(TILES):
                pe.wait_ge(xn_ready, t // 2 + 1)
                nc.tensor.matmul(tile_of(0, t), xn[:, t * P:(t + 1) * P], W("pin"), start=False, stop=True,
                                 skip_group_check=True).then_inc(pin_mm, 1)
            pe.wait_ge(ld_wb, 16)
            nc.tensor.matmul(ps[:, 4, 0:128], W("vprojT"), W("mvp"))
            nc.tensor.matmul(ps[:, 4, 128:256], W("mopT"), W("dout"))
            pe.wait_ge(bias_ready, 2)
            for n, (w, b) in enumerate((("mvp", "mvp_b"), ("dout", "dout_b"))):
                o = ps[:, 4, 256 + n * P:256 + (n + 1) * P]
                nc.tensor.matmul(o, bias_c[:, n, :], W(w), start=True, stop=False)
                ins = nc.tensor.matmul(o, ident[:, :], R(b), start=False, stop=True)
            ins.then_inc(fuse_mm, 1)
            pe.wait_ge(ld_wc, 16)
            for j in range(GE):
                nc.tensor.matmul(ps[:, 5, j * P:(j + 1) * P], W("denseT")[:, j * P:(j + 1) * P], W("pout"))
            nc.tensor.matmul(ps[:, 6, 0:1], W("pout"), V("dense_b"), start=True, stop=False)
            nc.tensor.matmul(ps[:, 6, 0:1], ident[:, :], V("pout_b"), start=False, stop=True).then_inc(fuse_mm, 1)

            soff_attw = w_sb[:, WAT["soff"][0]:WAT["attw"][1]]
            r_proj = r_sb[:, RAT["soff_b"][0]:RAT["attw_b"][1]].unsqueeze(1).to_broadcast([P, 2, 3 * HP])

            def proj_bias(h):
                for j in range(2):
                    nc.tensor.matmul(proj_ps(h)[:, 2 * j:2 * j + 2, :], ident[:, :], r_proj, start=True, stop=False,
                                     skip_group_check=True)

            pe.wait_ge(t0_ready, 2)
            pe.wait_ge(lns["ln1"]["var"], 2)
            proj_bias(0)
            turn(lns["ln1"], 2)
            pe.wait_ge(fuse_ready, 2)
            proj_bias(1)
            for t in range(TILES):
                pe.wait_ge(lns["ln1"]["out"], t // (TILES // 2) + 1)
                nc.tensor.matmul(proj_ps(t // 4)[:, t % 4, :], q_c[:, t * P:(t + 1) * P], soff_attw,
                                 start=False, stop=True, skip_group_check=True).then_inc(proj_mm, 1)

            def values(b):
                o = val_ps(b).rearrange("r (k c) -> r k c", k=NK)
                nc.tensor.matmul(o[:, 0:2, :], ident[:, :], b_val.unsqueeze(1).to_broadcast([P, 2, P]),
                                 start=True, stop=False, skip_group_check=True)
                nc.tensor.matmul(o[:, 2, :], ident_less[:, :], b_val, start=False, stop=False, skip_group_check=True)
                for k in range(NK):
                    rows_k = P if k < 2 else P - 1
                    first = b * HW + k
                    ins = nc.tensor.matmul(o[0:rows_k, k, :], q_c[:, first:first + 2 * rows_k - 1:2], w_val,
                                           start=False, stop=True, skip_group_check=True)
                ins.then_inc(val_mm, 1)

            pe.wait_ge(fuse_ready, 3)
            for b in VALUE_ORDER[:3]:
                values(b)
            pe.wait_ge(terms_ready, 1)
            pe.wait_ge(proj_ready, 4)
            pe.wait_ge(dve_consts, 2)
            for g in range(2):
                for n in range(TILES):
                    t = 2 * (n % B) + n // B
                    nc.tensor.transpose(ps[:, g, 64 * n:64 * n + 64].bitcast(BF16),
                                        terms[:, t, 4 * g:4 * g + 4, :, :].rearrange("q h c p -> q (h c p)"),
                                        ident_b[:, :]).then_inc(terms_mm, 1)
            values(VALUE_ORDER[3])
            pe.wait_ge(terms_t_ready, 2)
            pe.wait_ge(sel_ready, 4)
            pe.wait_ge(g_ready, G_CREDIT)

            def distances(i, u, c):
                pe.wait_ge(hot_ready, 8 * i + 4 * u + c + 1)
                for p in (2 * c, 2 * c + 1):
                    ins = nc.tensor.matmul(ps[:, 2 * (c % 2) + p % 2, :],
                                           sel[:, bass.ds(i % 4, 1), p, :].rearrange("k h j -> k (h j)"),
                                           terms_t[:, bass.ds(i // 4, 1), u * HALF:(u + 1) * HALF].rearrange(
                                               "k g q -> k (g q)"))
                ins.then_inc(dist_mm, 1)

            def gather(i, u, b):
                if b == 0:
                    pe.wait_ge(hot_ready, 8 * i + 4 * u + 4 + HOT_CREDIT)
                if b % 2 == 0:
                    pe.wait_ge(g_free, 4 * i + 2 * u + b // 2 + 1)
                for p in range(NP):
                    for s in range(PARTS):
                        rhs = val_p[s][:, b, bass.ds(i, 1), :, :].rearrange("r h k d -> r (h k d)")
                        ins = nc.tensor.matmul(ps[:, 4 + b, p * NK * DH:(p + 1) * NK * DH], hot[:, u, p, b, :], rhs,
                                               start=(s == 0), stop=(s == PARTS - 1))
                if b % 2:
                    ins.then_inc(g_ready, 1)

            def residual():
                for h in range(2):
                    nc.tensor.matmul(ps[:, 2 + h, :], ident[:, :], four(t0_k, h), start=True, stop=False,
                                     skip_group_check=True)
                for t in range(TILES):
                    nc.tensor.matmul(tile_of(2, t), q_c[:, t * P:(t + 1) * P], W("dout"), start=False, stop=False,
                                     skip_group_check=True)

            def sample(i, last):
                for c in range(NP // 2):
                    distances(i, 1, c)
                    gather(i, 0, c)
                for c in range(NP // 2):
                    if not last:
                        distances(i + 1, 0, c)
                    gather(i, 1, c)

            for c in range(NP // 2):
                if c == 1:
                    pe.wait_ge(val_r1, 2)
                distances(0, 0, c)
            pe.wait_ge(val_p1, 2)
            with pe.Fori(0, NH - 1) as i:
                sample(i, False)
            sample(NH - 1, True)
            residual()
            for t in range(TILES):
                if t == 0:
                    pe.wait_ge(prod_free, 4 * NH + FREE_CREDIT)
                nc.tensor.transpose(tile_of(0, t), msda[:, t, :, :].rearrange("q h d -> q (h d)"),
                                    ident[:, :]).then_inc(msda_mm, 1)
            for t in range(TILES):
                pe.wait_ge(msda_c_ready, t // 4 + 1)
                nc.tensor.matmul(tile_of(2, t), msda_c[:, t * P:(t + 1) * P], w_out, start=False, stop=True,
                                 skip_group_check=True).then_inc(out_mm, 1)
            turn(lns["ln3"], 4)
            pe.wait_ge(geglu_parted, 2)

            def geglu_step(n):
                h, j = n // GE, n % GE
                pe.wait_ge(hn_h_ready, h + 1)
                for at, bank, done, used in ((GE + j, n % 2, gate_mm, gelu_ready), (j, 6 + n % 2, lin_mm, ff_ready)):
                    if n >= 2:
                        pe.wait_ge(used, n - 1)
                    cols = slice(at * P, (at + 1) * P)
                    nc.tensor.matmul(ps[:, bank, :], geglu_h[:, cols], half(hn_h, h), start=True, stop=False)
                    nc.tensor.matmul(ps[:, bank, :], geglu_l[:, cols], half(hn_h, h), start=False, stop=False)
                    pe.wait_ge(hn_l_ready, h + 1)
                    nc.tensor.matmul(ps[:, bank, :], geglu_h[:, cols], half(hn_l, h), start=False, stop=True).then_inc(done, 1)

            def feed_forward_out(t):
                cols = slice(t * P, (t + 1) * P)
                nc.tensor.matmul(tile_of(2, t), x_sb[:, cols], ident[:, :], start=True, stop=False)
                pe.wait_ge(t1_c_ready, t // 4 + 1)
                nc.tensor.matmul(tile_of(2, t), t1_c[:, cols], W("pout"), start=False, stop=False)
                pe.wait_ge(ff_ready, GE * (t // 4 + 1))
                for j in range(GE):
                    ins = nc.tensor.matmul(tile_of(2, t), ff[:, j, cols], w_dp[:, j, :], start=False, stop=(j == GE - 1))
                ins.then_inc(x1_mm, 1)

            for n in range(GE):
                geglu_step(n)
            pe.wait_ge(t1_ready, 2)
            for t in range(TILES):
                nc.tensor.transpose(tile_of(4, t), t1_k[:, t, :], ident[:, :]).then_inc(t1_mm, 1)
            geglu_step(GE)
            pe.wait_ge(x_biased, 1)
            for t in range(4):
                feed_forward_out(t)
            for n in range(GE + 1, 2 * GE):
                geglu_step(n)
            for t in range(4, TILES):
                feed_forward_out(t)
                if t == 5:
                    turn(lns["lna"], 4, (0,))

            def project(b, n):
                if not (isinstance(b, int) and b == 0 and n < 2):
                    pe.wait_ge(qk_ready, 4 * b + n - 1)
                pe.wait_ge(z1_l_ready, b // 2 + 1)
                for j in range(2):
                    at_w = AH * HROWS * (n % 2) + (2 * (n // 2) + j) * P
                    for k, (w, z) in enumerate(((wqk_h, z1_h), (wqk_l, z1_h), (wqk_h, z1_l))):
                        ins = nc.tensor.matmul(ps[:, 6 + n % 2, j * HW:(j + 1) * HW], w[:, at_w:at_w + P],
                                               z[:, bass.ds(b * HW, HW)], start=(k == 0), stop=(k == 2))
                ins.then_inc(qk_mm, 1)

            def head(slot, q_or_k, h):
                r = HROWS * (h % 2)
                return qkp[q_or_k][r:r + SPLIT, slot, h // 2, :]

            def scores(b, slot, h):
                if h in (0, AH // 2):
                    pe.wait_ge(qk_ready, 4 * b + (4 if h else 2))
                if h == 0 and not (isinstance(b, int) and b == 0):
                    pe.wait_ge(nmax_t_ready, b)
                if h >= 2:
                    pe.wait_ge(nmax_ready, AH * b + h - 1)
                for t in range(2):
                    ins = nc.tensor.matmul(ps[:, h % 2, t * HW:(t + 1) * HW], head(slot, 0, h)[:, t * P:(t + 1) * P],
                                           head(slot, 1, h))
                ins.then_inc(sc_mm, 1)

            def turn_max(b):
                pe.wait_ge(nmax_ready, AH * b + AH)
                for t in range(2):
                    ins = nc.tensor.transpose(ps[0:AH, 0, t * P:(t + 1) * P], nmax[:, t, :], ident[:, :])
                ins.then_inc(nt_mm, 1)

            def scores_t(b, slot, h):
                if h == 0:
                    pe.wait_ge(nmax_t_ready, b + 1)
                pe.wait_ge(prob_ready, AH * b + h + 1)
                for t in range(2):
                    o = ps[:, 2 + h % 2, t * HW:(t + 1) * HW]
                    nc.tensor.matmul(o, pick[:, h:h + 1].to_broadcast([AH, P]), nmax_t[:, slot, :], start=True, stop=False)
                    ins = nc.tensor.matmul(o, head(slot, 1, h)[:, t * P:(t + 1) * P], head(slot, 0, h), start=False, stop=True)
                ins.then_inc(st_mm, 1)

            def weigh_values(b, slot, h):
                pe.wait_ge(prob_ready, AH * b + h + 1 + FREE_CREDIT)
                if h == 0:
                    pe.wait_ge(v_placed, b + 1)
                    pe.wait_ge(o_raw_ready, b + O_CREDIT)
                for t in range(2):
                    ins = nc.tensor.matmul(ps[:, 4, (h // 4) * HW:(h // 4 + 1) * HW], v_wide[:, slot, t, h, :],
                                           prob_t[:, h % 2, t * HW:(t + 1) * HW],
                                           start=(h % 4 == 0 and t == 0), stop=(h % 4 == 3 and t == 1))
                ins.then_inc(pv_mm, 1)

            def turn_out(b):
                pe.wait_ge(o_raw_ready, b + 1 + O_CREDIT)
                pe.wait_ge(o_ready, b + O_CREDIT)
                for t in range(2):
                    for g in range(2):
                        at_t = (2 * t + g) * P
                        ins = nc.tensor.transpose(ps[:, 5, at_t:at_t + P],
                                                  o_raw[:, g * HW + t * P:g * HW + (t + 1) * P], ident[:, :])
                ins.then_inc(turn_mm, 1)

            def turn_outputs(h):
                pe.wait_ge(o_ready, 2 * h + 2 + O_CREDIT)
                for t in range(4 * h, 4 * h + 4):
                    nc.tensor.transpose(tile_of(6, t), o_tok[:, t, :, :].rearrange("q h d -> q (h d)"),
                                        ident[:, :]).then_inc(ot_mm, 1)

            def project_out(h):
                pe.wait_ge(o_c_ready, h + 1)
                for t in range(4 * h, 4 * h + 4):
                    nc.tensor.matmul(tile_of(0, t), o_c[:, t * P:(t + 1) * P], W("wproj")).then_inc(ap_mm, 1)

            def attend(b, slot, last):
                for h in range(AH):
                    if not last:
                        if h < 2:
                            project(b + 1, 2 * h)
                            project(b + 1, 2 * h + 1)
                        elif h < 6:
                            scores(b + 1, 1 - slot, 2 * h - 4)
                            scores(b + 1, 1 - slot, 2 * h - 3)
                        elif h == 6:
                            turn_max(b + 1)
                    weigh_values(b, slot, h)
                    if h + 2 < AH:
                        scores_t(b, slot, h + 2)
                    elif not last:
                        scores_t(b + 1, 1 - slot, h + 2 - AH)
                    if last and h == 3:
                        turn_outputs(0)
                    if last and h == 5:
                        project_out(0)
                turn_out(b)

            pe.wait_ge(z1_h_ready, 1)
            pe.wait_ge(wqk_parted, 2)
            pe.wait_ge(dve_consts, 2)
            project(0, 0)
            project(0, 1)
            scores(0, 0, 0)
            scores(0, 0, 1)
            project(0, 2)
            project(0, 3)
            turn(lns["lna"], 4, (1,))
            scores(0, 0, 2)
            scores(0, 0, 3)
            pe.wait_ge(lns["lna"]["out"], 2)
            for t in range(TILES):
                nc.tensor.matmul(tile_of(4, t), z1[:, t * P:(t + 1) * P], W("wv")).then_inc(v_mm, 1)
            for h in range(4, AH):
                scores(0, 0, h)
            turn_max(0)
            pe.wait_ge(v_ready, 2)
            pe.wait_ge(x1_ready, 2)
            scores_t(0, 0, 0)
            scores_t(0, 0, 1)
            with pe.Fori(0, B // 2 - 1) as i:
                attend(2 * i, 0, False)
                attend(2 * i + 1, 1, False)
            attend(B - 2, 0, False)
            attend(B - 1, 1, True)
            turn_outputs(1)
            project_out(1)
            for h in range(2):
                turn(lns["lnf"], 2, (h,))
                pe.wait_ge(x2_ready, h + 1)
                for t in range(4 * h, 4 * h + 4):
                    nc.tensor.transpose(tile_of(6, t), x2_k[:, t, :], ident[:, :]).then_inc(x2_mm, 1)
                pe.wait_ge(lns["lnf"]["out"], h + 1)
                for t in range(4 * h, 4 * h + 4):
                    nc.tensor.matmul(ps[:, 4 + h, t % 4 * E:(t % 4 + 1) * E], z2[:, t * P:(t + 1) * P], W("gate")).then_inc(lg_mm, 1)
            pe.wait_ge(route_ready, 1)
            pe.wait_ge(pool_step, 5)
            for t in range(TILES):
                nc.tensor.transpose(ps[:, 5, 64 * t:64 * t + 64].bitcast(BF16), chosen_b[:, t, :],
                                    ident_b[:, :]).then_inc(rt_mm, 1)

            def choose(e, h):
                first = isinstance(e, int) and e == 0
                if isinstance(e, int) and e == 1 and h == 0:
                    pe.wait_ge(xm_ready, 1)
                elif not first:
                    pe.wait_ge(xm_ready, 2 * e + h)
                nc.tensor.matmul(ps[:, 2 * h if first else 0, :], ident_b[:, bass.ds(e, 1)].to_broadcast([P, P]),
                                 half(chosen_t, h)).then_inc(mb_mm, 1)

            def hidden(e, n, following):
                if following:
                    choose(e + 1, 0)
                pe.wait_ge(w1_parted, e + 1)
                for f in range(FT):
                    at_slot = FT * n + f
                    pe.wait_ge(h_used, FT * e + f + 1 - BACK[at_slot] + U_CREDIT)
                    cols = slice(f * P, (f + 1) * P)
                    for h in range(2):
                        if f == 0:
                            pe.wait_ge(xm_ready, 2 * e + h + 1)
                        o = ps[:, SLOTS[at_slot] + h, :]
                        nc.tensor.matmul(o, w1_h[:, n, cols], half(xm_h[:, n, :], h), start=True, stop=False)
                        nc.tensor.matmul(o, w1_h[:, n, cols], half(xm_l[:, n, :], h), start=False, stop=False)
                        ins = nc.tensor.matmul(o, w1_l[:, n, cols], half(xm_h[:, n, :], h), start=False, stop=True)
                    ins.then_inc(h_mm, 1)
                    if following and f == 1:
                        choose(e + 1, 1)
                    if not following and f == 2:
                        pe.wait_ge(route_ready, 2)
                        for t in range(TILES):
                            nc.tensor.transpose(ps[0:E, 6 + t // 4, P * (t % 4):P * (t % 4) + P], route[:, t, :],
                                                ident[:, :]).then_inc(rt_mm, 1)

            def mean_out(e, n):
                pe.wait_ge(y_rows_ready, e + 1)
                nc.tensor.matmul(ps[0:E, 1, 0:P], own_col[:, n, :], y_rows[:, n, :], start=False, stop=False,
                                 skip_group_check=True).then_inc(y_mm, 1)

            def expert_pair(i, first, last):
                hidden(2 * i, 0, True)
                if not first:
                    mean_out(2 * i - 2, 0)
                hidden(2 * i + 1, 1, not last)
                if not first:
                    mean_out(2 * i - 1, 1)

            pe.wait_ge(x2_ready, 2)
            for t in range(TILES):
                ins = nc.tensor.matmul(ps[:, 1, 2 * P:2 * P + E], ones_b[:, :], chosen_b[:, t, 0:E], start=(t == 0),
                                       stop=(t == TILES - 1))
            ins.then_inc(cnt_mm, 1)
            pe.wait_ge(route_t_ready, 1)
            choose(0, 0)
            choose(0, 1)
            pe.wait_ge(cnt_read, 1)
            nc.tensor.matmul(ps[0:E, 1, 0:P], zero_c[:, :], ident[:, :], start=True, stop=False, skip_group_check=True)
            pe.wait_ge(x2_c_ready, 2)
            expert_pair(0, True, False)
            with pe.Fori(1, E // 2 - 1) as i:
                expert_pair(i, False, False)
            expert_pair(E // 2 - 1, False, True)
            mean_out(E - 2, 0)
            mean_out(E - 1, 1)
            pe.wait_ge(y_ready, 1)
            pe.wait_ge(route_t_ready, 2)
            pe.wait_ge(h_used, E * FT + U_CREDIT)
            for h in range(2):
                nc.tensor.matmul(ps[:, 2 + h, :], y_mean[:, :], half(route_t, h)).then_inc(moe_mm, 1)


def kernel(**inputs):
    import numpy as np
    import concourse.bacc as bacc
    from concourse.bass_utils import run_bass_kernel_spmd as run

    a = {n: np.asarray(v) for n, v in inputs.items()}

    def L(n):
        return a["L0_conv_" + n]

    def thrice(w):
        heads = w.T.reshape(C, AH, AD)
        return np.concatenate([heads] * 3 + [np.zeros_like(heads)], axis=2).reshape(C, AH * HROWS)

    soff_w = L("soff_w").reshape(C, HP, 2).transpose(0, 2, 1).reshape(C, 2 * HP)
    soff_b = L("soff_b").reshape(HP, 2).transpose(1, 0).reshape(2 * HP)
    parts = dict(pin=L("pin_w"), vprojT=L("vproj_w").T, mvp=L("mvp_w"), soff=soff_w, attw=L("attw_w"),
                 mopT=L("mop_w").T, dout=L("dout_w"), geglu=L("geglu_w"),
                 denseT=L("dense_w").T, pout=L("pout_w"), wq=thrice(a["L1_attn_wq"]), wk=thrice(a["L1_attn_wk"]),
                 wv=a["L1_attn_wv"].T, wproj=a["L1_attn_wproj"].T, gate=a["L1_ffn_gate_weight"].T)
    vecs = {n: L(n).reshape(-1, P).T for n in VAT}
    rows = dict(mvp_b=L("mvp_b"), soff_b=soff_b, attw_b=L("attw_b"), pin_b=L("pin_b"), dout_b=L("dout_b"))
    arrays = dict(
        x=a["x"].reshape(B, C, HW),
        weights=np.concatenate([parts[n] for n in WAT], axis=1),
        vectors=np.concatenate([vecs[n] for n in VAT], axis=1),
        rows=np.concatenate([rows[n] for n in RAT]).reshape(1, RTOTAL),
        w1_t=a["L1_ffn_w1"].transpose(0, 2, 1),
        w2_t=a["L1_ffn_w2"].transpose(2, 0, 1).reshape(FT, P, E, C).transpose(1, 2, 0, 3).reshape(P, E * FT, C),
    )
    nc = bacc.Bacc("TRN2", target_bir_lowering=False, num_devices=1)
    feeds, args = {}, []
    for name, v in arrays.items():
        v = np.ascontiguousarray(v)
        feeds[f"in_{name}"] = v
        args.append(nc.dram_tensor(f"in_{name}", v.shape, F32, kind="ExternalInput").ap())
    out = nc.dram_tensor("out", (B, C, HW), F32, kind="ExternalOutput").ap()
    build(nc, *args, out)
    r = run(nc, [feeds], core_ids=[0])
    return r.results[0]["out"].reshape(B, C, 16, 16)
```
